# Optimizing a Trainium2 kernel written in Bass

```python
import numpy as np
import jax
import jax.numpy as jnp

def _softmax(x, axis=-1):
    return jax.nn.softmax(x, axis=axis)

def _gelu(x):
    return jax.nn.gelu(x, approximate=True)

def _silu(x):
    return jax.nn.silu(x)

def _sigmoid(x):
    return jax.nn.sigmoid(x)

def _layernorm(x, axis=-1, eps=1e-05):
    m = jnp.mean(x, axis=axis, keepdims=True)
    v = jnp.var(x, axis=axis, keepdims=True)
    return (x - m) / jnp.sqrt(v + eps)

def _scatter_add(tgt, idx, src, axis=0):
    return tgt.at[idx].add(src)

def _segment_sum(src, seg, n):
    return jax.ops.segment_sum(src, seg, n)
kernel_name = 'mk_seq_postln_d1_jaxref_r4_3acb21'

def setup_inputs(seed: int=0):
    np.random.seed(seed)
    _w = jnp.asarray

    def _L0_attn_setup():
        import jax, jax.numpy as jnp
        import numpy as np
        CHUNK = 32
        HEADS = 4
        EPS_RMS = 1e-05

        def silu(x):
            return jax.nn.silu(x)

        def l2norm(x, eps=1e-06):
            return x * jax.lax.rsqrt(jnp.sum(x * x, axis=-1, keepdims=True) + eps)

        def short_conv(x, w):
            K = w.shape[1]
            L = x.shape[1]
            xp = jnp.pad(x, ((0, 0), (K - 1, 0), (0, 0)))
            out = xp[:, 0:L, :] * w[:, 0]
            for k in range(1, K):
                out = out + xp[:, k:k + L, :] * w[:, k]
            return out

        def delta_rule_chunkwise(q, k, v, beta, chunk=CHUNK):
            b, h, l, dk = q.shape
            dv = v.shape[-1]
            n = l // chunk
            q = l2norm(q)
            k = l2norm(k)
            v = v * beta[..., None]
            k_beta = k * beta[..., None]
            resh = lambda x: x.reshape(b, h, n, chunk, -1)
            q, k, v, k_beta = map(resh, (q, k, v, k_beta))
            strict_lower = jnp.tril(jnp.ones((chunk, chunk), bool), -1)
            attn = jnp.where(strict_lower, -(k_beta @ jnp.swapaxes(k, -1, -2)), 0.0)
            for i in range(1, chunk):
                row = attn[..., i, :]
                new = attn[..., i, :i] + jnp.einsum('...j,...jk->...k', row, attn[..., :, :i])
                attn = attn.at[..., i, :i].set(new)
            attn = attn + jnp.eye(chunk, dtype=attn.dtype)
            u = attn @ v
            w = attn @ k_beta
            lower_incl = jnp.tril(jnp.ones((chunk, chunk), bool))
            qc, kc, uc, wc = [jnp.moveaxis(x, 2, 0) for x in (q, k, u, w)]
            S0 = jnp.zeros((b, h, dk, dv), q.dtype)

            def step(S, inp):
                q_i, k_i, u_i, w_i = inp
                attn_i = jnp.where(lower_incl, q_i @ jnp.swapaxes(k_i, -1, -2), 0.0)
                u_adj = u_i - w_i @ S
                o_i = q_i @ S + attn_i @ u_adj
                S = S + jnp.swapaxes(k_i, -1, -2) @ u_adj
                return (S, o_i)
            S, o = jax.lax.scan(step, S0, (qc, kc, uc, wc))
            o = jnp.moveaxis(o, 0, 2).reshape(b, h, l, dv)
            return (o, S)

        def ema_rule(v, gamma):
            v_t = jnp.moveaxis(v, 2, 0)
            g_t = jnp.moveaxis(gamma, 2, 0)
            s0 = jnp.zeros(v.shape[:2] + (v.shape[-1],), v.dtype)

            def step(s, inp):
                vt, gt = inp
                s = gt[..., None] * s + (1.0 - gt[..., None]) * vt
                return (s, s)
            s_fin, out = jax.lax.scan(step, s0, (v_t, g_t))
            return (jnp.moveaxis(out, 0, 2), s_fin)

        def rms_norm(x, w, eps=EPS_RMS):
            return x * jax.lax.rsqrt(jnp.mean(x * x, axis=-1, keepdims=True) + eps) * w
        key = jax.random.key(seed)
        ks = jax.random.split(key, 16)
        b, l, d = (4, 512, 256)
        H, conv_K = (HEADS, 4)
        s = 0.02
        return {'hidden_states': jax.random.normal(ks[0], (b, l, d), jnp.float32), 'Wq': jax.random.normal(ks[1], (d, d), jnp.float32) * s, 'Wk': jax.random.normal(ks[2], (d, d), jnp.float32) * s, 'Wv': jax.random.normal(ks[3], (d, d), jnp.float32) * s, 'conv_q': jax.random.normal(ks[4], (d, conv_K), jnp.float32) * 0.3, 'conv_k': jax.random.normal(ks[5], (d, conv_K), jnp.float32) * 0.3, 'conv_v': jax.random.normal(ks[6], (d, conv_K), jnp.float32) * 0.3, 'Wb': jax.random.normal(ks[7], (d, H), jnp.float32) * s, 'Wdec': jax.random.normal(ks[8], (d, H), jnp.float32) * s, 'Wmix': jax.random.normal(ks[9], (d, H), jnp.float32) * s, 'conv_mix': jax.random.normal(ks[10], (H, conv_K), jnp.float32) * 0.3, 'mix_bias': jnp.full((H,), -2.0, jnp.float32), 'rms_w': jnp.ones((d // H,), jnp.float32), 'Wo': jax.random.normal(ks[11], (d, d), jnp.float32) * s}
    _L0_attn_in = _L0_attn_setup()

    def _L0_ffn_setup():
        import jax, jax.numpy as jnp
        import numpy as np
        DIM = 256
        DEPTH = 2
        HEADS = 8
        DIM_HEAD = 64
        WINDOW = 128
        INNER = HEADS * DIM_HEAD
        HID = int(DIM * 4 * 2 / 3)
        B, N = (2, 2048)
        QK_SCALE = 8.0

        def shift_token(t):
            t1, t2 = jnp.split(t, 2, axis=-1)
            t2 = jnp.pad(t2, ((0, 0), (1, 0), (0, 0)))[:, :-1]
            return jnp.concatenate([t1, t2], axis=-1)

        def l2norm(t):
            return t / jnp.clip(jnp.linalg.norm(t, axis=-1, keepdims=True), 1e-12)

        def rotate_half(x):
            x1, x2 = jnp.split(x, 2, axis=-1)
            return jnp.concatenate([-x2, x1], axis=-1)

        def rotary_xpos(q, k):
            n = q.shape[-2]
            half_idx = jnp.arange(0, DIM_HEAD, 2, dtype=jnp.float32)
            inv_freq = 1.0 / 10000.0 ** (half_idx / DIM_HEAD)
            t = jnp.arange(n, dtype=jnp.float32)
            freqs = t[:, None] * inv_freq[None, :]
            freqs = jnp.concatenate([freqs, freqs], axis=-1)
            base = (half_idx + 0.4 * DIM_HEAD) / (1.4 * DIM_HEAD)
            power = (t - n // 2) / float(WINDOW // 2)
            scale = base[None, :] ** power[:, None]
            scale = jnp.concatenate([scale, scale], axis=-1)
            cos, sin = (jnp.cos(freqs), jnp.sin(freqs))
            q = q * cos * scale + rotate_half(q) * sin * scale
            k = k * cos / scale + rotate_half(k) * sin / scale
            return (q, k)

        def local_attention(q, k, v):
            b, h, n, d = q.shape
            w = n // WINDOW
            bq = q.reshape(b, h, w, WINDOW, d) * QK_SCALE
            bk = k.reshape(b, h, w, WINDOW, d)
            bv = v.reshape(b, h, w, WINDOW, d)

            def look_around(t):
                p = jnp.pad(t, ((0, 0), (0, 0), (1, 0), (0, 0), (0, 0)))
                return jnp.concatenate([p[:, :, :w], p[:, :, 1:]], axis=3)
            bk, bv = (look_around(bk), look_around(bv))
            bt = jnp.arange(n).reshape(w, WINDOW)
            btp = jnp.pad(bt, ((1, 0), (0, 0)), constant_values=-1)
            btk = jnp.concatenate([btp[:w], btp[1:]], axis=1)
            sim = jnp.einsum('bhwid,bhwjd->bhwij', bq, bk)
            i = bt[:, :, None]
            j = btk[:, None, :]
            mask = (i < j) | (i > j + WINDOW) | (j == -1)
            sim = jnp.where(mask, -jnp.finfo(sim.dtype).max, sim)
            attn = jax.nn.softmax(sim, axis=-1)
            out = jnp.einsum('bhwij,bhwjd->bhwid', attn, bv)
            return out.reshape(b, h, n, d)

        def _layer(x, wqkv, qs, ksc, wo, lg, lb, w1, b1, w2, b2):
            b, n, _ = x.shape
            h = shift_token(x)
            qkv = h @ wqkv
            q, k, v = jnp.split(qkv, 3, axis=-1)
            to_heads = lambda t: t.reshape(b, n, HEADS, DIM_HEAD).transpose(0, 2, 1, 3)
            q, k, v = (to_heads(q), to_heads(k), to_heads(v))
            q = l2norm(q) * qs
            k = l2norm(k) * ksc
            q, k = rotary_xpos(q, k)
            o = local_attention(q, k, v)
            o = o.transpose(0, 2, 1, 3).reshape(b, n, INNER)
            x = x + o @ wo
            h = shift_token(x)
            mu = h.mean(-1, keepdims=True)
            var = h.var(-1, keepdims=True)
            h = (h - mu) / jnp.sqrt(var + 1e-05) * lg + lb
            h = h @ w1 + b1
            a, g = jnp.split(h, 2, axis=-1)
            h = a * jax.nn.gelu(g, approximate=False)
            x = x + h @ w2 + b2
            return x
        key = jax.random.key(seed)
        ks = jax.random.split(key, 6)
        return {'x': jax.random.normal(ks[0], (B, N, DIM), jnp.float32), 'wqkv': jax.random.normal(ks[1], (DEPTH, DIM, 3 * INNER), jnp.float32) * 0.02, 'q_scale': jnp.ones((DEPTH, DIM_HEAD), jnp.float32), 'k_scale': jnp.ones((DEPTH, DIM_HEAD), jnp.float32), 'wo': jax.random.normal(ks[2], (DEPTH, INNER, DIM), jnp.float32) * 0.02, 'ln_g': jnp.ones((DEPTH, DIM), jnp.float32), 'ln_b': jnp.zeros((DEPTH, DIM), jnp.float32), 'w1': jax.random.normal(ks[3], (DEPTH, DIM, 2 * HID), jnp.float32) * 0.02, 'b1': jnp.zeros((DEPTH, 2 * HID), jnp.float32), 'w2': jax.random.normal(ks[4], (DEPTH, HID, DIM), jnp.float32) * 0.02, 'b2': jnp.zeros((DEPTH, DIM), jnp.float32)}
    _L0_ffn_in = _L0_ffn_setup()
    _d = {'L0_attn_hidden_states': _L0_attn_in['hidden_states'], 'L0_attn_Wq': _L0_attn_in['Wq'], 'L0_attn_Wk': _L0_attn_in['Wk'], 'L0_attn_Wv': _L0_attn_in['Wv'], 'L0_attn_conv_q': _L0_attn_in['conv_q'], 'L0_attn_conv_k': _L0_attn_in['conv_k'], 'L0_attn_conv_v': _L0_attn_in['conv_v'], 'L0_attn_Wb': _L0_attn_in['Wb'], 'L0_attn_Wdec': _L0_attn_in['Wdec'], 'L0_attn_Wmix': _L0_attn_in['Wmix'], 'L0_attn_conv_mix': _L0_attn_in['conv_mix'], 'L0_attn_mix_bias': _L0_attn_in['mix_bias'], 'L0_attn_rms_w': _L0_attn_in['rms_w'], 'L0_attn_Wo': _L0_attn_in['Wo'], 'L0_ffn_wqkv': _L0_ffn_in['wqkv'], 'L0_ffn_q_scale': _L0_ffn_in['q_scale'], 'L0_ffn_k_scale': _L0_ffn_in['k_scale'], 'L0_ffn_wo': _L0_ffn_in['wo'], 'L0_ffn_ln_g': _L0_ffn_in['ln_g'], 'L0_ffn_ln_b': _L0_ffn_in['ln_b'], 'L0_ffn_w1': _L0_ffn_in['w1'], 'L0_ffn_b1': _L0_ffn_in['b1'], 'L0_ffn_w2': _L0_ffn_in['w2'], 'L0_ffn_b2': _L0_ffn_in['b2']}
    _x0 = _d['L0_attn_hidden_states']
    _d['L0_attn_hidden_states'] = jax.random.normal(jax.random.fold_in(jax.random.key(seed), 1), (2, 2048, 256), dtype=_x0.dtype)
    del _x0
    return _d

def reference(L0_attn_hidden_states, L0_attn_Wq, L0_attn_Wk, L0_attn_Wv, L0_attn_conv_q, L0_attn_conv_k, L0_attn_conv_v, L0_attn_Wb, L0_attn_Wdec, L0_attn_Wmix, L0_attn_conv_mix, L0_attn_mix_bias, L0_attn_rms_w, L0_attn_Wo, L0_ffn_wqkv, L0_ffn_q_scale, L0_ffn_k_scale, L0_ffn_wo, L0_ffn_ln_g, L0_ffn_ln_b, L0_ffn_w1, L0_ffn_b1, L0_ffn_w2, L0_ffn_b2):

    def _L0_attn_ref(hidden_states, Wq, Wk, Wv, conv_q, conv_k, conv_v, Wb, Wdec, Wmix, conv_mix, mix_bias, rms_w, Wo):
        import jax, jax.numpy as jnp
        import numpy as np
        CHUNK = 32
        HEADS = 4
        EPS_RMS = 1e-05

        def silu(x):
            return jax.nn.silu(x)

        def l2norm(x, eps=1e-06):
            return x * jax.lax.rsqrt(jnp.sum(x * x, axis=-1, keepdims=True) + eps)

        def short_conv(x, w):
            K = w.shape[1]
            L = x.shape[1]
            xp = jnp.pad(x, ((0, 0), (K - 1, 0), (0, 0)))
            out = xp[:, 0:L, :] * w[:, 0]
            for k in range(1, K):
                out = out + xp[:, k:k + L, :] * w[:, k]
            return out

        def delta_rule_chunkwise(q, k, v, beta, chunk=CHUNK):
            b, h, l, dk = q.shape
            dv = v.shape[-1]
            n = l // chunk
            q = l2norm(q)
            k = l2norm(k)
            v = v * beta[..., None]
            k_beta = k * beta[..., None]
            resh = lambda x: x.reshape(b, h, n, chunk, -1)
            q, k, v, k_beta = map(resh, (q, k, v, k_beta))
            strict_lower = jnp.tril(jnp.ones((chunk, chunk), bool), -1)
            attn = jnp.where(strict_lower, -(k_beta @ jnp.swapaxes(k, -1, -2)), 0.0)
            for i in range(1, chunk):
                row = attn[..., i, :]
                new = attn[..., i, :i] + jnp.einsum('...j,...jk->...k', row, attn[..., :, :i])
                attn = attn.at[..., i, :i].set(new)
            attn = attn + jnp.eye(chunk, dtype=attn.dtype)
            u = attn @ v
            w = attn @ k_beta
            lower_incl = jnp.tril(jnp.ones((chunk, chunk), bool))
            qc, kc, uc, wc = [jnp.moveaxis(x, 2, 0) for x in (q, k, u, w)]
            S0 = jnp.zeros((b, h, dk, dv), q.dtype)

            def step(S, inp):
                q_i, k_i, u_i, w_i = inp
                attn_i = jnp.where(lower_incl, q_i @ jnp.swapaxes(k_i, -1, -2), 0.0)
                u_adj = u_i - w_i @ S
                o_i = q_i @ S + attn_i @ u_adj
                S = S + jnp.swapaxes(k_i, -1, -2) @ u_adj
                return (S, o_i)
            S, o = jax.lax.scan(step, S0, (qc, kc, uc, wc))
            o = jnp.moveaxis(o, 0, 2).reshape(b, h, l, dv)
            return (o, S)

        def ema_rule(v, gamma):
            v_t = jnp.moveaxis(v, 2, 0)
            g_t = jnp.moveaxis(gamma, 2, 0)
            s0 = jnp.zeros(v.shape[:2] + (v.shape[-1],), v.dtype)

            def step(s, inp):
                vt, gt = inp
                s = gt[..., None] * s + (1.0 - gt[..., None]) * vt
                return (s, s)
            s_fin, out = jax.lax.scan(step, s0, (v_t, g_t))
            return (jnp.moveaxis(out, 0, 2), s_fin)

        def rms_norm(x, w, eps=EPS_RMS):
            return x * jax.lax.rsqrt(jnp.mean(x * x, axis=-1, keepdims=True) + eps) * w
        b, l, d = hidden_states.shape
        H = HEADS
        dk = d // H
        dv = d // H
        q = silu(short_conv(hidden_states @ Wq, conv_q))
        k = silu(short_conv(hidden_states @ Wk, conv_k))
        v = silu(short_conv(hidden_states @ Wv, conv_v))
        mix_inp = silu(short_conv(hidden_states @ Wmix, conv_mix))
        q = silu(q)
        k = silu(k)
        to_heads = lambda x, dh: jnp.transpose(x.reshape(b, l, H, dh), (0, 2, 1, 3))
        q_d = to_heads(q, dk)
        k_d = to_heads(k, dk)
        v_d = to_heads(v, dv)
        beta = jax.nn.sigmoid(hidden_states @ Wb)
        beta_d = jnp.transpose(beta, (0, 2, 1))
        o_d, S = delta_rule_chunkwise(q_d, k_d, v_d, beta_d)
        o_d = jnp.transpose(o_d, (0, 2, 1, 3))
        gamma = jax.nn.sigmoid(hidden_states @ Wdec)
        gamma_d = jnp.transpose(gamma, (0, 2, 1))
        ema_out, ema_state = ema_rule(v_d, gamma_d)
        ema_out = jnp.transpose(ema_out, (0, 2, 1, 3))
        mix = jax.nn.sigmoid(mix_inp + mix_bias)
        o = (1.0 - mix[..., None]) * o_d + mix[..., None] * ema_out
        o = rms_norm(o, rms_w)
        out = o.reshape(b, l, H * dv) @ Wo
        return out

    def _L0_ffn_ref(x, wqkv, q_scale, k_scale, wo, ln_g, ln_b, w1, b1, w2, b2):
        import jax, jax.numpy as jnp
        import numpy as np
        DIM = 256
        DEPTH = 2
        HEADS = 8
        DIM_HEAD = 64
        WINDOW = 128
        INNER = HEADS * DIM_HEAD
        HID = int(DIM * 4 * 2 / 3)
        B, N = (2, 2048)
        QK_SCALE = 8.0

        def shift_token(t):
            t1, t2 = jnp.split(t, 2, axis=-1)
            t2 = jnp.pad(t2, ((0, 0), (1, 0), (0, 0)))[:, :-1]
            return jnp.concatenate([t1, t2], axis=-1)

        def l2norm(t):
            return t / jnp.clip(jnp.linalg.norm(t, axis=-1, keepdims=True), 1e-12)

        def rotate_half(x):
            x1, x2 = jnp.split(x, 2, axis=-1)
            return jnp.concatenate([-x2, x1], axis=-1)

        def rotary_xpos(q, k):
            n = q.shape[-2]
            half_idx = jnp.arange(0, DIM_HEAD, 2, dtype=jnp.float32)
            inv_freq = 1.0 / 10000.0 ** (half_idx / DIM_HEAD)
            t = jnp.arange(n, dtype=jnp.float32)
            freqs = t[:, None] * inv_freq[None, :]
            freqs = jnp.concatenate([freqs, freqs], axis=-1)
            base = (half_idx + 0.4 * DIM_HEAD) / (1.4 * DIM_HEAD)
            power = (t - n // 2) / float(WINDOW // 2)
            scale = base[None, :] ** power[:, None]
            scale = jnp.concatenate([scale, scale], axis=-1)
            cos, sin = (jnp.cos(freqs), jnp.sin(freqs))
            q = q * cos * scale + rotate_half(q) * sin * scale
            k = k * cos / scale + rotate_half(k) * sin / scale
            return (q, k)

        def local_attention(q, k, v):
            b, h, n, d = q.shape
            w = n // WINDOW
            bq = q.reshape(b, h, w, WINDOW, d) * QK_SCALE
            bk = k.reshape(b, h, w, WINDOW, d)
            bv = v.reshape(b, h, w, WINDOW, d)

            def look_around(t):
                p = jnp.pad(t, ((0, 0), (0, 0), (1, 0), (0, 0), (0, 0)))
                return jnp.concatenate([p[:, :, :w], p[:, :, 1:]], axis=3)
            bk, bv = (look_around(bk), look_around(bv))
            bt = jnp.arange(n).reshape(w, WINDOW)
            btp = jnp.pad(bt, ((1, 0), (0, 0)), constant_values=-1)
            btk = jnp.concatenate([btp[:w], btp[1:]], axis=1)
            sim = jnp.einsum('bhwid,bhwjd->bhwij', bq, bk)
            i = bt[:, :, None]
            j = btk[:, None, :]
            mask = (i < j) | (i > j + WINDOW) | (j == -1)
            sim = jnp.where(mask, -jnp.finfo(sim.dtype).max, sim)
            attn = jax.nn.softmax(sim, axis=-1)
            out = jnp.einsum('bhwij,bhwjd->bhwid', attn, bv)
            return out.reshape(b, h, n, d)

        def _layer(x, wqkv, qs, ksc, wo, lg, lb, w1, b1, w2, b2):
            b, n, _ = x.shape
            h = shift_token(x)
            qkv = h @ wqkv
            q, k, v = jnp.split(qkv, 3, axis=-1)
            to_heads = lambda t: t.reshape(b, n, HEADS, DIM_HEAD).transpose(0, 2, 1, 3)
            q, k, v = (to_heads(q), to_heads(k), to_heads(v))
            q = l2norm(q) * qs
            k = l2norm(k) * ksc
            q, k = rotary_xpos(q, k)
            o = local_attention(q, k, v)
            o = o.transpose(0, 2, 1, 3).reshape(b, n, INNER)
            x = x + o @ wo
            h = shift_token(x)
            mu = h.mean(-1, keepdims=True)
            var = h.var(-1, keepdims=True)
            h = (h - mu) / jnp.sqrt(var + 1e-05) * lg + lb
            h = h @ w1 + b1
            a, g = jnp.split(h, 2, axis=-1)
            h = a * jax.nn.gelu(g, approximate=False)
            x = x + h @ w2 + b2
            return x
        for l in range(DEPTH):
            x = _layer(x, wqkv[l], q_scale[l], k_scale[l], wo[l], ln_g[l], ln_b[l], w1[l], b1[l], w2[l], b2[l])
        return x
    x = L0_attn_hidden_states
    x = _layernorm(x + _L0_attn_ref(x, L0_attn_Wq, L0_attn_Wk, L0_attn_Wv, L0_attn_conv_q, L0_attn_conv_k, L0_attn_conv_v, L0_attn_Wb, L0_attn_Wdec, L0_attn_Wmix, L0_attn_conv_mix, L0_attn_mix_bias, L0_attn_rms_w, L0_attn_Wo), axis=-1)
    x = _layernorm(x + _L0_ffn_ref(x, L0_ffn_wqkv, L0_ffn_q_scale, L0_ffn_k_scale, L0_ffn_wo, L0_ffn_ln_g, L0_ffn_ln_b, L0_ffn_w1, L0_ffn_b1, L0_ffn_w2, L0_ffn_b2), axis=-1)
    return x

_drawn_inputs = setup_inputs


def setup_inputs(seed=0):
    import zlib

    import numpy as np

    out = dict(_drawn_inputs(seed))
    spreads = {'L0_attn_mix_bias': (-2.0, 0.6),
     'L0_attn_rms_w': (1.0, 0.2),
     'L0_ffn_q_scale': (1.0, 0.6),
     'L0_ffn_k_scale': (1.0, 0.6),
     'L0_ffn_ln_g': (1.0, 0.6),
     'L0_ffn_ln_b': (0.0, 0.8),
     'L0_ffn_b1': (0.0, 0.8),
     'L0_ffn_b2': (0.0, 0.1)}
    factors = {'L0_attn_Wdec': 6.775,
     'L0_attn_Wmix': 8.0,
     'L0_attn_conv_mix': 8.0,
     'L0_ffn_wqkv': 3.332,
     'L0_ffn_wo': 3.296}
    for name, (base, spread) in spreads.items():
        noise = np.random.default_rng([zlib.crc32(name.encode()), seed]).standard_normal(out[name].shape)
        drawn = base * np.exp(spread * noise) if base else spread * noise
        out[name] = jnp.asarray(drawn.astype(out[name].dtype))
    for name, factor in factors.items():
        out[name] = (out[name] * factor).astype(out[name].dtype)
    return out
```

```python
from contextlib import ExitStack

import concourse.bass as bass
from concourse import mybir

F32 = mybir.dt.float32
BF16 = mybir.dt.bfloat16
ALU = mybir.AluOpType
ACT = mybir.ActivationFunctionType
AX = mybir.AxisListType

P = 128
B, L, D = 2, 2048, 256
W = 128
NW = L // W
UNITS = B * NW
DEPTH = 2
FH, DH = 8, 64
INNER = FH * DH
HID = int(D * 4 * 2 / 3)
HC = HID // 2
NU = -(-HID // P)
AH, DA = 4, 64
CK = 4
NF = 3 * D // P
NLEV = 6
LN_EPS = 1e-5
RMS_EPS = 1e-5
MASKED = -1e30
AHEAD = 2


class Signal:

    def __init__(self, sem, per=1):
        self.sem, self.sems, self.per = sem, [sem], per

    def __call__(self, n, k=0):
        return self.sem, (n + AHEAD) * self.per + k + 1


class EachSignal:

    def __init__(self, sems, per=1):
        self.sems, self.per = sems, per

    def __call__(self, n, b, k=0):
        return self.sems[b], (n + AHEAD) * self.per + k + 1


def credit(eng, signals):
    for s in signals:
        for sem in s.sems:
            eng.sem_inc(sem, AHEAD * s.per)


def before(reads, n, use):
    signal, k = reads[use - 1]
    return signal(n if use else n - 1, k)


def head_of(g, j):
    return 4 * (g // 2) + 2 * j + g % 2


def over_heads(ap, heads):
    return ap.unsqueeze(1).broadcast_to([ap.shape[0], heads, ap.shape[1]])


def along(ap, n):
    return ap.unsqueeze(2).broadcast_to([ap.shape[0], ap.shape[1], n])


def setup(nc, sems, a, t):
    with ExitStack() as ctx:
        def sb(name, shape, dt=F32):
            return ctx.enter_context(nc.sbuf_tensor("s_" + name, shape, dt))

        def sem(name):
            return sems.enter_context(nc.semaphore("s_" + name))

        lg = sb("lg", [P, DEPTH, 2])
        lb = sb("lb", [P, DEPTH, 2])
        row = sb("row", [1, DEPTH, 2 * HID + D])
        rest = sb("rest", [1, DEPTH, 2 * HID + D])
        rest2 = sb("rest2", [1, DEPTH, 2 * HID + D])
        parts = sb("parts", [1, 3, DEPTH, 2 * HID + D], BF16)
        shift_ps = [ctx.enter_context(nc.psum_tensor(f"s_shift{i}", [P, 512], F32)) for i in range(8)]
        loaded, w1_loaded, zeroed, tables = sem("loaded"), sem("w1_loaded"), sem("zeroed"), sem("tables")
        shifted, added, split, spread, folded = sem("shifted"), sem("added"), sem("split"), sem("spread"), sem("folded")
        block = ctx.enter_context(nc.Block())

        @block.sync
        def _(sp):
            sp.dma_start(t["w1"][:], a["w1"].rearrange("l (k p) n -> p l k n", p=P)).then_inc(w1_loaded, 16)
            sp.dma_start(lg[:], a["ln_g"].rearrange("l (k p) -> p l k", p=P), allow_slow_non_contiguous=True).then_inc(w1_loaded, 16)
            sp.dma_start(lb[:], a["ln_b"].rearrange("l (k p) -> p l k", p=P), allow_slow_non_contiguous=True).then_inc(w1_loaded, 16)
            sp.dma_start(row[:, :, 0:2 * HID], a["b1"].rearrange("(o l) n -> o l n", o=1)).then_inc(w1_loaded, 16)
            sp.dma_start(row[:, :, 2 * HID:], a["b2"].rearrange("(o l) n -> o l n", o=1)).then_inc(w1_loaded, 16)
            sp.dma_start(t["wqkv"][:], a["wqkv"].rearrange("l (k p) n -> p l k n", p=P)).then_inc(loaded, 16)
            sp.dma_start(t["wo"][:], a["wo"].rearrange("l (k p) n -> p l k n", p=P)).then_inc(loaded, 16)
            full = (NU - 1) * P
            for l in range(DEPTH):
                sp.dma_start(t["w2"][:, l, 0:NU - 1, :], a["w2"][l, 0:full, :].rearrange("(k p) n -> p k n", p=P))\
                    .then_inc(loaded, 16)
            sp.dma_start(t["w2"][0:HID - full, :, NU - 1, :], a["w2"][:, full:HID, :].rearrange("l p n -> p l n"))\
                .then_inc(loaded, 16)
            sp.dma_start(t["rope"][:].rearrange("p (w c) -> p w c", w=NW), a["rope"].rearrange("(w p) c -> p w c", p=P))\
                .then_inc(loaded, 16)
            sp.wait_ge(split, 5)
            for i in range(3):
                sp.dma_start(t["bias1"][i:i + 1, :, :], parts[:, i, :, 0:2 * HID]).then_inc(spread, 16)
                sp.dma_start(t["bias2"][i:i + 1, :, :], parts[:, i, :, 2 * HID:]).then_inc(spread, 16)
            sp.wait_ge(spread, 16 * 6)
            sp.wait_ge(loaded, 16 * (4 + DEPTH))

        @block.scalar
        def _(act):
            n = 0
            for l in range(DEPTH):
                for i, name in enumerate(("q_scale", "k_scale")):
                    src = a[name][l:l + 1, :]
                    first = 2 * i * DH
                    for to, frm, size in ((0, 0, DH), (DH, DH // 2, DH // 2), (DH + DH // 2, 0, DH // 2)):
                        act.dma_start(t["scales"][:, l, first + to:first + to + size],
                                      src[:, frm:frm + size].broadcast_to([P, size])).then_inc(tables, 16)
                        n += 1
            act.wait_ge(tables, 16 * n)

        @block.gpsimd
        def _(pool):
            for i, (tile, value) in enumerate(((t["identb"], 0.0), (t["mask"], 0.0), (t["bias1"], 0.0),
                                               (t["bias2"], 0.0), (t["ones3"], 1.0))):
                pool.memset(tile[:], value).then_inc(zeroed, 1)
            pool.wait_ge(zeroed, 5)
            pool.affine_select(out=t["identb"][:], in_=t["identb"][:], compare_op=ALU.not_equal, fill=1.0, base=0,
                               pattern=[[-1, P]], channel_multiplier=1).then_inc(zeroed, 1)
            m = t["mask"][:].rearrange("p (w a k) -> p w a k", w=NW, a=2)
            pool.affine_select(out=m[:, :, 0, :], in_=m[:, :, 0, :], compare_op=ALU.is_ge, fill=MASKED, base=0,
                               pattern=[[0, NW], [1, W]], channel_multiplier=-1).then_inc(zeroed, 1)
            pool.affine_select(out=m[:, :, 1, :], in_=m[:, :, 1, :], compare_op=ALU.is_ge, fill=MASKED, base=0,
                               pattern=[[0, NW], [-1, W]], channel_multiplier=1).then_inc(zeroed, 1)
            pool.wait_ge(zeroed, 8)
            pool.memset(m[:, 0, 0, :], MASKED).then_inc(zeroed, 1)
            pool.wait_ge(shifted, 1)
            for l in range(DEPTH):
                for k in range(2):
                    pool.tensor_scalar(t["w1"][:, l, k, :], t["w1"][:, l, k, :], lg[:, l, k:k + 1], None, ALU.mult)\
                        .then_inc(folded, 1)
            pool.wait_ge(folded, 2 * DEPTH)
            pool.wait_ge(zeroed, 9)

        @block.tensor
        def _(pe):
            pe.wait_ge(w1_loaded, 16 * 5)
            for l in range(DEPTH):
                for c in range(4):
                    for k in range(2):
                        mm = pe.matmul(shift_ps[4 * l + c][0:1, 0:HC], lb[:, l, k:k + 1], t["w1"][:, l, k, c * HC:(c + 1) * HC],
                                       start=(k == 0), stop=(k == 1))
            mm.then_inc(shifted, 1)

        @block.vector
        def _(dve):
            dve.wait_ge(shifted, 1)
            for l in range(DEPTH):
                for c in range(4):
                    cols = slice(c * HC, (c + 1) * HC)
                    dve.tensor_tensor(row[:, l, cols], row[:, l, cols], shift_ps[4 * l + c][0:1, 0:HC], ALU.add).then_inc(added, 1)
            dve.wait_ge(added, 4 * DEPTH)
            dve.wait_ge(zeroed, 5)
            dve.tensor_copy(parts[:, 0], row[:]).then_inc(split, 1)
            dve.wait_ge(split, 1)
            dve.tensor_tensor(rest[:], row[:], parts[:, 0], ALU.subtract).then_inc(split, 1)
            dve.wait_ge(split, 2)
            dve.tensor_copy(parts[:, 1], rest[:]).then_inc(split, 1)
            dve.wait_ge(split, 3)
            dve.tensor_tensor(rest2[:], rest[:], parts[:, 1], ALU.subtract).then_inc(split, 1)
            dve.wait_ge(split, 4)
            dve.tensor_copy(parts[:, 2], rest2[:]).then_inc(split, 1)


def delta_layer(nc, sems, t, a, x_norm_dram):
    with ExitStack() as ctx:
        def sb(name, shape, dt=F32):
            return ctx.enter_context(nc.sbuf_tensor("a_" + name, shape, dt))

        def pb(name):
            return ctx.enter_context(nc.psum_tensor("a_" + name, [P, 512], F32))

        held = []

        def sem(name):
            held.append(sems.enter_context(nc.semaphore("a_" + name)))
            return held[-1]

        def signal(name, per=1):
            return Signal(sem(name), per)

        def signals(name, per=1):
            return EachSignal([sem(f"{name}{b}") for b in range(B)], per)

        def each(name, shape):
            return [sb(f"{name}{b}", shape) for b in range(B)]

        X, ident, nhalf = t["X"], t["ident"], t["nhalf"]

        wA = sb("wA", [P, 2, 3 * D])
        wbeta = sb("wbeta", [P, 2, AH])
        wmix = sb("wmix", [P, 2, AH])
        wdec = sb("wdec", [P, 2, AH])
        wdecw = sb("wdecw", [P, 2, D])
        woA = sb("woA", [P, 2, D])
        rmsw = sb("rmsw", [P, 1])
        cw = sb("cw", [P, NF, CK])
        cmix = sb("cmix", [AH, CK])
        mbias = sb("mbias", [AH, 1])
        mhalf = sb("mhalf", [AH, 1])
        tables = sb("tables", [P, NLEV + 3, P])
        xT = sb("xT", [P, B, 2, P])
        pre = sb("pre", [P, NF, B, CK - 1 + P])
        prem = sb("prem", [AH, B, CK - 1 + P])
        conv = sb("conv", [P, NF, B, P])
        convm = sb("convm", [AH, B, P])
        th = sb("th", [P, NF, B, P])
        thm = sb("thm", [AH, B, P])
        s1 = sb("s1", [P, NF, B, P])
        s1m = sb("s1m", [AH, B, P])
        mth = sb("mth", [AH, B, P])
        s2 = sb("s2", [P, 4, B, P])
        gth = sb("gth", [P, 2, B, P])
        gam = sb("gam", [P, 2, B, P])
        inn = sb("inn", [P, 2, B, P])
        ema = sb("ema", [P, 2, B, P])
        est = sb("est", [P, 2, B])
        xw = each("xw", [P, D])
        bth = each("bth", [P, AH])
        beta = each("beta", [P, 2, AH])
        mixs = each("mixs", [P, 2, AH])
        sqa = each("sqa", [P, 2 * D])
        ss = each("ss", [P, 2 * AH])
        se = each("se", [P, 2 * AH])
        rn = each("rn", [P, 2 * AH])
        qk = each("qk", [P, 2 * D])
        vb = each("vb", [P, D])
        emat = each("emat", [P, D])
        kb = each("kb", [P, D])
        tT = each("tT", [P, 2, 3, P])
        LP = each("LP", [P, AH, 2, P])
        m1 = each("m1", [P, AH, P])
        R = each("R", [P, AH, P])
        T = each("T", [P, AH, P])
        Xs = each("Xs", [P, AH, P])
        St = each("St", [P, 2, DA])
        r = each("r", [P, AH, DA])
        u = each("u", [P, AH, DA])
        om = each("om", [P, D])
        em = each("em", [P, D])
        o2 = each("o2", [P, D])
        sqo = each("sqo", [P, D])
        so = each("so", [P, AH])
        sv = each("sv", [P, AH])
        ro = each("ro", [P, AH])
        o3 = each("o3", [P, D])
        o3T = each("o3T", [P, 2, P])
        xs = each("xs", [P, D])
        st = each("st", [P, 6])
        mv = each("mv", [P, 2])
        ve = each("ve", [P, 1])
        rstd = each("rstd", [P, 1])

        FA, FB, FC, Z = pb("FA"), pb("FB"), pb("FC"), pb("Z")
        Q0 = [pb("Q00"), pb("Q01")]
        Q1 = [pb("Q10"), pb("Q11")]

        xw_ready = signals("xw_ready")
        q0_full, q1_full = signals("q0_full", 2 * NLEV + 3), signals("q1_full", NLEV + 3)
        xT_ready = signals("xT_ready")
        pre_qk, pre_v, gth_ready, bth_ready, prem_ready = (signals(x) for x in ("pre_qk", "pre_v", "gth", "bth", "prem"))
        beta_ready = signals("beta_ready", 2)
        sqa_ready, ss_ready, se_ready, rn_ready, qk_ready = (signals(x) for x in ("sqa", "ss", "se", "rn", "qk"))
        vb_ready, emat_ready, kb_ready = (signals(x) for x in ("vb", "emat", "kb"))
        mixs_ready = signals("mixs", 2)
        kbq_turned, k_turned = signals("kbq_turned"), signals("k_turned")
        lp_ready = signals("lp", 2)
        m1_ready, R_ready, T_ready, Xs_ready = signals("m1"), signals("R", NLEV + 1), signals("T", NLEV), signals("Xs", NLEV)
        r_ready, u_ready, S_ready = signals("r", 2), signals("u"), signals("S")
        om_ready, em_ready, o2_ready = signals("om", 2), signals("em"), signals("o2")
        sqo_ready, so_ready, sv_ready, ro_ready, o3_ready = (signals(x) for x in ("sqo", "so", "sv", "ro", "o3"))
        o3T_ready, xs_ready, st_ready, mv_ready, ve_ready, rstd_ready, x_ready = (
            signals(x) for x in ("o3T", "xs", "st", "mv", "ve", "rstd", "x"))
        fa_full, fb_full, fc_full, z_full = signal("fa_full", 6), signal("fb_full", 6), signal("fc_full", 10), signal("z_full", 4)
        conv_done, convm_done = signal("conv", NF * CK), signal("convm", CK)
        carried = signal("carried", 2)
        th_ready, s1_ready, th2_ready, s2_ready = signal("th", 2), signal("s1", 2), signal("th2"), signal("s2")
        thm_ready, s1m_ready, mth_ready = signal("thm"), signal("s1m"), signal("mth")
        gam_ready, inn_ready, ema_ready, est_ready = signal("gam"), signal("inn"), signal("ema", 2 * B), signal("est")
        weights, folded, zeroed, stored = sem("weights"), sem("folded"), sem("zeroed"), sem("stored")
        passed_pe, passed_dve, passed_pool = sem("passed_pe"), sem("passed_dve"), sem("passed_pool")
        N_WEIGHTS = 19
        N_ZEROED = 3 + B

        fa_read = [(xT_ready, b, 0) for b in range(B)] + [(qk_ready, b, 0) for b in range(B)] + [(kbq_turned, b, 0) for b in range(B)]
        fb_read = [(pre_qk, b, 0) for b in range(B)] + [(emat_ready, b, 0) for b in range(B)] + [(lp_ready, b, 0) for b in range(B)]
        fc_read = [(s, b, 0) for b in range(B) for s in (gth_ready, prem_ready)] + [(mixs_ready, b, 1) for b in range(B)]\
            + [(k_turned, b, 0) for b in range(B)] + [(lp_ready, b, 1) for b in range(B)]
        z_read = [(om_ready, b, 1) for b in range(B)] + [(o3T_ready, b, 0) for b in range(B)]
        q0_read = [x for i in range(NLEV) for x in ((T_ready, i), (Xs_ready, i))] + [(r_ready, 0), (u_ready, 0), (S_ready, 0)]
        q1_read = [(R_ready, i + 1) for i in range(NLEV)] + [(r_ready, 1), (om_ready, 0), (xs_ready, 0)]

        def freed_pair(reads, w, use):
            signal, b, k = reads[use - 1]
            return signal(w if use else w - 1, b, k)

        def freed(reads, w, b, use):
            signal, k = reads[use - 1]
            return signal(w if use else w - 1, b, k)

        block = ctx.enter_context(nc.Block())

        def pairs(eng, early, late, at):
            for step in early(0):
                pass

            def pair(w, ahead):
                steps = early(w + 1) if ahead else iter(())
                for i, _ in enumerate(late(w)):
                    for _ in range(at.count(i)):
                        next(steps, None)
                for _ in steps:
                    pass

            with eng.Fori(0, NW - 1) as w:
                pair(w, True)
            pair(NW - 1, False)

        @block.tensor
        def _(pe):
            credit(pe, [fa_full, fb_full, fc_full, q0_full, q1_full, z_full])
            pe.wait_ge(folded, 3)
            pe.wait_ge(zeroed, N_ZEROED)

            def early(w):
                for b in range(B):
                    pe.wait_ge(*xw_ready(w, b))
                    pe.wait_ge(*freed_pair(fa_read, w, b))
                    for j in range(2):
                        mm = pe.transpose(FA[:, j * P:(j + 1) * P], xw[b][:, j * P:(j + 1) * P], ident[:])
                    mm.then_inc(fa_full.sem, 1)
                yield
                for b in range(B):
                    pe.wait_ge(*xT_ready(w, b))
                    pe.wait_ge(*freed_pair(fb_read, w, b))
                    for f in range(4):
                        for k in range(2):
                            mm = pe.matmul(FB[:, f * P:(f + 1) * P], wA[:, k, f * P:(f + 1) * P], xT[:, b, k, :],
                                           start=(k == 0), stop=(k == 1))
                    mm.then_inc(fb_full.sem, 1)
                    yield
                    pe.wait_ge(*freed_pair(fc_read, w, 2 * b))
                    for f in range(4):
                        for k in range(2):
                            lhsT = wA[:, k, (4 + f) * P:(5 + f) * P] if f < 2 else wdecw[:, k, (f - 2) * P:(f - 1) * P]
                            mm = pe.matmul(FC[:, f * P:(f + 1) * P], lhsT, xT[:, b, k, :], start=(k == 0), stop=(k == 1))
                    mm.then_inc(fc_full.sem, 1)
                    yield
                    pe.wait_ge(*freed_pair(fc_read, w, 2 * b + 1))
                    for k in range(2):
                        pe.matmul(FC[:, 0:AH], xT[:, b, k, :], wbeta[:, k, :], start=(k == 0), stop=(k == 1))
                    for k in range(2):
                        mm = pe.matmul(FC[0:AH, P:2 * P], wmix[:, k, :], xT[:, b, k, :], start=(k == 0), stop=(k == 1))
                    mm.then_inc(fc_full.sem, 1)
                    yield

            def turn(bank, full, w, use, reads, tiles):
                pe.wait_ge(*freed_pair(reads, w, use))
                for i, tile in enumerate(tiles):
                    mm = pe.transpose(bank[:, i * P:(i + 1) * P], tile, ident[:])
                mm.then_inc(full.sem, 1)

            def late(w):
                pe.wait_ge(*mth_ready(w))
                for b in range(B):
                    pe.wait_ge(*freed_pair(fc_read, w, 4 + b))
                    pe.sem_inc(passed_pe, 1)
                    pe.transpose(FC[:, 0:AH], mth[:, b, :], ident[0:AH, 0:AH]).then_inc(fc_full.sem, 1)
                pe.wait_ge(*s2_ready(w))
                pe.wait_ge(*ema_ready(w, 2 * B - 1))
                for b in range(B):
                    turn(FA, fa_full, w, 2 + b, fa_read, [s2[:, f, b, :] for f in range(4)])
                    turn(FB, fb_full, w, 2 + b, fb_read, [s1[:, 4 + f, b, :] for f in range(2)] + [ema[:, f, b, :] for f in range(2)])
                for b in range(B):
                    pe.wait_ge(*kb_ready(w, b))
                    turn(FA, fa_full, w, 4 + b, fa_read,
                         [x for f in range(2) for x in (kb[b][:, f * P:(f + 1) * P], qk[b][:, f * P:(f + 1) * P])])
                    turn(FC, fc_full, w, 6 + b, fc_read, [qk[b][:, (2 + f) * P:(3 + f) * P] for f in range(2)])
                for b in range(B):
                    pe.wait_ge(*kbq_turned(w, b))
                    pe.wait_ge(*k_turned(w, b))
                    for e, (bank, full, use, reads) in enumerate(((FB, fb_full, 4, fb_read), (FC, fc_full, 8, fc_read))):
                        pe.wait_ge(*freed_pair(reads, w, use + b))
                        rows = slice(DA * e, DA * (e + 1))
                        for f in range(2):
                            mm = pe.matmul(bank[:, f * 2 * P:(f + 1) * 2 * P], tT[b][rows, f, 2, :],
                                           tT[b][rows, f, 0:2, :].rearrange("p a k -> p (a k)"), start=True, stop=True)
                        mm.then_inc(full.sem, 1)
                for i in range(NLEV):
                    for b in range(B):
                        pe.wait_ge(*R_ready(w, b, i))
                        pe.wait_ge(*freed(q0_read, w, b, 2 * i))
                        for h in range(AH):
                            mm = pe.transpose(Q0[b][:, h * P:(h + 1) * P], R[b][:, h, :], ident[:])
                        mm.then_inc(q0_full.sems[b], 1)
                    yield
                    for b in range(B):
                        pe.wait_ge(*T_ready(w, b, i))
                        for h in range(AH):
                            mm = pe.matmul(Q0[b][:, h * P:(h + 1) * P], LP[b][:, h, 0, :], T[b][:, h, :], start=True, stop=True)
                        mm.then_inc(q0_full.sems[b], 1)
                    yield
                    for b in range(B):
                        pe.wait_ge(*Xs_ready(w, b, i))
                        pe.wait_ge(*freed(q1_read, w, b, i))
                        for h in range(AH):
                            mm = pe.matmul(Q1[b][:, h * P:(h + 1) * P], Xs[b][:, h, :], R[b][:, h, :], start=True, stop=True)
                        mm.then_inc(q1_full.sems[b], 1)
                    yield
                for b in range(B):
                    pe.wait_ge(*S_ready(w - 1, b))
                    for e, (bank, full, reads, use) in enumerate(((Q0[b], q0_full, q0_read, 2 * NLEV), (Q1[b], q1_full, q1_read, NLEV))):
                        pe.wait_ge(*freed(reads, w, b, use))
                        rows = slice(DA * e, DA * (e + 1))
                        for f in range(2):
                            mm = pe.matmul(bank[:, f * DA:(f + 1) * DA], tT[b][rows, f, 0, :], St[b][rows, f, :], start=True, stop=True)
                        mm.then_inc(full.sems[b], 1)
                for b in range(B):
                    pe.wait_ge(*r_ready(w, b, 1))
                    pe.wait_ge(*R_ready(w, b, NLEV))
                    for h in range(AH):
                        mm = pe.matmul(Q0[b][:, h * DA:(h + 1) * DA], R[b][:, h, :], r[b][:, h, :], start=True, stop=True)
                    mm.then_inc(q0_full.sems[b], 1)
                for b in range(B):
                    pe.wait_ge(*u_ready(w, b))
                    for e in range(2):
                        bank = (Q1[b], Z)[e]
                        pe.wait_ge(*(freed_pair(z_read, w, b) if e else freed(q1_read, w, b, NLEV + 1)))
                        rows = slice(DA * e, DA * (e + 1))
                        for f in range(2):
                            h = 2 * e + f
                            cols = slice(f * DA, (f + 1) * DA)
                            pe.matmul(bank[:, cols], tT[b][rows, f, 1, :], St[b][rows, f, :], start=True, stop=False)
                            mm = pe.matmul(bank[:, cols], LP[b][:, h, 1, :], u[b][:, h, :], start=False, stop=True)
                        mm.then_inc((q1_full.sems[b], z_full.sem)[e], 1)
                for b in range(B):
                    for e in range(2):
                        for f in range(2):
                            mm = pe.matmul(Q0[b][DA * e:DA * (e + 1), f * DA:(f + 1) * DA],
                                           qk[b][:, D + (2 * f + e) * DA:D + (2 * f + e + 1) * DA], u[b][:, 2 * e + f, :],
                                           start=True, stop=True)
                    mm.then_inc(q0_full.sems[b], 1)
                yield
                for b in range(B):
                    pe.wait_ge(*o3_ready(w, b))
                    turn(Z, z_full, w, 2 + b, z_read, [o3[b][:, f * P:(f + 1) * P] for f in range(2)])
                for b in range(B):
                    pe.wait_ge(*o3T_ready(w, b))
                    pe.wait_ge(*freed(q1_read, w, b, NLEV + 2))
                    for k in range(2):
                        mm = pe.matmul(Q1[b][:, 0:D], o3T[b][:, k, :], woA[:, k, :], start=(k == 0), stop=(k == 1))
                    mm.then_inc(q1_full.sems[b], 1)

            pairs(pe, early, late, [1, 2, 3, 4, 5, 6, 7])

        @block.vector
        def _(dve):
            credit(dve, [beta_ready, ss_ready, qk_ready, vb_ready, mixs_ready, lp_ready, m1_ready, R_ready, Xs_ready, r_ready,
                         S_ready, om_ready, o2_ready, so_ready, o3_ready, xs_ready, st_ready, mv_ready, x_ready,
                         conv_done, convm_done, s1_ready, s1m_ready, s2_ready, gam_ready, inn_ready, ema_ready])
            dve.wait_ge(weights, 16 * N_WEIGHTS)
            dve.tensor_copy(wdecw[:].rearrange("p k (h d) -> p k h d", h=AH), wdec[:].unsqueeze(3).broadcast_to([P, 2, AH, DA]))\
                .then_inc(folded, 1)
            dve.tensor_scalar(woA[:].rearrange("p k n -> p (k n)"), woA[:].rearrange("p k n -> p (k n)"), rmsw[:], None, ALU.mult)\
                .then_inc(folded, 1)
            dve.tensor_scalar(mhalf[:], mbias[:], 0.5, None, ALU.mult).then_inc(folded, 1)
            for b in range(B):
                dve.memset(St[b][:], 0.0).then_inc(zeroed, 1)
            dve.wait_ge(zeroed, N_ZEROED)

            def early(w):
                for tap in range(CK):
                    if tap == 0:
                        for b in range(B):
                            dve.wait_ge(*pre_qk(w, b))
                            dve.wait_ge(*gth_ready(w, b))
                            dve.wait_ge(*prem_ready(w, b))
                        dve.wait_ge(*th_ready(w - 1, 1))
                        dve.wait_ge(*thm_ready(w - 1))
                    for f in range(NF + 1):
                        m = f == NF
                        src, acc, c = (prem[:], convm[:], cmix) if m else (pre[:, f], conv[:, f], cw[:, f, :])
                        src = src[:, :, CK - 1 - tap:CK - 1 - tap + P]
                        weight = c[:, CK - 1 - tap:CK - tap]
                        if tap:
                            dve.wait_ge(*(convm_done(w, tap - 1) if m else conv_done(w, NF * (tap - 1) + f)))
                            op = dve.scalar_tensor_tensor(out=acc, in0=src, scalar=weight, in1=acc, op0=ALU.mult, op1=ALU.add)
                        else:
                            op = dve.tensor_scalar(acc, src, weight, None, ALU.mult)
                        op.then_inc((convm_done if m else conv_done).sem, 1)
                    yield
                for b in range(B):
                    dve.wait_ge(*gth_ready(w, b))
                dve.tensor_scalar(gam[:], gth[:], 0.5, 0.5, ALU.mult, ALU.add).then_inc(gam_ready.sem, 1)
                dve.wait_ge(*th_ready(w, 0))
                dve.scalar_tensor_tensor(out=s1[:, 0:4], in0=th[:, 0:4], scalar=1.0, in1=conv[:, 0:4], op0=ALU.add, op1=ALU.mult)\
                    .then_inc(s1_ready.sem, 1)
                dve.wait_ge(*thm_ready(w))
                dve.scalar_tensor_tensor(out=s1m[:], in0=thm[:], scalar=1.0, in1=convm[:], op0=ALU.add, op1=ALU.mult)\
                    .then_inc(s1m_ready.sem, 1)
                dve.wait_ge(*th_ready(w, 1))
                dve.wait_ge(*fb_full(w - 1, 3))
                dve.scalar_tensor_tensor(out=s1[:, 4:6], in0=th[:, 4:6], scalar=1.0, in1=conv[:, 4:6], op0=ALU.add, op1=ALU.mult)\
                    .then_inc(s1_ready.sem, 1)
                dve.wait_ge(*s1_ready(w, 1))
                dve.scalar_tensor_tensor(out=inn[:], in0=gth[:], scalar=1.0, in1=s1[:, 4:6], op0=ALU.subtract, op1=ALU.mult)\
                    .then_inc(inn_ready.sem, 1)
                dve.wait_ge(*inn_ready(w))
                dve.wait_ge(*est_ready(w - 1))
                for f in range(2):
                    for b in range(B):
                        dve.tensor_tensor_scan(ema[:, f, b, :], gam[:, f, b, :], inn[:, f, b, :], est[:, f, b:b + 1],
                                               ALU.mult, ALU.add).then_inc(ema_ready.sem, 1)
                yield
                dve.wait_ge(*th2_ready(w))
                dve.wait_ge(*fa_full(w - 1, 3))
                dve.scalar_tensor_tensor(out=s2[:], in0=th[:, 0:4], scalar=1.0, in1=s1[:, 0:4], op0=ALU.add, op1=ALU.mult)\
                    .then_inc(s2_ready.sem, 1)
                yield

            def late(w):
                for b in range(B):
                    dve.wait_ge(*bth_ready(w, b))
                    dve.tensor_scalar(beta[b][:, 0, :], bth[b][:], 0.5, 0.5, ALU.mult, ALU.add).then_inc(beta_ready.sems[b], 1)
                    dve.tensor_scalar(beta[b][:, 1, :], bth[b][:], 0.25, 0.25, ALU.mult, ALU.add).then_inc(beta_ready.sems[b], 1)
                    dve.wait_ge(*fc_full(w, 4 + b))
                    dve.tensor_scalar(mixs[b][:, 0, :], FC[:, 0:AH], 0.5, 0.5, ALU.mult, ALU.add).then_inc(mixs_ready.sems[b], 1)
                    dve.tensor_scalar(mixs[b][:, 1, :], FC[:, 0:AH], -0.5, 0.5, ALU.mult, ALU.add).then_inc(mixs_ready.sems[b], 1)
                for b in range(B):
                    dve.wait_ge(*sqa_ready(w, b))
                    dve.tensor_reduce(ss[b][:], sqa[b][:].rearrange("p (h d) -> p h d", h=2 * AH), AX.X, ALU.add)\
                        .then_inc(ss_ready.sems[b], 1)
                    dve.wait_ge(*fb_full(w, 2 + b))
                    dve.wait_ge(*beta_ready(w, b, 1))
                    dve.tensor_tensor(vb[b][:].rearrange("p (h d) -> p h d", h=AH), FB[:, 0:D].rearrange("p (h d) -> p h d", h=AH),
                                      along(beta[b][:, 1, :], DA), ALU.mult).then_inc(vb_ready.sems[b], 1)
                    dve.wait_ge(*rn_ready(w, b))
                    dve.tensor_tensor(qk[b][:].rearrange("p (h d) -> p h d", h=2 * AH), FA[:].rearrange("p (h d) -> p h d", h=2 * AH),
                                      along(rn[b][:], DA), ALU.mult).then_inc(qk_ready.sems[b], 1)
                for b in range(B):
                    for e, (bank, full, use) in enumerate(((FB, fb_full, 4), (FC, fc_full, 8))):
                        dve.wait_ge(*full(w, use + b))
                        dve.tensor_tensor(LP[b][:, 2 * e:2 * e + 2].rearrange("p f a k -> p f (a k)"),
                                          bank[:].rearrange("p (f k) -> p f k", f=2),
                                          tables[:, NLEV + 1:NLEV + 3, :].rearrange("p a k -> p (a k)").unsqueeze(1)
                                          .broadcast_to([P, 2, 2 * P]), ALU.mult).then_inc(lp_ready.sems[b], 1)
                    dve.wait_ge(*lp_ready(w, b, 1))
                    dve.tensor_tensor(m1[b][:], LP[b][:, :, 0, :], over_heads(tables[:, NLEV, :], AH), ALU.mult)\
                        .then_inc(m1_ready.sems[b], 1)
                    dve.wait_ge(*m1_ready(w, b))
                    dve.tensor_tensor(R[b][:], over_heads(ident[:], AH), m1[b][:], ALU.subtract).then_inc(R_ready.sems[b], 1)
                for i in range(NLEV):
                    for b in range(B):
                        dve.wait_ge(*q0_full(w, b, 2 * i + 1))
                        dve.tensor_tensor(Xs[b][:], Q0[b][:].rearrange("p (h k) -> p h k", h=AH), over_heads(tables[:, i, :], AH),
                                          ALU.mult).then_inc(Xs_ready.sems[b], 1)
                    yield
                    for b in range(B):
                        dve.wait_ge(*q1_full(w, b, i))
                        dve.tensor_tensor(R[b][:], R[b][:], Q1[b][:].rearrange("p (h k) -> p h k", h=AH), ALU.subtract)\
                            .then_inc(R_ready.sems[b], 1)
                    yield
                for b in range(B):
                    for e in range(2):
                        dve.wait_ge(*(q1_full(w, b, NLEV) if e else q0_full(w, b, 2 * NLEV)))
                        if e == 0:
                            dve.wait_ge(*vb_ready(w, b))
                        dve.tensor_tensor(r[b][:, 2 * e:2 * e + 2, :], vb[b][:].rearrange("p (f e d) -> p e f d", f=2, e=2)[:, e],
                                          (Q0[b], Q1[b])[e][:, 0:2 * DA].rearrange("p (f d) -> p f d", f=2), ALU.subtract)\
                            .then_inc(r_ready.sems[b], 1)
                yield
                for b in range(B):
                    for e in range(2):
                        dve.wait_ge(*(z_full(w, b) if e else q1_full(w, b, NLEV + 1)))
                        dve.tensor_tensor(om[b][:].rearrange("p (f e d) -> p e f d", f=2, e=2)[:, e],
                                          (Q1[b], Z)[e][:, 0:2 * DA].rearrange("p (f d) -> p f d", f=2),
                                          along(mixs[b][:, 1, :].rearrange("p (f e) -> p e f", e=2)[:, e], DA), ALU.mult)\
                            .then_inc(om_ready.sems[b], 1)
                    dve.wait_ge(*om_ready(w, b, 1))
                    dve.wait_ge(*em_ready(w, b))
                    dve.tensor_tensor(o2[b][:], om[b][:], em[b][:], ALU.add).then_inc(o2_ready.sems[b], 1)
                for b in range(B):
                    dve.wait_ge(*q0_full(w, b, 2 * NLEV + 2))
                    dve.tensor_tensor(St[b][:].rearrange("p f d -> p (f d)"), St[b][:].rearrange("p f d -> p (f d)"),
                                      Q0[b][:, 0:2 * DA], ALU.add).then_inc(S_ready.sems[b], 1)
                for b in range(B):
                    dve.wait_ge(*sqo_ready(w, b))
                    dve.tensor_reduce(so[b][:], sqo[b][:].rearrange("p (h d) -> p h d", h=AH), AX.X, ALU.add)\
                        .then_inc(so_ready.sems[b], 1)
                yield
                for b in range(B):
                    dve.wait_ge(*ro_ready(w, b))
                    dve.tensor_tensor(o3[b][:].rearrange("p (h d) -> p h d", h=AH), o2[b][:].rearrange("p (h d) -> p h d", h=AH),
                                      along(ro[b][:], DA), ALU.mult).then_inc(o3_ready.sems[b], 1)
                yield
                for b in range(B):
                    dve.wait_ge(*q1_full(w, b, NLEV + 2))
                    dve.tensor_tensor(xs[b][:], Q1[b][:, 0:D], X[:, bass.ds((b * NW + w) * D, D)], ALU.add).then_inc(xs_ready.sems[b], 1)
                    dve.wait_ge(*xs_ready(w, b))
                    dve.bn_stats(st[b][:], xs[b][:]).then_inc(st_ready.sems[b], 1)
                    dve.wait_ge(*st_ready(w, b))
                    dve.sem_inc(passed_dve, 1)
                    dve.bn_aggr(mv[b][:], st[b][:]).then_inc(mv_ready.sems[b], 1)
                for b in range(B):
                    dve.wait_ge(*rstd_ready(w, b))
                    dve.tensor_scalar(X[:, bass.ds((b * NW + w) * D, D)], xs[b][:], mv[b][:, 0:1], rstd[b][:],
                                      ALU.subtract, ALU.mult).then_inc(x_ready.sems[b], 1)

            pairs(dve, early, late, [6, 7, 8, 9, 12, 13])

        @block.scalar
        def _(act):
            credit(act, [xT_ready, pre_qk, gth_ready, bth_ready, prem_ready, sqa_ready, emat_ready, kbq_turned, k_turned, T_ready,
                         u_ready, sqo_ready, o3T_ready, th_ready, th2_ready, thm_ready, mth_ready])
            act.wait_ge(folded, 3)
            act.wait_ge(zeroed, N_ZEROED)

            def gates(w, b):
                act.wait_ge(*fc_full(w, 2 * b + 1))
                act.wait_ge(*beta_ready(w - 1, b, 1))
                act.activation(bth[b][:], FC[:, 0:AH], ACT.Tanh, scale=0.5).then_inc(bth_ready.sems[b], 1)
                act.activation(prem[:, b, CK - 1:], FC[0:AH, P:2 * P], ACT.Copy).then_inc(prem_ready.sems[b], 1)

            def projected(w, b):
                act.wait_ge(*fb_full(w, b))
                if b == 0:
                    act.wait_ge(*carried(w - 1, 1))
                act.activation(pre[:, 0:4, b, CK - 1:], FB[:].rearrange("p (f k) -> p f k", f=4), ACT.Copy).then_inc(pre_qk.sems[b], 1)
                act.wait_ge(*fc_full(w, 2 * b))
                act.activation(pre[:, 4:6, b, CK - 1:], FC[:, 0:2 * P].rearrange("p (f k) -> p f k", f=2), ACT.Copy)
                if b == 0:
                    act.wait_ge(*inn_ready(w - 1))
                act.activation(gth[:, :, b, :], FC[:, 2 * P:].rearrange("p (f k) -> p f k", f=2), ACT.Tanh, scale=0.5)\
                    .then_inc(gth_ready.sems[b], 1)

            def early(w):
                for b in range(B):
                    act.wait_ge(*fa_full(w, b))
                    act.wait_ge(*fc_full(w - 1, 3))
                    act.activation(xT[:, b].rearrange("p k n -> p (k n)"), FA[:, 0:2 * P], ACT.Copy).then_inc(xT_ready.sems[b], 1)
                yield
                projected(w, 0)
                yield
                gates(w, 0)
                projected(w, 1)
                yield
                gates(w, 1)
                yield
                act.wait_ge(*conv_done(w, NF * CK - 1))
                act.wait_ge(*s2_ready(w - 1))
                act.activation(th[:, 0:4], conv[:, 0:4], ACT.Tanh, scale=0.5).then_inc(th_ready.sem, 1)
                act.wait_ge(*convm_done(w, CK - 1))
                act.activation(thm[:], convm[:], ACT.Tanh, scale=0.5).then_inc(thm_ready.sem, 1)
                act.activation(th[:, 4:6], conv[:, 4:6], ACT.Tanh, scale=0.5).then_inc(th_ready.sem, 1)
                yield
                act.wait_ge(*s1_ready(w, 0))
                act.activation(th[:, 0:4], s1[:, 0:4], ACT.Tanh, scale=0.25).then_inc(th2_ready.sem, 1)
                act.wait_ge(*s1m_ready(w))
                act.wait_ge(*fc_full(w - 1, 5))
                act.activation(mth[:], s1m[:], ACT.Tanh, scale=0.25, bias=mhalf[:]).then_inc(mth_ready.sem, 1)
                yield

            def late(w):
                for b in range(B):
                    act.wait_ge(*fa_full(w, 2 + b))
                    act.activation(sqa[b][:], FA[:], ACT.Square).then_inc(sqa_ready.sems[b], 1)
                    act.wait_ge(*vb_ready(w, b))
                    act.activation(emat[b][:], FB[:, D:2 * D], ACT.Copy, scale=-0.25).then_inc(emat_ready.sems[b], 1)
                for b in range(B):
                    act.wait_ge(*fa_full(w, 4 + b))
                    act.activation(tT[b][:, :, 0:2, :].rearrange("p f a k -> p f (a k)"), FA[:].rearrange("p (f k) -> p f k", f=2),
                                   ACT.Copy).then_inc(kbq_turned.sems[b], 1)
                    act.wait_ge(*fc_full(w, 6 + b))
                    act.activation(tT[b][:, :, 2, :], FC[:, 0:2 * P].rearrange("p (f k) -> p f k", f=2), ACT.Copy)\
                        .then_inc(k_turned.sems[b], 1)
                for i in range(NLEV):
                    for b in range(B):
                        act.wait_ge(*q0_full(w, b, 2 * i))
                        act.activation(T[b][:].rearrange("p h k -> p (h k)"), Q0[b][:], ACT.Copy).then_inc(T_ready.sems[b], 1)
                    yield
                for b in range(B):
                    act.wait_ge(*q0_full(w, b, 2 * NLEV + 1))
                    act.activation(u[b][:].rearrange("p h d -> p (h d)"), Q0[b][:, 0:D], ACT.Copy).then_inc(u_ready.sems[b], 1)
                yield
                for b in range(B):
                    act.wait_ge(*o2_ready(w, b))
                    act.activation(sqo[b][:], o2[b][:], ACT.Square).then_inc(sqo_ready.sems[b], 1)
                yield
                for b in range(B):
                    act.wait_ge(*z_full(w, 2 + b))
                    act.activation(o3T[b][:].rearrange("p f k -> p (f k)"), Z[:, 0:2 * P], ACT.Copy).then_inc(o3T_ready.sems[b], 1)

            pairs(act, early, late, [0, 1, 2, 3, 5, 6])

        @block.gpsimd
        def _(pool):
            credit(pool, [xw_ready, se_ready, rn_ready, kb_ready, em_ready, sv_ready, ro_ready, ve_ready, rstd_ready, carried, est_ready])
            for tile in (pre[:, :, :, 0:CK - 1], prem[:, :, 0:CK - 1], est[:]):
                pool.memset(tile, 0.0).then_inc(zeroed, 1)
            pool.wait_ge(weights, 16 * N_WEIGHTS)

            def early(w):
                for b in range(B):
                    pool.wait_ge(*fa_full(w - 1, b))
                    pool.sem_inc(passed_pool, 1)
                    pool.tensor_copy(xw[b][:], X[:, bass.ds((b * NW + w) * D, D)]).then_inc(xw_ready.sems[b], 1)
                yield
                pool.wait_ge(*conv_done(w, NF * CK - 1))
                pool.sem_inc(passed_pool, 1)
                pool.tensor_copy(pre[:, :, :, 0:CK - 1], pre[:, :, :, P:]).then_inc(carried.sem, 1)
                pool.wait_ge(*convm_done(w, CK - 1))
                pool.sem_inc(passed_pool, 1)
                pool.tensor_copy(prem[:, :, 0:CK - 1], prem[:, :, P:]).then_inc(carried.sem, 1)
                yield
                pool.wait_ge(*ema_ready(w, 2 * B - 1))
                pool.sem_inc(passed_pool, 1)
                pool.tensor_copy(est[:], ema[:, :, :, P - 1]).then_inc(est_ready.sem, 1)
                yield

            def late(w):
                for b in range(B):
                    pool.wait_ge(*ss_ready(w, b))
                    pool.sem_inc(passed_pool, 1)
                    pool.tensor_scalar(se[b][:], ss[b][:], 16e-6, None, ALU.add).then_inc(se_ready.sems[b], 1)
                    pool.wait_ge(*se_ready(w, b))
                    pool.tensor_tensor(rn[b][:], se[b][:], nhalf[:, 0:2 * AH], ALU.pow).then_inc(rn_ready.sems[b], 1)
                for b in range(B):
                    pool.wait_ge(*qk_ready(w, b))
                    pool.wait_ge(*beta_ready(w, b, 1))
                    pool.tensor_tensor(kb[b][:].rearrange("p (h d) -> p h d", h=AH), qk[b][:, D:].rearrange("p (h d) -> p h d", h=AH),
                                       along(beta[b][:, 0, :], DA), ALU.mult).then_inc(kb_ready.sems[b], 1)
                yield
                for b in range(B):
                    pool.wait_ge(*emat_ready(w, b))
                    pool.wait_ge(*mixs_ready(w, b, 1))
                    pool.tensor_tensor(em[b][:].rearrange("p (h d) -> p h d", h=AH), emat[b][:].rearrange("p (h d) -> p h d", h=AH),
                                       along(mixs[b][:, 0, :], DA), ALU.mult).then_inc(em_ready.sems[b], 1)
                yield
                for b in range(B):
                    pool.wait_ge(*so_ready(w, b))
                    pool.sem_inc(passed_pool, 1)
                    pool.tensor_scalar(sv[b][:], so[b][:], 1.0 / DA, RMS_EPS, ALU.mult, ALU.add).then_inc(sv_ready.sems[b], 1)
                    pool.wait_ge(*sv_ready(w, b))
                    pool.tensor_tensor(ro[b][:], sv[b][:], nhalf[:, 0:AH], ALU.pow).then_inc(ro_ready.sems[b], 1)
                for b in range(B):
                    pool.wait_ge(*mv_ready(w, b))
                    pool.sem_inc(passed_pool, 1)
                    pool.tensor_scalar(ve[b][:], mv[b][:, 1:2], LN_EPS, None, ALU.add).then_inc(ve_ready.sems[b], 1)
                    pool.wait_ge(*ve_ready(w, b))
                    pool.tensor_tensor(rstd[b][:], ve[b][:], nhalf[:, 0:1], ALU.pow).then_inc(rstd_ready.sems[b], 1)

            pairs(pool, early, late, [0, 1, 1])

        @block.sync
        def _(sp):
            def rows(t, b):
                return t.rearrange("b (w p) d -> b p w d", p=P)[b]

            def load(out, src):
                sp.dma_start(out, src, allow_slow_non_contiguous=True).then_inc(weights, 16)

            x_sb = X[:].rearrange("p (b w d) -> p b w d", b=B, w=NW)
            for half in range(2):
                for b in range(B):
                    ws = slice(half * NW // 2, (half + 1) * NW // 2)
                    load(x_sb[:, b, ws], rows(a["x"], b)[:, ws])
            for i, name in enumerate(("Wq", "Wk", "Wv")):
                load(wA[:, :, i * D:(i + 1) * D], a[name].rearrange("(k p) n -> p k n", p=P))
            for tile, name in ((wbeta, "Wb"), (wmix, "Wmix"), (wdec, "Wdec"), (woA, "Wo")):
                load(tile[:], a[name].rearrange("(k p) n -> p k n", p=P))
            for e in range(2):
                load(rmsw[DA * e:DA * (e + 1), :], a["rms_w"].rearrange("(p o) -> p o", o=1))
            for i, name in enumerate(("conv_q", "conv_k", "conv_v")):
                load(cw[:, 2 * i:2 * i + 2, :], a[name].rearrange("(f p) c -> p f c", p=P))
            load(cmix[:], a["conv_mix"])
            load(mbias[:], a["mix_bias"].rearrange("(p o) -> p o", o=1))
            load(tables[:], a["tables"].rearrange("p (i k) -> p i k", k=P))

            def store(w, b):
                sp.wait_ge(*x_ready(w, b))
                sp.dma_start(x_norm_dram[b, bass.ds(w * P, P), :], X[:, bass.ds((b * NW + w) * D, D)]).then_inc(stored, 16)

            with sp.Fori(0, NW) as w:
                for b in range(B):
                    store(w, b)
            sp.wait_ge(stored, 16 * UNITS)

    return held


def ffn_layers(nc, ctx, t, x_norm_dram, out_dram):

    def sb(name, shape, dt=F32):
        return ctx.enter_context(nc.sbuf_tensor("f_" + name, shape, dt))

    def pb(name):
        return ctx.enter_context(nc.psum_tensor("f_" + name, [P, 512], F32))

    def signal(name, per=1):
        return Signal(ctx.enter_context(nc.semaphore("f_" + name)), per)

    X, ident, identb = t["X"], t["ident"], t["identb"]
    wqkv, wo, w1, w2 = t["wqkv"], t["wo"], t["w1"], t["w2"]
    bias1, bias2, ones3 = t["bias1"], t["bias2"], t["ones3"]
    rope, scales, mask = t["rope"], t["scales"], t["mask"]

    xw = [sb(f"xw{b}", [P, D]) for b in range(B)]
    xT = [sb(f"xT{b}", [P, 2, W + 1]) for b in range(B)]
    tab = sb("tab", [P, 4, DH])
    sq = sb("sq", [P, 2, INNER])
    ss = sb("ss", [P, 2, FH])
    rn = sb("rn", [P, 2, FH])
    rf = sb("rf", [P, 2, FH])
    rot = sb("rot", [P, 2, INNER])
    rc = sb("rc", [P, 2, INNER])
    rs = sb("rs", [P, 2, INNER])
    qk = sb("qk", [P, 2, INNER])
    qT = sb("qT", [P, 4, W])
    kT = [sb(f"kT{b}", [P, 4, 2, W]) for b in range(B)]
    V = [sb(f"V{b}", [P, 2, INNER]) for b in range(B)]
    nmax = sb("nmax", [P, FH])
    psum_e = sb("psum_e", [P, FH])
    rsum = sb("rsum", [P, FH])
    E = [sb(f"E{i}", [P, 2, 2 * W]) for i in range(2)]
    ET = [sb(f"ET{i}", [P, 2, 2, W]) for i in range(2)]
    o = sb("o", [P, INNER])
    oT = sb("oT", [P, 4, W])
    x1 = sb("x1", [P, D])
    yT = [sb(f"yT{b}", [P, W + 1]) for b in range(B)]
    st = sb("st", [P, 2, 6])
    mv = sb("mv", [P, 2])
    rstd = sb("rstd", [P, 1])
    ve = sb("ve", [P, 1])
    ve2 = sb("ve2", [P, 1])
    z = sb("z", [P, D])
    zT = sb("zT", [P, 2, W])
    gel = sb("gel", [P, 2, HC])
    u = sb("u", [P, 2 * HC])
    uT = sb("uT", [P, NU, W])
    xn = [sb(f"xn{b}", [P, D]) for b in range(B)]
    yres = sb("yres", [P, D])
    ysum = sb("ysum", [P, D])
    st2 = sb("st2", [P, 6])
    mv2 = sb("mv2", [P, 2])
    rstd2 = sb("rstd2", [P, 1])
    y = [sb(f"y{b}", [P, D]) for b in range(B)]
    nhalf = t["nhalf"]

    F0, F1 = pb("F0"), pb("F1")
    S = [pb("S0"), pb("S1")]
    T = [pb("T0"), pb("T1")]
    O, G = pb("O"), pb("G")

    f0_full, f1_full = signal("f0_full", 3), signal("f1_full", 3)
    s_full = [signal("s0_full", 3), signal("s1_full", 3)]
    t_full = [signal("t0_full", 5), signal("t1_full", 4)]
    o_full, g_full = signal("o_full", 3), signal("g_full", 3)
    xw_ready = signal("xw_ready")
    xT_ready = signal("xT_ready")
    xT_carried = signal("xT_carried")
    tab_ready = signal("tab_ready")
    sq_ready = signal("sq_ready", 2)
    ss_ready = signal("ss_ready", 2)
    rn_floor = signal("rn_floor", 2)
    et_used = signal("et_used", 3)
    rn_ready = signal("rn_ready", 2)
    rc_ready = signal("rc_ready", 2)
    rs_ready = signal("rs_ready", 2)
    rot_summed = signal("rot_summed", 2)
    qk_ready = signal("qk_ready", 2)
    v_ready = signal("v_ready")
    v_carried = signal("v_carried")
    k_carried = signal("k_carried")
    qT_ready = signal("qT_ready")
    kT_ready = signal("kT_ready")
    nmax_ready = signal("nmax_ready", 4)
    e_ready = signal("e_ready", 4)
    eT_ready = signal("eT_ready", 4)
    rsum_ready = signal("rsum_ready")
    o_ready = signal("o_ready")
    oT_ready = signal("oT_ready")
    x1_ready = signal("x1_ready")
    yT_ready = signal("yT_ready")
    yT_carried = signal("yT_carried")
    st_ready = signal("st_ready", 2)
    mv_ready = signal("mv_ready")
    var_eps = signal("var_eps")
    rstd_ready = signal("rstd_ready")
    z_ready = signal("z_ready", 2)
    zT_ready = signal("zT_ready")
    gel_ready = signal("gel_ready", 2)
    u_ready = signal("u_ready", 2)
    uTa_ready = signal("uTa_ready")
    uTb_ready = signal("uTb_ready")
    x_ready = signal("x_ready")
    xn_loaded = [ctx.enter_context(nc.semaphore(f"f_xn_loaded{b}")) for b in range(B)]
    ysum_ready = signal("ysum_ready")
    st2_ready = signal("st2_ready")
    mv2_ready = signal("mv2_ready")
    var2_eps = signal("var2_eps")
    rstd2_ready = signal("rstd2_ready")
    y_ready = signal("y_ready")
    y_stored = [ctx.enter_context(nc.semaphore(f"f_y_stored{b}")) for b in range(B)]
    passed_dve = ctx.enter_context(nc.semaphore("f_passed_dve"))
    passed_pool = ctx.enter_context(nc.semaphore("f_passed_pool"))
    carries_zero = ctx.enter_context(nc.semaphore("f_carries_zero"))

    f0_read = [(xT_ready, 0), (rs_ready, 1), (qT_ready, 0)]
    f1_read = [(rs_ready, 0), (v_ready, 0), (kT_ready, 0)]
    s_read = [[(e_ready, 0), (e_ready, 2), (gel_ready, 0)], [(e_ready, 1), (e_ready, 3), (u_ready, 0)]]
    t_read = [[(eT_ready, 0), (eT_ready, 2), (oT_ready, 0), (zT_ready, 0), (uTb_ready, 0)],
              [(eT_ready, 1), (eT_ready, 3), (yT_ready, 0), (uTa_ready, 0)]]
    o_read = [(o_ready, 0), (z_ready, 1), (u_ready, 1)]
    g_read = [(x1_ready, 0), (gel_ready, 1), (x_ready, 0)]

    block = ctx.enter_context(nc.Block())

    def n_of(l, w, b):
        return l * UNITS + B * w + b

    def layers(eng, front, back, open_layer=None):
        for l in range(DEPTH):
            if open_layer:
                open_layer(l)
            front(l, 0, 0)

            def pair(w, last):
                back(l, w, 0, (l, w, 1))
                back(l, w, 1, None if last else (l, w + 1, 0))

            with eng.Fori(0, NW - 1) as w:
                pair(w, False)
            pair(NW - 1, True)

    @block.tensor
    def _(pe):
        credit(pe, [f0_full, f1_full, s_full[0], s_full[1], t_full[0], t_full[1], o_full, g_full, et_used])

        def xT_turn(l, w, b):
            n = n_of(l, w, b)
            pe.wait_ge(*xw_ready(n))
            pe.wait_ge(*before(f0_read, n, 0))
            for j in range(2):
                mm = pe.transpose(F0[:, j * W:(j + 1) * W], xw[b][:, j * P:(j + 1) * P], ident[:])
            mm.then_inc(f0_full.sem, 1)

        def project(l, w, b, part):
            n = n_of(l, w, b)
            bank, full, read, use = [(F1, f1_full, f1_read, 0), (F0, f0_full, f0_read, 1), (F1, f1_full, f1_read, 1)][part]
            if part == 0:
                pe.wait_ge(*xT_ready(n))
            pe.wait_ge(*before(read, n, use))
            pe.matmul(bank[:], xT[b][:, 0, 1:W + 1], wqkv[:, l, 0, part * INNER:(part + 1) * INNER], start=True, stop=False)
            pe.matmul(bank[:], xT[b][:, 1, 0:W], wqkv[:, l, 1, part * INNER:(part + 1) * INNER], start=False, stop=True)\
                .then_inc(full.sem, 1)

        def qk_turn(l, w, b, part):
            n = n_of(l, w, b)
            bank, full, read = [(F0, f0_full, f0_read), (F1, f1_full, f1_read)][part]
            pe.wait_ge(*qk_ready(n, part))
            pe.wait_ge(*before(read, n, 2))
            for c in range(4):
                mm = pe.transpose(bank[:, c * W:(c + 1) * W], qk[:, part, c * P:(c + 1) * P], ident[:])
            mm.then_inc(full.sem, 1)

        def front(l, w, b):
            xT_turn(l, w, b)
            for part in range(3):
                project(l, w, b, part)
            for part in range(2):
                qk_turn(l, w, b, part)

        def scores(l, w, b, g):
            n = n_of(l, w, b)
            bank = S[g % 2]
            if g == 0:
                pe.wait_ge(*qT_ready(n))
                pe.wait_ge(*kT_ready(n))
            pe.wait_ge(*before(s_read[g % 2], n, g // 2))
            for j in range(2):
                pe.matmul(bank[:, j * 256:(j + 1) * 256], identb[:], mask[:, bass.ds(w * 256, 256)], start=(j == 0), stop=False,
                          skip_group_check=True)
            rows = slice(64 * (g % 2), 64 * (g % 2) + 64)
            for j in range(2):
                c = 2 * (g // 2) + j
                mm = pe.matmul(bank[:, j * 256:(j + 1) * 256], qT[rows, c, :], kT[b][rows, c, :, :].rearrange("p a k -> p (a k)"),
                               start=False, stop=(j == 1), skip_group_check=True)
            mm.then_inc(s_full[g % 2].sem, 1)

        def probs_turn(l, w, b, g):
            n = n_of(l, w, b)
            pe.wait_ge(*e_ready(n, g))
            pe.wait_ge(*before(t_read[g % 2], n, g // 2))
            for j in range(2):
                for a in range(2):
                    mm = pe.transpose(T[g % 2][:, (2 * j + a) * W:(2 * j + a + 1) * W], E[g % 2][:, j, a * W:(a + 1) * W], ident[:])
            mm.then_inc(t_full[g % 2].sem, 1)

        def attend(l, w, b, g):
            n = n_of(l, w, b)
            if g == 0:
                pe.wait_ge(*v_ready(n))
                pe.wait_ge(*before(o_read, n, 0))
            pe.wait_ge(*eT_ready(n, g))
            for j in range(2):
                h = head_of(g, j)
                for a in range(2):
                    mm = pe.matmul(O[:, h * DH:(h + 1) * DH], ET[g % 2][:, j, a, :], V[b][:, a, h * DH:(h + 1) * DH],
                                   start=(a == 0), stop=(a == 1))
            if g == 3:
                mm.then_inc(o_full.sem, 1)
            else:
                mm.then_inc(et_used.sem, 1)

        def out_turn(l, w, b):
            n = n_of(l, w, b)
            pe.wait_ge(*o_ready(n))
            pe.wait_ge(*before(t_read[0], n, 2))
            for c in range(4):
                mm = pe.transpose(T[0][:, c * W:(c + 1) * W], o[:, c * P:(c + 1) * P], ident[:])
            mm.then_inc(t_full[0].sem, 1)

        def out_project(l, w, b):
            n = n_of(l, w, b)
            pe.wait_ge(*oT_ready(n))
            pe.wait_ge(*before(g_read, n, 0))
            for c in range(4):
                mm = pe.matmul(G[:, 0:D], oT[:, c, :], wo[:, l, c, :], start=(c == 0), stop=(c == 3))
            mm.then_inc(g_full.sem, 1)

        def shift_down(l, w, b):
            n = n_of(l, w, b)
            pe.wait_ge(*x1_ready(n))
            pe.wait_ge(*before(t_read[1], n, 2))
            pe.transpose(T[1][:, 0:W], x1[:, P:D], ident[:]).then_inc(t_full[1].sem, 1)

        def shift_back(l, w, b):
            n = n_of(l, w, b)
            pe.wait_ge(*yT_ready(n))
            pe.wait_ge(*before(o_read, n, 1))
            pe.transpose(O[:, 0:P], yT[b][:, 0:W], ident[:]).then_inc(o_full.sem, 1)

        def z_turn(l, w, b):
            n = n_of(l, w, b)
            pe.wait_ge(*z_ready(n, 1))
            pe.wait_ge(*before(t_read[0], n, 3))
            for j in range(2):
                mm = pe.transpose(T[0][:, j * W:(j + 1) * W], z[:, j * P:(j + 1) * P], ident[:])
            mm.then_inc(t_full[0].sem, 1)

        def hidden(l, w, b, c):
            n = n_of(l, w, b)
            if c == 0:
                pe.wait_ge(*zT_ready(n))
            gate = [(S[0], s_full[0], s_read[0], 2), (G, g_full, g_read, 1)][c]
            value = [(S[1], s_full[1], s_read[1], 2), (O, o_full, o_read, 2)][c]
            for (bank, full, read, use), first in ((gate, HID), (value, 0)):
                pe.wait_ge(*before(read, n, use))
                cols = slice(first + c * HC, first + (c + 1) * HC)
                pe.matmul(bank[:, 0:HC], ones3[:], bias1[:, l, cols], start=True, stop=False)
                pe.matmul(bank[:, 0:HC], zT[:, 0, :], w1[:, l, 0, cols], start=False, stop=False)
                pe.matmul(bank[:, 0:HC], zT[:, 1, :], w1[:, l, 1, cols], start=False, stop=True).then_inc(full.sem, 1)

        def hidden_turn(l, w, b):
            n = n_of(l, w, b)
            pe.wait_ge(*before(t_read[1], n, 3))
            for c in range(NU):
                if c == 0:
                    pe.wait_ge(*u_ready(n, 0))
                if c == 2:
                    pe.wait_ge(*u_ready(n, 1))
                if c == 4:
                    pe.wait_ge(*before(t_read[0], n, 4))
                k = min(P, HID - c * P)
                mm = pe.transpose(T[1 - c // 4][0:k, (c % 4) * W:(c % 4 + 1) * W], u[:, c * P:c * P + k], ident[:])
                if c in (3, NU - 1):
                    mm.then_inc(t_full[1 - c // 4].sem, 1)

        def down(l, w, b):
            n = n_of(l, w, b)
            pe.wait_ge(*before(g_read, n, 2))
            pe.matmul(G[:, 0:D], ones3[:], bias2[:, l, :], start=True, stop=False)
            for c in range(NU):
                if c == 0:
                    pe.wait_ge(*uTa_ready(n))
                if c == 4:
                    pe.wait_ge(*uTb_ready(n))
                k = min(P, HID - c * P)
                mm = pe.matmul(G[:, 0:D], uT[0:k, c, :], w2[0:k, l, c, :], start=False, stop=(c == NU - 1))
            mm.then_inc(g_full.sem, 1)

        def back(l, w, b, nxt):
            me = (l, w, b)
            scores(*me, 0)
            scores(*me, 1)
            if nxt:
                xT_turn(*nxt)
            probs_turn(*me, 0)
            scores(*me, 2)
            probs_turn(*me, 1)
            scores(*me, 3)
            attend(*me, 0)
            if nxt:
                project(*nxt, 0)
            probs_turn(*me, 2)
            attend(*me, 1)
            probs_turn(*me, 3)
            attend(*me, 2)
            attend(*me, 3)
            if nxt:
                project(*nxt, 1)
            out_turn(*me)
            out_project(*me)
            if nxt:
                project(*nxt, 2)
            shift_down(*me)
            shift_back(*me)
            z_turn(*me)
            hidden(*me, 0)
            hidden(*me, 1)
            if nxt:
                qk_turn(*nxt, 0)
                qk_turn(*nxt, 1)
            hidden_turn(*me)
            down(*me)

        def open_layer(l):
            if l == 0:
                pe.wait_ge(carries_zero, 8)

        layers(pe, front, back, open_layer)

    @block.vector
    def _(dve):
        credit(dve, [ss_ready, rc_ready, rs_ready, nmax_ready, eT_ready, rsum_ready, o_ready, x1_ready, st_ready,
                     mv_ready, z_ready, u_ready, uTa_ready, x_ready, ysum_ready, st2_ready, mv2_ready])

        def norm_sum(l, w, b, part):
            n = n_of(l, w, b)
            dve.wait_ge(*sq_ready(n, part))
            dve.wait_ge(*rn_floor(n - 1, part))
            dve.tensor_reduce(ss[:, part, :], sq[:, part, :].rearrange("p (h d) -> p h d", h=FH), AX.X, ALU.add)\
                .then_inc(ss_ready.sem, 1)

        def rotate(l, w, b, part):
            n = n_of(l, w, b)
            bank = [F1, F0][part]
            xh = bank[:].rearrange("p (h d) -> p h d", h=FH)
            out = rs[:, part, :].rearrange("p (h d) -> p h d", h=FH)
            if part == 0:
                dve.wait_ge(*tab_ready(n))
            dve.wait_ge(*rot_summed(n - 1, part))
            dve.tensor_tensor(rc[:, part, :].rearrange("p (h d) -> p h d", h=FH), xh, over_heads(tab[:, 2 * part, :], FH),
                              ALU.mult).then_inc(rc_ready.sem, 1)
            half = DH // 2
            dve.tensor_tensor(out[:, :, 0:half], xh[:, :, half:DH], over_heads(tab[:, 2 * part + 1, 0:half], FH), ALU.mult)
            dve.tensor_tensor(out[:, :, half:DH], xh[:, :, 0:half], over_heads(tab[:, 2 * part + 1, half:DH], FH), ALU.mult)\
                .then_inc(rs_ready.sem, 1)

        def front_q(l, w, b):
            norm_sum(l, w, b, 0)
            rotate(l, w, b, 0)

        def front_k(l, w, b):
            norm_sum(l, w, b, 1)
            rotate(l, w, b, 1)

        def front(l, w, b):
            front_q(l, w, b)
            front_k(l, w, b)

        def row_max(l, w, b, g):
            n = n_of(l, w, b)
            dve.wait_ge(*s_full[g % 2](n, g // 2))
            if g == 0:
                dve.wait_ge(*e_ready(n - 1, 3))
            dve.tensor_reduce(nmax[:, 2 * g:2 * g + 2], S[g % 2][:].rearrange("p (j k) -> p j k", j=2), AX.X, ALU.max,
                              negate=True).then_inc(nmax_ready.sem, 1)

        def probs_out(l, w, b, g):
            n = n_of(l, w, b)
            dve.wait_ge(*t_full[g % 2](n, g // 2))
            if g < 2:
                dve.wait_ge(*o_full(n - 1, 0))
            else:
                dve.wait_ge(*et_used(n, g - 2))
            dve.tensor_copy(ET[g % 2][:].rearrange("p j a k -> p (j a k)"), T[g % 2][:]).then_inc(eT_ready.sem, 1)

        def normalise(l, w, b):
            n = n_of(l, w, b)
            dve.wait_ge(*e_ready(n, 3))
            dve.reciprocal(rsum[:], psum_e[:]).then_inc(rsum_ready.sem, 1)
            dve.wait_ge(*rsum_ready(n))
            dve.wait_ge(*o_full(n, 0))
            dve.wait_ge(*t_full[0](n - 1, 2))
            dve.tensor_tensor(o[:].rearrange("p (h d) -> p h d", h=FH), O[:].rearrange("p (h d) -> p h d", h=FH),
                              along(rsum[:], DH), ALU.mult).then_inc(o_ready.sem, 1)

        def residual(l, w, b):
            n = n_of(l, w, b)
            dve.wait_ge(*g_full(n, 0))
            dve.wait_ge(*t_full[1](n - 1, 2))
            dve.wait_ge(*x_ready(n - 1))
            dve.tensor_tensor(x1[:], G[:, 0:D], X[:, bass.ds((b * NW + w) * D, D)], ALU.add)\
                .then_inc(x1_ready.sem, 1)

        def stats(l, w, b):
            n = n_of(l, w, b)
            dve.wait_ge(*x1_ready(n))
            dve.wait_ge(*mv_ready(n - 1))
            dve.bn_stats(st[:, 0, :], x1[:, 0:P]).then_inc(st_ready.sem, 1)
            dve.wait_ge(*o_full(n, 1))
            dve.bn_stats(st[:, 1, :], O[:, 0:P]).then_inc(st_ready.sem, 1)
            dve.wait_ge(*st_ready(n, 1))
            dve.wait_ge(*z_ready(n - 1, 1))
            dve.sem_inc(passed_dve, 1)
            dve.bn_aggr(mv[:], st[:].rearrange("p a c -> p (a c)")).then_inc(mv_ready.sem, 1)
            dve.wait_ge(*rstd_ready(n))
            dve.wait_ge(*t_full[0](n - 1, 3))
            dve.wait_ge(*mv_ready(n))
            dve.tensor_scalar(z[:, 0:P], x1[:, 0:P], mv[:, 0:1], rstd[:], ALU.subtract, ALU.mult).then_inc(z_ready.sem, 1)
            dve.tensor_scalar(z[:, P:D], O[:, 0:P], mv[:, 0:1], rstd[:], ALU.subtract, ALU.mult)\
                .then_inc(z_ready.sem, 1)

        def gated(l, w, b, c):
            n = n_of(l, w, b)
            dve.wait_ge(*gel_ready(n, c))
            dve.wait_ge(*(s_full[1] if c == 0 else o_full)(n, 2))
            if c == 0:
                dve.wait_ge(*t_full[0](n - 1, 4))
            bank = [S[1], O][c]
            dve.tensor_tensor(u[:, c * HC:(c + 1) * HC], gel[:, c, :], bank[:, 0:HC], ALU.mult)\
                .then_inc(u_ready.sem, 1)

        def hidden_out(l, w, b):
            n = n_of(l, w, b)
            dve.wait_ge(*t_full[1](n, 3))
            dve.wait_ge(*g_full(n - 1, 2))
            dve.tensor_copy(uT[:, 0:4, :].rearrange("p c k -> p (c k)"), T[1][:])\
                .then_inc(uTa_ready.sem, 1)

        def finish(l, w, b):
            n = n_of(l, w, b)
            dve.wait_ge(*g_full(n, 2))
            dve.wait_ge(*x1_ready(n))
            if l < DEPTH - 1:
                dve.wait_ge(*xw_ready(n))
                dve.tensor_tensor(X[:, bass.ds((b * NW + w) * D, D)], G[:, 0:D], x1[:], ALU.add)\
                    .then_inc(x_ready.sem, 1)
            else:
                m = n - UNITS
                dve.tensor_tensor(yres[:], G[:, 0:D], x1[:], ALU.add)\
                    .then_inc(x_ready.sem, 1)
                dve.wait_ge(*x_ready(n))
                dve.wait_ge(xn_loaded[b], 16 * (w + 1))
                dve.wait_ge(*y_ready(m - 1))
                dve.tensor_tensor(ysum[:], yres[:], xn[b][:], ALU.add).then_inc(ysum_ready.sem, 1)
                dve.wait_ge(*ysum_ready(m))
                dve.bn_stats(st2[:], ysum[:]).then_inc(st2_ready.sem, 1)
                dve.wait_ge(*st2_ready(m))
                dve.sem_inc(passed_dve, 1)
                dve.bn_aggr(mv2[:], st2[:]).then_inc(mv2_ready.sem, 1)

        def back(l, w, b, nxt):
            me = (l, w, b)
            row_max(*me, 0)
            row_max(*me, 1)
            probs_out(*me, 0)
            row_max(*me, 2)
            probs_out(*me, 1)
            row_max(*me, 3)
            if nxt:
                norm_sum(*nxt, 0)
                rotate(*nxt, 0)
            probs_out(*me, 2)
            probs_out(*me, 3)
            normalise(*me)
            if nxt:
                norm_sum(*nxt, 1)
                rotate(*nxt, 1)
            residual(*me)
            stats(*me)
            gated(*me, 0)
            gated(*me, 1)
            hidden_out(*me)
            finish(*me)

        layers(dve, front, back)

    @block.scalar
    def _(act):
        credit(act, [xT_ready, sq_ready, v_ready, qT_ready, kT_ready, e_ready, oT_ready, yT_ready, zT_ready, gel_ready,
                     uTb_ready])

        def xT_out(l, w, b):
            n = n_of(l, w, b)
            act.wait_ge(*f0_full(n, 0))
            act.wait_ge(*xT_carried(n - 2))
            act.activation(xT[b][:, :, 1:W + 1], F0[:, 0:2 * W].rearrange("p (j k) -> p j k", j=2), ACT.Copy)\
                .then_inc(xT_ready.sem, 1)

        def squares(l, w, b, part):
            n = n_of(l, w, b)
            bank, full = [(F1, f1_full), (F0, f0_full)][part]
            act.wait_ge(*full(n, part))
            act.wait_ge(*ss_ready(n - 1, part))
            act.activation(sq[:, part, :], bank[:], ACT.Square).then_inc(sq_ready.sem, 1)

        def v_out(l, w, b):
            n = n_of(l, w, b)
            act.wait_ge(*f1_full(n, 1))
            act.wait_ge(*v_carried(n - 2))
            act.activation(V[b][:, 1, :], F1[:], ACT.Copy).then_inc(v_ready.sem, 1)

        def qT_out(l, w, b):
            n = n_of(l, w, b)
            act.wait_ge(*f0_full(n, 2))
            act.wait_ge(*s_full[1](n - 1, 1))
            act.activation(qT[:].rearrange("p c k -> p (c k)"), F0[:], ACT.Copy)\
                .then_inc(qT_ready.sem, 1)

        def kT_out(l, w, b):
            n = n_of(l, w, b)
            act.wait_ge(*f1_full(n, 2))
            act.wait_ge(*k_carried(n - 2))
            act.activation(kT[b][:, :, 1, :], F1[:].rearrange("p (c k) -> p c k", c=4), ACT.Copy)\
                .then_inc(kT_ready.sem, 1)

        def front(l, w, b):
            xT_out(l, w, b)
            squares(l, w, b, 0)
            squares(l, w, b, 1)
            v_out(l, w, b)
            qT_out(l, w, b)
            kT_out(l, w, b)

        def exponents(l, w, b, g):
            n = n_of(l, w, b)
            act.wait_ge(*nmax_ready(n, g))
            if g == 0:
                act.wait_ge(*rsum_ready(n - 1))
            act.wait_ge(*(t_full[g % 2](n - 1, 1) if g < 2 else t_full[g % 2](n, 0)))
            for j in range(2):
                h = 2 * g + j
                e = act.activation(E[g % 2][:, j, :], S[g % 2][:, j * 256:(j + 1) * 256], ACT.Exp, bias=nmax[:, h:h + 1],
                                   accum_out=psum_e[:, head_of(g, j):head_of(g, j) + 1])
            e.then_inc(e_ready.sem, 1)

        def oT_out(l, w, b):
            n = n_of(l, w, b)
            act.wait_ge(*t_full[0](n, 2))
            act.wait_ge(*g_full(n - 1, 0))
            act.activation(oT[:].rearrange("p c k -> p (c k)"), T[0][:], ACT.Copy)\
                .then_inc(oT_ready.sem, 1)

        def yT_out(l, w, b):
            n = n_of(l, w, b)
            act.wait_ge(*t_full[1](n, 2))
            act.wait_ge(*yT_carried(n - 2))
            act.activation(yT[b][:, 1:W + 1], T[1][:, 0:W], ACT.Copy).then_inc(yT_ready.sem, 1)

        def zT_out(l, w, b):
            n = n_of(l, w, b)
            act.wait_ge(*t_full[0](n, 3))
            act.wait_ge(*o_full(n - 1, 2))
            act.activation(zT[:].rearrange("p c k -> p (c k)"), T[0][:, 0:2 * W], ACT.Copy)\
                .then_inc(zT_ready.sem, 1)

        def gelu(l, w, b, c):
            n = n_of(l, w, b)
            bank, full, use = [(S[0], s_full[0], 2), (G, g_full, 1)][c]
            act.wait_ge(*full(n, use))
            act.wait_ge(*u_ready(n - 1, c))
            act.activation(gel[:, c, :], bank[:, 0:HC], ACT.Gelu).then_inc(gel_ready.sem, 1)

        def uT_out(l, w, b):
            n = n_of(l, w, b)
            act.wait_ge(*t_full[0](n, 4))
            act.wait_ge(*g_full(n - 1, 2))
            act.activation(uT[:, 4, :], T[0][:, 0:W], ACT.Copy)
            k = HID - (NU - 1) * P
            act.activation(uT[0:k, NU - 1, :], T[0][0:k, W:2 * W], ACT.Copy)\
                .then_inc(uTb_ready.sem, 1)

        def back(l, w, b, nxt):
            me = (l, w, b)
            exponents(*me, 0)
            exponents(*me, 1)
            if nxt:
                xT_out(*nxt)
            exponents(*me, 2)
            exponents(*me, 3)
            if nxt:
                squares(*nxt, 0)
                squares(*nxt, 1)
            oT_out(*me)
            if nxt:
                v_out(*nxt)
            yT_out(*me)
            zT_out(*me)
            gelu(*me, 0)
            gelu(*me, 1)
            if nxt:
                qT_out(*nxt)
                kT_out(*nxt)
            uT_out(*me)

        def open_layer(l):
            act.wait_ge(carries_zero, 8 + 4 * l)

        layers(act, front, back, open_layer)

    @block.gpsimd
    def _(pool):
        credit(pool, [xw_ready, xT_carried, tab_ready, rn_floor, rn_ready, rot_summed, qk_ready, v_carried, k_carried,
                      yT_carried, var_eps, rstd_ready, var2_eps, rstd2_ready, y_ready])

        def rows_in(l, w, b):
            n = n_of(l, w, b)
            pool.wait_ge(*f0_full(n - 2, 0))
            pool.sem_inc(passed_pool, 1)
            pool.tensor_copy(xw[b][:], X[:, bass.ds((b * NW + w) * D, D)]).then_inc(xw_ready.sem, 1)
            pool.wait_ge(*rs_ready(n - 1, 1))
            pool.tensor_tensor(tab[:].rearrange("p a d -> p (a d)"), rope[:, bass.ds(w * 4 * DH, 4 * DH)],
                               scales[:, l, :], ALU.mult).then_inc(tab_ready.sem, 1)

        def norm(l, w, b, part):
            n = n_of(l, w, b)
            pool.wait_ge(*ss_ready(n, part))
            pool.sem_inc(passed_pool, 1)
            pool.tensor_scalar(rf[:, part, :], ss[:, part, :], 1e-24, None, ALU.max).then_inc(rn_floor.sem, 1)
            pool.wait_ge(*rn_floor(n, part))
            pool.tensor_tensor(rn[:, part, :], rf[:, part, :], nhalf[:, 0:FH], ALU.pow).then_inc(rn_ready.sem, 1)
            pool.wait_ge(*rs_ready(n, part))
            pool.wait_ge(*rc_ready(n, part))
            pool.tensor_tensor(rot[:, part, :], rc[:, part, :], rs[:, part, :], ALU.add).then_inc(rot_summed.sem, 1)
            pool.wait_ge(*rot_summed(n, part))
            pool.wait_ge(*rn_ready(n, part))
            pool.wait_ge(*[f0_full, f1_full][part](n - 1, 2))
            pool.tensor_tensor(qk[:, part, :].rearrange("p (h d) -> p h d", h=FH),
                               rot[:, part, :].rearrange("p (h d) -> p h d", h=FH), along(rn[:, part, :], DH), ALU.mult)\
                .then_inc(qk_ready.sem, 1)

        def carry_x(l, w, b):
            n = n_of(l, w, b)
            pool.wait_ge(*f1_full(n, 1))
            pool.sem_inc(passed_pool, 1)
            pool.tensor_copy(xT[b][:, 1, 0:1], xT[b][:, 1, W:W + 1]).then_inc(xT_carried.sem, 1)

        def front(l, w, b):
            rows_in(l, w, b)
            norm(l, w, b, 0)
            norm(l, w, b, 1)
            carry_x(l, w, b)

        def carry_k(l, w, b):
            n = n_of(l, w, b)
            pool.wait_ge(*s_full[1](n, 1))
            pool.wait_ge(*s_full[0](n, 1))
            pool.sem_inc(passed_pool, 1)
            pool.tensor_copy(kT[b][:, :, 0, :], kT[b][:, :, 1, :]).then_inc(k_carried.sem, 1)

        def carry_v(l, w, b):
            n = n_of(l, w, b)
            pool.wait_ge(*o_full(n, 0))
            pool.sem_inc(passed_pool, 1)
            pool.tensor_copy(V[b][:, 0, :], V[b][:, 1, :]).then_inc(v_carried.sem, 1)

        def rstd_of(l, w, b):
            n = n_of(l, w, b)
            pool.wait_ge(*mv_ready(n))
            pool.sem_inc(passed_pool, 1)
            pool.tensor_scalar(ve[:], mv[:, 1:2], LN_EPS, None, ALU.add).then_inc(var_eps.sem, 1)
            pool.wait_ge(*var_eps(n))
            pool.wait_ge(*z_ready(n - 1, 1))
            pool.tensor_tensor(rstd[:], ve[:], nhalf[:, 0:1], ALU.pow).then_inc(rstd_ready.sem, 1)

        def carry_y(l, w, b):
            n = n_of(l, w, b)
            pool.wait_ge(*o_full(n, 1))
            pool.sem_inc(passed_pool, 1)
            pool.tensor_copy(yT[b][:, 0:1], yT[b][:, W:W + 1]).then_inc(yT_carried.sem, 1)

        def last_norm(l, w, b):
            m = n_of(l, w, b) - UNITS
            pool.wait_ge(*mv2_ready(m))
            pool.sem_inc(passed_pool, 1)
            pool.tensor_scalar(ve2[:], mv2[:, 1:2], LN_EPS, None, ALU.add).then_inc(var2_eps.sem, 1)
            pool.wait_ge(*var2_eps(m))
            pool.tensor_tensor(rstd2[:], ve2[:], nhalf[:, 0:1], ALU.pow).then_inc(rstd2_ready.sem, 1)
            pool.wait_ge(*rstd2_ready(m))
            pool.wait_ge(y_stored[b], 16 * (w + 1))
            pool.sem_inc(passed_pool, 1)
            pool.tensor_scalar(y[b][:], ysum[:], mv2[:, 0:1], rstd2[:], ALU.subtract, ALU.mult).then_inc(y_ready.sem, 1)

        def back(l, w, b, nxt):
            me = (l, w, b)
            if nxt:
                rows_in(*nxt)
                norm(*nxt, 0)
            carry_k(*me)
            if nxt:
                norm(*nxt, 1)
                carry_x(*nxt)
            carry_v(*me)
            rstd_of(*me)
            carry_y(*me)
            if l == DEPTH - 1:
                last_norm(*me)

        def open_layer(l):
            if l:
                pool.wait_ge(*x_ready(l * UNITS - 1))
                pool.wait_ge(*yT_carried(l * UNITS - 1))
                pool.wait_ge(*xT_carried(l * UNITS - 1))
            for b in range(B):
                pool.memset(xT[b][:, 1, 0:1], 0.0).then_inc(carries_zero, 1)
                pool.memset(yT[b][:, 0:1], 0.0).then_inc(carries_zero, 1)
                if l == 0:
                    pool.memset(V[b][:, 0, :], 0.0).then_inc(carries_zero, 1)
                    pool.memset(kT[b][:, :, 0, :], 0.0).then_inc(carries_zero, 1)

        layers(pool, front, back, open_layer)

    @block.sync
    def _(sp):
        for b in range(B):
            sp.sem_inc(y_stored[b], 16)

        def rows(w, b):
            m = B * w + b
            sp.wait_ge(*ysum_ready(m - 2))
            sp.dma_start(xn[b][:], x_norm_dram[b, bass.ds(w * W, W), :]).then_inc(xn_loaded[b], 16)

        def store(w, b):
            m = B * w + b
            sp.wait_ge(*y_ready(m))
            sp.dma_start(out_dram[b, bass.ds(w * W, W), :], y[b][:]).then_inc(y_stored[b], 16)

        rows(0, 0)
        rows(0, 1)
        with sp.Fori(0, NW - 1) as w:
            for b in range(B):
                store(w, b)
                rows(w + 1, b)
        for b in range(B):
            store(NW - 1, b)
        for b in range(B):
            sp.wait_ge(y_stored[b], 16 * (NW + 1))
def rope_tables(np):
    f = np.float32
    half = np.arange(0, DH, 2, dtype=f)
    freqs = np.arange(L, dtype=f)[:, None] * (f(1.0) / f(10000.0) ** (half / f(DH)))[None, :]
    base = (half + f(0.4 * DH)) / f(1.4 * DH)
    power = (np.arange(L, dtype=f) - f(L // 2)) / f(W // 2)
    scale = base[None, :] ** power[:, None]
    cos, sin, scale = np.cos(freqs), np.sin(freqs), np.concatenate([scale, scale], axis=1)
    cos = np.concatenate([cos, cos], axis=1)
    sin = np.concatenate([-sin, sin], axis=1)
    factor = f(8.0)
    return np.concatenate([cos * scale * factor, sin * scale * factor, cos / scale, sin / scale], axis=1).astype(f)


def resident(nc, ctx):
    def sb(name, shape):
        return ctx.enter_context(nc.sbuf_tensor("r_" + name, shape, F32))

    return {"X": sb("X", [P, B * NW * D]), "ident": sb("ident", [P, P]), "nhalf": sb("nhalf", [P, 8])}


def ffn_resident(nc, ctx):
    def sb(name, shape, dt=F32):
        return ctx.enter_context(nc.sbuf_tensor("r_" + name, shape, dt))

    return {
        "wqkv": sb("wqkv", [P, DEPTH, 2, 3 * INNER]), "wo": sb("wo", [P, DEPTH, INNER // P, D]),
        "w1": sb("w1", [P, DEPTH, 2, 2 * HID]), "w2": sb("w2", [P, DEPTH, NU, D]),
        "bias1": sb("bias1", [P, DEPTH, 2 * HID], BF16), "bias2": sb("bias2", [P, DEPTH, D], BF16),
        "ones3": sb("ones3", [P, P], BF16), "identb": sb("identb", [P, P], BF16),
        "rope": sb("rope", [P, NW * 4 * DH]), "scales": sb("scales", [P, DEPTH, 4 * DH]),
        "mask": sb("mask", [P, NW * 2 * W], BF16),
    }


def delta_tables(np):
    i, j = np.arange(P)[:, None], np.arange(P)[None, :]
    joins = [(i // (2 * s) == j // (2 * s)) & (i % (2 * s) >= s) & (j % (2 * s) < s) for s in (2 ** n for n in range(NLEV + 1))]
    return np.concatenate(joins[1:] + [joins[0].T, i < j, i <= j], axis=1).astype(np.float32)


def program(nc, a, out):
    x_norm_dram = nc.dram_tensor("x_norm", (B, L, D), F32, kind="Internal").ap()
    with ExitStack() as ctx:
        t = resident(nc, ctx)
        steps = ctx.enter_context(nc.semaphore("ident_steps"))
        with nc.Block() as block:
            @block.gpsimd
            def _(pool):
                pool.memset(t["ident"][:], 0.0).then_inc(steps, 1)
                pool.memset(t["nhalf"][:], -0.5).then_inc(steps, 1)
                pool.wait_ge(steps, 2)
                pool.affine_select(out=t["ident"][:], in_=t["ident"][:], compare_op=ALU.not_equal, fill=1.0, base=0,
                                   pattern=[[-1, P]], channel_multiplier=1).then_inc(steps, 1)
                pool.wait_ge(steps, 3)

        with ExitStack() as delta:
            held = delta_layer(nc, delta, t, a, x_norm_dram)
            with nc.Block() as block:
                @block.gpsimd
                def _(pool):
                    for sem in held:
                        pool.sem_clear(sem)
        with ExitStack() as ffn:
            t.update(ffn_resident(nc, ffn))
            setup(nc, ctx, a, t)
            ffn_layers(nc, ffn, t, x_norm_dram, out)


_INS = {"hidden_states": "x", "Wq": "Wq", "Wk": "Wk", "Wv": "Wv", "conv_q": "conv_q", "conv_k": "conv_k", "conv_v": "conv_v",
        "Wb": "Wb", "Wdec": "Wdec", "Wmix": "Wmix", "conv_mix": "conv_mix", "mix_bias": "mix_bias", "rms_w": "rms_w", "Wo": "Wo"}
_FFN_INS = ["wqkv", "q_scale", "k_scale", "wo", "ln_g", "ln_b", "w1", "b1", "w2", "b2"]


def kernel(**inputs):
    import numpy as np
    import concourse.bacc as bacc
    from concourse.bass_utils import run_bass_kernel_spmd

    nc = bacc.Bacc("TRN2", target_bir_lowering=False, num_devices=1)
    arrays, a = {}, {}

    def put(key, array):
        name = f"in_{key}_dram"
        arrays[name] = np.ascontiguousarray(array)
        a[key] = nc.dram_tensor(name, array.shape, mybir.dt.from_np(arrays[name].dtype), kind="ExternalInput").ap()

    for name, key in _INS.items():
        put(key, inputs["L0_attn_" + name])
    for name in _FFN_INS:
        put(name, inputs["L0_ffn_" + name])
    put("rope", rope_tables(np))
    put("tables", delta_tables(np))
    out = nc.dram_tensor("out_0_dram", (B, L, D), F32, kind="ExternalOutput").ap()
    program(nc, a, out)
    r = run_bass_kernel_spmd(nc, [arrays], core_ids=[0])
    return r.results[0]["out_0_dram"]
```

```python
from contextlib import ExitStack

import concourse.bass as bass
from concourse import mybir

F32 = mybir.dt.float32
BF16 = mybir.dt.bfloat16
ALU = mybir.AluOpType
ACT = mybir.ActivationFunctionType
AX = mybir.AxisListType

P = 128
B, L, D = 2, 2048, 256
W = 128
NW = L // W
UNITS = B * NW
DEPTH = 2
FH, DH = 8, 64
INNER = FH * DH
HID = int(D * 4 * 2 / 3)
HC = HID // 2
NU = -(-HID // P)
AH, DA = 4, 64
CK = 4
NF = 3 * D // P
NLEV = 6
LN_EPS = 1e-5
RMS_EPS = 1e-5
MASKED = -1e30
AHEAD = 2


class Signal:

    def __init__(self, sem, per=1):
        self.sem, self.sems, self.per = sem, [sem], per

    def __call__(self, n, k=0):
        return self.sem, (n + AHEAD) * self.per + k + 1


class EachSignal:

    def __init__(self, sems, per=1):
        self.sems, self.per = sems, per

    def __call__(self, n, b, k=0):
        return self.sems[b], (n + AHEAD) * self.per + k + 1


def credit(eng, signals):
    for s in signals:
        for sem in s.sems:
            eng.sem_inc(sem, AHEAD * s.per)


def before(reads, n, use):
    signal, k = reads[use - 1]
    return signal(n if use else n - 1, k)


def head_of(g, j):
    return 4 * (g // 2) + 2 * j + g % 2


def over_heads(ap, heads):
    return ap.unsqueeze(1).broadcast_to([ap.shape[0], heads, ap.shape[1]])


def along(ap, n):
    return ap.unsqueeze(2).broadcast_to([ap.shape[0], ap.shape[1], n])


def setup(nc, sems, a, t):
    with ExitStack() as ctx:
        def sb(name, shape, dt=F32):
            return ctx.enter_context(nc.sbuf_tensor("s_" + name, shape, dt))

        def sem(name):
            return sems.enter_context(nc.semaphore("s_" + name))

        lg = sb("lg", [P, DEPTH, 2])
        lb = sb("lb", [P, DEPTH, 2])
        row = sb("row", [1, DEPTH, 2 * HID + D])
        rest = sb("rest", [1, DEPTH, 2 * HID + D])
        rest2 = sb("rest2", [1, DEPTH, 2 * HID + D])
        parts = sb("parts", [1, 3, DEPTH, 2 * HID + D], BF16)
        shift_ps = [ctx.enter_context(nc.psum_tensor(f"s_shift{i}", [P, 512], F32)) for i in range(8)]
        loaded, w1_loaded, zeroed, tables = sem("loaded"), sem("w1_loaded"), sem("zeroed"), sem("tables")
        shifted, added, split, spread, folded = sem("shifted"), sem("added"), sem("split"), sem("spread"), sem("folded")
        block = ctx.enter_context(nc.Block())

        @block.sync
        def _(sp):
            sp.dma_start(t["w1"][:], a["w1"].rearrange("l (k p) n -> p l k n", p=P)).then_inc(w1_loaded, 16)
            sp.dma_start(lg[:], a["ln_g"].rearrange("l (k p) -> p l k", p=P), allow_slow_non_contiguous=True).then_inc(w1_loaded, 16)
            sp.dma_start(lb[:], a["ln_b"].rearrange("l (k p) -> p l k", p=P), allow_slow_non_contiguous=True).then_inc(w1_loaded, 16)
            sp.dma_start(row[:, :, 0:2 * HID], a["b1"].rearrange("(o l) n -> o l n", o=1)).then_inc(w1_loaded, 16)
            sp.dma_start(row[:, :, 2 * HID:], a["b2"].rearrange("(o l) n -> o l n", o=1)).then_inc(w1_loaded, 16)
            sp.dma_start(t["wqkv"][:], a["wqkv"].rearrange("l (k p) n -> p l k n", p=P)).then_inc(loaded, 16)
            sp.dma_start(t["wo"][:], a["wo"].rearrange("l (k p) n -> p l k n", p=P)).then_inc(loaded, 16)
            full = (NU - 1) * P
            for l in range(DEPTH):
                sp.dma_start(t["w2"][:, l, 0:NU - 1, :], a["w2"][l, 0:full, :].rearrange("(k p) n -> p k n", p=P))\
                    .then_inc(loaded, 16)
            sp.dma_start(t["w2"][0:HID - full, :, NU - 1, :], a["w2"][:, full:HID, :].rearrange("l p n -> p l n"))\
                .then_inc(loaded, 16)
            sp.dma_start(t["rope"][:].rearrange("p (w c) -> p w c", w=NW), a["rope"].rearrange("(w p) c -> p w c", p=P))\
                .then_inc(loaded, 16)
            sp.wait_ge(split, 5)
            for i in range(3):
                sp.dma_start(t["bias1"][i:i + 1, :, :], parts[:, i, :, 0:2 * HID]).then_inc(spread, 16)
                sp.dma_start(t["bias2"][i:i + 1, :, :], parts[:, i, :, 2 * HID:]).then_inc(spread, 16)
            sp.wait_ge(spread, 16 * 6)
            sp.wait_ge(loaded, 16 * (4 + DEPTH))

        @block.scalar
        def _(act):
            n = 0
            for l in range(DEPTH):
                for i, name in enumerate(("q_scale", "k_scale")):
                    src = a[name][l:l + 1, :]
                    first = 2 * i * DH
                    for to, frm, size in ((0, 0, DH), (DH, DH // 2, DH // 2), (DH + DH // 2, 0, DH // 2)):
                        act.dma_start(t["scales"][:, l, first + to:first + to + size],
                                      src[:, frm:frm + size].broadcast_to([P, size])).then_inc(tables, 16)
                        n += 1
            act.wait_ge(tables, 16 * n)

        @block.gpsimd
        def _(pool):
            for i, (tile, value) in enumerate(((t["identb"], 0.0), (t["mask"], 0.0), (t["bias1"], 0.0),
                                               (t["bias2"], 0.0), (t["ones3"], 1.0))):
                pool.memset(tile[:], value).then_inc(zeroed, 1)
            pool.wait_ge(zeroed, 5)
            pool.affine_select(out=t["identb"][:], in_=t["identb"][:], compare_op=ALU.not_equal, fill=1.0, base=0,
                               pattern=[[-1, P]], channel_multiplier=1).then_inc(zeroed, 1)
            m = t["mask"][:].rearrange("p (w a k) -> p w a k", w=NW, a=2)
            pool.affine_select(out=m[:, :, 0, :], in_=m[:, :, 0, :], compare_op=ALU.is_ge, fill=MASKED, base=0,
                               pattern=[[0, NW], [1, W]], channel_multiplier=-1).then_inc(zeroed, 1)
            pool.affine_select(out=m[:, :, 1, :], in_=m[:, :, 1, :], compare_op=ALU.is_ge, fill=MASKED, base=0,
                               pattern=[[0, NW], [-1, W]], channel_multiplier=1).then_inc(zeroed, 1)
            pool.wait_ge(zeroed, 8)
            pool.memset(m[:, 0, 0, :], MASKED).then_inc(zeroed, 1)
            pool.wait_ge(shifted, 1)
            for l in range(DEPTH):
                for k in range(2):
                    pool.tensor_scalar(t["w1"][:, l, k, :], t["w1"][:, l, k, :], lg[:, l, k:k + 1], None, ALU.mult)\
                        .then_inc(folded, 1)
            pool.wait_ge(folded, 2 * DEPTH)
            pool.wait_ge(zeroed, 9)

        @block.tensor
        def _(pe):
            pe.wait_ge(w1_loaded, 16 * 5)
            for l in range(DEPTH):
                for c in range(4):
                    for k in range(2):
                        mm = pe.matmul(shift_ps[4 * l + c][0:1, 0:HC], lb[:, l, k:k + 1], t["w1"][:, l, k, c * HC:(c + 1) * HC],
                                       start=(k == 0), stop=(k == 1))
            mm.then_inc(shifted, 1)

        @block.vector
        def _(dve):
            dve.wait_ge(shifted, 1)
            for l in range(DEPTH):
                for c in range(4):
                    cols = slice(c * HC, (c + 1) * HC)
                    dve.tensor_tensor(row[:, l, cols], row[:, l, cols], shift_ps[4 * l + c][0:1, 0:HC], ALU.add).then_inc(added, 1)
            dve.wait_ge(added, 4 * DEPTH)
            dve.wait_ge(zeroed, 5)
            dve.tensor_copy(parts[:, 0], row[:]).then_inc(split, 1)
            dve.wait_ge(split, 1)
            dve.tensor_tensor(rest[:], row[:], parts[:, 0], ALU.subtract).then_inc(split, 1)
            dve.wait_ge(split, 2)
            dve.tensor_copy(parts[:, 1], rest[:]).then_inc(split, 1)
            dve.wait_ge(split, 3)
            dve.tensor_tensor(rest2[:], rest[:], parts[:, 1], ALU.subtract).then_inc(split, 1)
            dve.wait_ge(split, 4)
            dve.tensor_copy(parts[:, 2], rest2[:]).then_inc(split, 1)


def delta_layer(nc, sems, t, a, x_norm_dram):
    with ExitStack() as ctx:
        def sb(name, shape, dt=F32):
            return ctx.enter_context(nc.sbuf_tensor("a_" + name, shape, dt))

        def pb(name):
            return ctx.enter_context(nc.psum_tensor("a_" + name, [P, 512], F32))

        held = []

        def sem(name):
            held.append(sems.enter_context(nc.semaphore("a_" + name)))
            return held[-1]

        def signal(name, per=1):
            return Signal(sem(name), per)

        def signals(name, per=1):
            return EachSignal([sem(f"{name}{b}") for b in range(B)], per)

        def each(name, shape):
            return [sb(f"{name}{b}", shape) for b in range(B)]

        X, ident, nhalf = t["X"], t["ident"], t["nhalf"]

        wA = sb("wA", [P, 2, 3 * D])
        wbeta = sb("wbeta", [P, 2, AH])
        wmix = sb("wmix", [P, 2, AH])
        wdec = sb("wdec", [P, 2, AH])
        wdecw = sb("wdecw", [P, 2, D])
        woA = sb("woA", [P, 2, D])
        rmsw = sb("rmsw", [P, 1])
        cw = sb("cw", [P, NF, CK])
        cmix = sb("cmix", [AH, CK])
        mbias = sb("mbias", [AH, 1])
        mhalf = sb("mhalf", [AH, 1])
        tables = sb("tables", [P, NLEV + 3, P])
        xT = sb("xT", [P, B, 2, P])
        pre = sb("pre", [P, NF, B, CK - 1 + P])
        prem = sb("prem", [AH, B, CK - 1 + P])
        conv = sb("conv", [P, NF, B, P])
        convm = sb("convm", [AH, B, P])
        th = sb("th", [P, NF, B, P])
        thm = sb("thm", [AH, B, P])
        s1 = sb("s1", [P, NF, B, P])
        s1m = sb("s1m", [AH, B, P])
        mth = sb("mth", [AH, B, P])
        s2 = sb("s2", [P, 4, B, P])
        gth = sb("gth", [P, 2, B, P])
        gam = sb("gam", [P, 2, B, P])
        inn = sb("inn", [P, 2, B, P])
        ema = sb("ema", [P, 2, B, P])
        est = sb("est", [P, 2, B])
        xw = each("xw", [P, D])
        bth = each("bth", [P, AH])
        beta = each("beta", [P, 2, AH])
        mixs = each("mixs", [P, 2, AH])
        sqa = each("sqa", [P, 2 * D])
        ss = each("ss", [P, 2 * AH])
        se = each("se", [P, 2 * AH])
        rn = each("rn", [P, 2 * AH])
        qk = each("qk", [P, 2 * D])
        vb = each("vb", [P, D])
        emat = each("emat", [P, D])
        kb = each("kb", [P, D])
        tT = each("tT", [P, 2, 3, P])
        LP = each("LP", [P, AH, 2, P])
        m1 = each("m1", [P, AH, P])
        R = each("R", [P, AH, P])
        T = each("T", [P, AH, P])
        Xs = each("Xs", [P, AH, P])
        St = each("St", [P, 2, DA])
        r = each("r", [P, AH, DA])
        u = each("u", [P, AH, DA])
        om = each("om", [P, D])
        em = each("em", [P, D])
        o2 = each("o2", [P, D])
        sqo = each("sqo", [P, D])
        so = each("so", [P, AH])
        sv = each("sv", [P, AH])
        ro = each("ro", [P, AH])
        o3 = each("o3", [P, D])
        o3T = each("o3T", [P, 2, P])
        xs = each("xs", [P, D])
        st = each("st", [P, 6])
        mv = each("mv", [P, 2])
        ve = each("ve", [P, 1])
        rstd = each("rstd", [P, 1])

        FA, FB, FC, Z = pb("FA"), pb("FB"), pb("FC"), pb("Z")
        Q0 = [pb("Q00"), pb("Q01")]
        Q1 = [pb("Q10"), pb("Q11")]

        xw_ready = signals("xw_ready")
        q0_full, q1_full = signals("q0_full", 2 * NLEV + 3), signals("q1_full", NLEV + 3)
        xT_ready = signals("xT_ready")
        pre_qk, pre_v, gth_ready, bth_ready, prem_ready = (signals(x) for x in ("pre_qk", "pre_v", "gth", "bth", "prem"))
        beta_ready = signals("beta_ready", 2)
        sqa_ready, ss_ready, se_ready, rn_ready, qk_ready = (signals(x) for x in ("sqa", "ss", "se", "rn", "qk"))
        vb_ready, emat_ready, kb_ready = (signals(x) for x in ("vb", "emat", "kb"))
        mixs_ready = signals("mixs", 2)
        kbq_turned, k_turned = signals("kbq_turned"), signals("k_turned")
        lp_ready = signals("lp", 2)
        m1_ready, R_ready, T_ready, Xs_ready = signals("m1"), signals("R", NLEV + 1), signals("T", NLEV), signals("Xs", NLEV)
        r_ready, u_ready, S_ready = signals("r", 2), signals("u"), signals("S")
        om_ready, em_ready, o2_ready = signals("om", 2), signals("em"), signals("o2")
        sqo_ready, so_ready, sv_ready, ro_ready, o3_ready = (signals(x) for x in ("sqo", "so", "sv", "ro", "o3"))
        o3T_ready, xs_ready, st_ready, mv_ready, ve_ready, rstd_ready, x_ready = (
            signals(x) for x in ("o3T", "xs", "st", "mv", "ve", "rstd", "x"))
        fa_full, fb_full, fc_full, z_full = signal("fa_full", 6), signal("fb_full", 6), signal("fc_full", 10), signal("z_full", 4)
        conv_done, convm_done = signal("conv", NF * CK), signal("convm", CK)
        carried = signal("carried", 2)
        th_ready, s1_ready, th2_ready, s2_ready = signal("th", 2), signal("s1", 2), signal("th2"), signal("s2")
        thm_ready, s1m_ready, mth_ready = signal("thm"), signal("s1m"), signal("mth")
        gam_ready, inn_ready, ema_ready, est_ready = signal("gam"), signal("inn"), signal("ema", 2 * B), signal("est")
        weights, folded, zeroed, stored = sem("weights"), sem("folded"), sem("zeroed"), sem("stored")
        passed_pe, passed_dve, passed_pool = sem("passed_pe"), sem("passed_dve"), sem("passed_pool")
        N_WEIGHTS = 19
        N_ZEROED = 3 + B

        fa_read = [(xT_ready, b, 0) for b in range(B)] + [(qk_ready, b, 0) for b in range(B)] + [(kbq_turned, b, 0) for b in range(B)]
        fb_read = [(pre_qk, b, 0) for b in range(B)] + [(emat_ready, b, 0) for b in range(B)] + [(lp_ready, b, 0) for b in range(B)]
        fc_read = [(s, b, 0) for b in range(B) for s in (gth_ready, prem_ready)] + [(mixs_ready, b, 1) for b in range(B)]\
            + [(k_turned, b, 0) for b in range(B)] + [(lp_ready, b, 1) for b in range(B)]
        z_read = [(om_ready, b, 1) for b in range(B)] + [(o3T_ready, b, 0) for b in range(B)]
        q0_read = [x for i in range(NLEV) for x in ((T_ready, i), (Xs_ready, i))] + [(r_ready, 0), (u_ready, 0), (S_ready, 0)]
        q1_read = [(R_ready, i + 1) for i in range(NLEV)] + [(r_ready, 1), (om_ready, 0), (xs_ready, 0)]

        def freed_pair(reads, w, use):
            signal, b, k = reads[use - 1]
            return signal(w if use else w - 1, b, k)

        def freed(reads, w, b, use):
            signal, k = reads[use - 1]
            return signal(w if use else w - 1, b, k)

        block = ctx.enter_context(nc.Block())

        def pairs(eng, early, late, at):
            for step in early(0):
                pass

            def pair(w, ahead):
                steps = early(w + 1) if ahead else iter(())
                for i, _ in enumerate(late(w)):
                    for _ in range(at.count(i)):
                        next(steps, None)
                for _ in steps:
                    pass

            with eng.Fori(0, NW - 1) as w:
                pair(w, True)
            pair(NW - 1, False)

        @block.tensor
        def _(pe):
            credit(pe, [fa_full, fb_full, fc_full, q0_full, q1_full, z_full])
            pe.wait_ge(folded, 3)
            pe.wait_ge(zeroed, N_ZEROED)

            def early(w):
                for b in range(B):
                    pe.wait_ge(*xw_ready(w, b))
                    pe.wait_ge(*freed_pair(fa_read, w, b))
                    for j in range(2):
                        mm = pe.transpose(FA[:, j * P:(j + 1) * P], xw[b][:, j * P:(j + 1) * P], ident[:])
                    mm.then_inc(fa_full.sem, 1)
                yield
                for b in range(B):
                    pe.wait_ge(*xT_ready(w, b))
                    pe.wait_ge(*freed_pair(fb_read, w, b))
                    for f in range(4):
                        for k in range(2):
                            mm = pe.matmul(FB[:, f * P:(f + 1) * P], wA[:, k, f * P:(f + 1) * P], xT[:, b, k, :],
                                           start=(k == 0), stop=(k == 1))
                    mm.then_inc(fb_full.sem, 1)
                    yield
                    pe.wait_ge(*freed_pair(fc_read, w, 2 * b))
                    for f in range(4):
                        for k in range(2):
                            lhsT = wA[:, k, (4 + f) * P:(5 + f) * P] if f < 2 else wdecw[:, k, (f - 2) * P:(f - 1) * P]
                            mm = pe.matmul(FC[:, f * P:(f + 1) * P], lhsT, xT[:, b, k, :], start=(k == 0), stop=(k == 1))
                    mm.then_inc(fc_full.sem, 1)
                    yield
                    pe.wait_ge(*freed_pair(fc_read, w, 2 * b + 1))
                    for k in range(2):
                        pe.matmul(FC[:, 0:AH], xT[:, b, k, :], wbeta[:, k, :], start=(k == 0), stop=(k == 1))
                    for k in range(2):
                        mm = pe.matmul(FC[0:AH, P:2 * P], wmix[:, k, :], xT[:, b, k, :], start=(k == 0), stop=(k == 1))
                    mm.then_inc(fc_full.sem, 1)
                    yield

            def turn(bank, full, w, use, reads, tiles):
                pe.wait_ge(*freed_pair(reads, w, use))
                for i, tile in enumerate(tiles):
                    mm = pe.transpose(bank[:, i * P:(i + 1) * P], tile, ident[:])
                mm.then_inc(full.sem, 1)

            def late(w):
                pe.wait_ge(*mth_ready(w))
                for b in range(B):
                    pe.wait_ge(*freed_pair(fc_read, w, 4 + b))
                    pe.sem_inc(passed_pe, 1)
                    pe.transpose(FC[:, 0:AH], mth[:, b, :], ident[0:AH, 0:AH]).then_inc(fc_full.sem, 1)
                pe.wait_ge(*s2_ready(w))
                pe.wait_ge(*ema_ready(w, 2 * B - 1))
                for b in range(B):
                    turn(FA, fa_full, w, 2 + b, fa_read, [s2[:, f, b, :] for f in range(4)])
                    turn(FB, fb_full, w, 2 + b, fb_read, [s1[:, 4 + f, b, :] for f in range(2)] + [ema[:, f, b, :] for f in range(2)])
                for b in range(B):
                    pe.wait_ge(*kb_ready(w, b))
                    turn(FA, fa_full, w, 4 + b, fa_read,
                         [x for f in range(2) for x in (kb[b][:, f * P:(f + 1) * P], qk[b][:, f * P:(f + 1) * P])])
                    turn(FC, fc_full, w, 6 + b, fc_read, [qk[b][:, (2 + f) * P:(3 + f) * P] for f in range(2)])
                for b in range(B):
                    pe.wait_ge(*kbq_turned(w, b))
                    pe.wait_ge(*k_turned(w, b))
                    for e, (bank, full, use, reads) in enumerate(((FB, fb_full, 4, fb_read), (FC, fc_full, 8, fc_read))):
                        pe.wait_ge(*freed_pair(reads, w, use + b))
                        rows = slice(DA * e, DA * (e + 1))
                        for f in range(2):
                            mm = pe.matmul(bank[:, f * 2 * P:(f + 1) * 2 * P], tT[b][rows, f, 2, :],
                                           tT[b][rows, f, 0:2, :].rearrange("p a k -> p (a k)"), start=True, stop=True)
                        mm.then_inc(full.sem, 1)
                for i in range(NLEV):
                    for b in range(B):
                        pe.wait_ge(*R_ready(w, b, i))
                        pe.wait_ge(*freed(q0_read, w, b, 2 * i))
                        for h in range(AH):
                            mm = pe.transpose(Q0[b][:, h * P:(h + 1) * P], R[b][:, h, :], ident[:])
                        mm.then_inc(q0_full.sems[b], 1)
                    yield
                    for b in range(B):
                        pe.wait_ge(*T_ready(w, b, i))
                        for h in range(AH):
                            mm = pe.matmul(Q0[b][:, h * P:(h + 1) * P], LP[b][:, h, 0, :], T[b][:, h, :], start=True, stop=True)
                        mm.then_inc(q0_full.sems[b], 1)
                    yield
                    for b in range(B):
                        pe.wait_ge(*Xs_ready(w, b, i))
                        pe.wait_ge(*freed(q1_read, w, b, i))
                        for h in range(AH):
                            mm = pe.matmul(Q1[b][:, h * P:(h + 1) * P], Xs[b][:, h, :], R[b][:, h, :], start=True, stop=True)
                        mm.then_inc(q1_full.sems[b], 1)
                    yield
                for b in range(B):
                    pe.wait_ge(*S_ready(w - 1, b))
                    for e, (bank, full, reads, use) in enumerate(((Q0[b], q0_full, q0_read, 2 * NLEV), (Q1[b], q1_full, q1_read, NLEV))):
                        pe.wait_ge(*freed(reads, w, b, use))
                        rows = slice(DA * e, DA * (e + 1))
                        for f in range(2):
                            mm = pe.matmul(bank[:, f * DA:(f + 1) * DA], tT[b][rows, f, 0, :], St[b][rows, f, :], start=True, stop=True)
                        mm.then_inc(full.sems[b], 1)
                for b in range(B):
                    pe.wait_ge(*r_ready(w, b, 1))
                    pe.wait_ge(*R_ready(w, b, NLEV))
                    for h in range(AH):
                        mm = pe.matmul(Q0[b][:, h * DA:(h + 1) * DA], R[b][:, h, :], r[b][:, h, :], start=True, stop=True)
                    mm.then_inc(q0_full.sems[b], 1)
                for b in range(B):
                    pe.wait_ge(*u_ready(w, b))
                    for e in range(2):
                        bank = (Q1[b], Z)[e]
                        pe.wait_ge(*(freed_pair(z_read, w, b) if e else freed(q1_read, w, b, NLEV + 1)))
                        rows = slice(DA * e, DA * (e + 1))
                        for f in range(2):
                            h = 2 * e + f
                            cols = slice(f * DA, (f + 1) * DA)
                            pe.matmul(bank[:, cols], tT[b][rows, f, 1, :], St[b][rows, f, :], start=True, stop=False)
                            mm = pe.matmul(bank[:, cols], LP[b][:, h, 1, :], u[b][:, h, :], start=False, stop=True)
                        mm.then_inc((q1_full.sems[b], z_full.sem)[e], 1)
                for b in range(B):
                    for e in range(2):
                        for f in range(2):
                            mm = pe.matmul(Q0[b][DA * e:DA * (e + 1), f * DA:(f + 1) * DA],
                                           qk[b][:, D + (2 * f + e) * DA:D + (2 * f + e + 1) * DA], u[b][:, 2 * e + f, :],
                                           start=True, stop=True)
                    mm.then_inc(q0_full.sems[b], 1)
                yield
                for b in range(B):
                    pe.wait_ge(*o3_ready(w, b))
                    turn(Z, z_full, w, 2 + b, z_read, [o3[b][:, f * P:(f + 1) * P] for f in range(2)])
                for b in range(B):
                    pe.wait_ge(*o3T_ready(w, b))
                    pe.wait_ge(*freed(q1_read, w, b, NLEV + 2))
                    for k in range(2):
                        mm = pe.matmul(Q1[b][:, 0:D], o3T[b][:, k, :], woA[:, k, :], start=(k == 0), stop=(k == 1))
                    mm.then_inc(q1_full.sems[b], 1)

            pairs(pe, early, late, [1, 2, 3, 4, 5, 6, 7])

        @block.vector
        def _(dve):
            credit(dve, [beta_ready, ss_ready, qk_ready, vb_ready, mixs_ready, lp_ready, m1_ready, R_ready, Xs_ready, r_ready,
                         S_ready, om_ready, o2_ready, so_ready, o3_ready, xs_ready, st_ready, mv_ready, x_ready,
                         conv_done, convm_done, s1_ready, s1m_ready, s2_ready, gam_ready, inn_ready, ema_ready])
            dve.wait_ge(weights, 16 * N_WEIGHTS)
            dve.tensor_copy(wdecw[:].rearrange("p k (h d) -> p k h d", h=AH), wdec[:].unsqueeze(3).broadcast_to([P, 2, AH, DA]))\
                .then_inc(folded, 1)
            dve.tensor_scalar(woA[:].rearrange("p k n -> p (k n)"), woA[:].rearrange("p k n -> p (k n)"), rmsw[:], None, ALU.mult)\
                .then_inc(folded, 1)
            dve.tensor_scalar(mhalf[:], mbias[:], 0.5, None, ALU.mult).then_inc(folded, 1)
            for b in range(B):
                dve.memset(St[b][:], 0.0).then_inc(zeroed, 1)
            dve.wait_ge(zeroed, N_ZEROED)

            def early(w):
                for tap in range(CK):
                    if tap == 0:
                        for b in range(B):
                            dve.wait_ge(*pre_qk(w, b))
                            dve.wait_ge(*gth_ready(w, b))
                            dve.wait_ge(*prem_ready(w, b))
                        dve.wait_ge(*th_ready(w - 1, 1))
                        dve.wait_ge(*thm_ready(w - 1))
                    for f in range(NF + 1):
                        m = f == NF
                        src, acc, c = (prem[:], convm[:], cmix) if m else (pre[:, f], conv[:, f], cw[:, f, :])
                        src = src[:, :, CK - 1 - tap:CK - 1 - tap + P]
                        weight = c[:, CK - 1 - tap:CK - tap]
                        if tap:
                            dve.wait_ge(*(convm_done(w, tap - 1) if m else conv_done(w, NF * (tap - 1) + f)))
                            op = dve.scalar_tensor_tensor(out=acc, in0=src, scalar=weight, in1=acc, op0=ALU.mult, op1=ALU.add)
                        else:
                            op = dve.tensor_scalar(acc, src, weight, None, ALU.mult)
                        op.then_inc((convm_done if m else conv_done).sem, 1)
                    yield
                for b in range(B):
                    dve.wait_ge(*gth_ready(w, b))
                dve.tensor_scalar(gam[:], gth[:], 0.5, 0.5, ALU.mult, ALU.add).then_inc(gam_ready.sem, 1)
                dve.wait_ge(*th_ready(w, 0))
                dve.scalar_tensor_tensor(out=s1[:, 0:4], in0=th[:, 0:4], scalar=1.0, in1=conv[:, 0:4], op0=ALU.add, op1=ALU.mult)\
                    .then_inc(s1_ready.sem, 1)
                dve.wait_ge(*thm_ready(w))
                dve.scalar_tensor_tensor(out=s1m[:], in0=thm[:], scalar=1.0, in1=convm[:], op0=ALU.add, op1=ALU.mult)\
                    .then_inc(s1m_ready.sem, 1)
                dve.wait_ge(*th_ready(w, 1))
                dve.wait_ge(*fb_full(w - 1, 3))
                dve.scalar_tensor_tensor(out=s1[:, 4:6], in0=th[:, 4:6], scalar=1.0, in1=conv[:, 4:6], op0=ALU.add, op1=ALU.mult)\
                    .then_inc(s1_ready.sem, 1)
                dve.wait_ge(*s1_ready(w, 1))
                dve.scalar_tensor_tensor(out=inn[:], in0=gth[:], scalar=1.0, in1=s1[:, 4:6], op0=ALU.subtract, op1=ALU.mult)\
                    .then_inc(inn_ready.sem, 1)
                dve.wait_ge(*inn_ready(w))
                dve.wait_ge(*est_ready(w - 1))
                for f in range(2):
                    for b in range(B):
                        dve.tensor_tensor_scan(ema[:, f, b, :], gam[:, f, b, :], inn[:, f, b, :], est[:, f, b:b + 1],
                                               ALU.mult, ALU.add).then_inc(ema_ready.sem, 1)
                yield
                dve.wait_ge(*th2_ready(w))
                dve.wait_ge(*fa_full(w - 1, 3))
                dve.scalar_tensor_tensor(out=s2[:], in0=th[:, 0:4], scalar=1.0, in1=s1[:, 0:4], op0=ALU.add, op1=ALU.mult)\
                    .then_inc(s2_ready.sem, 1)
                yield

            def late(w):
                for b in range(B):
                    dve.wait_ge(*bth_ready(w, b))
                    dve.tensor_scalar(beta[b][:, 0, :], bth[b][:], 0.5, 0.5, ALU.mult, ALU.add).then_inc(beta_ready.sems[b], 1)
                    dve.tensor_scalar(beta[b][:, 1, :], bth[b][:], 0.25, 0.25, ALU.mult, ALU.add).then_inc(beta_ready.sems[b], 1)
                    dve.wait_ge(*fc_full(w, 4 + b))
                    dve.tensor_scalar(mixs[b][:, 0, :], FC[:, 0:AH], 0.5, 0.5, ALU.mult, ALU.add).then_inc(mixs_ready.sems[b], 1)
                    dve.tensor_scalar(mixs[b][:, 1, :], FC[:, 0:AH], -0.5, 0.5, ALU.mult, ALU.add).then_inc(mixs_ready.sems[b], 1)
                for b in range(B):
                    dve.wait_ge(*sqa_ready(w, b))
                    dve.tensor_reduce(ss[b][:], sqa[b][:].rearrange("p (h d) -> p h d", h=2 * AH), AX.X, ALU.add)\
                        .then_inc(ss_ready.sems[b], 1)
                    dve.wait_ge(*fb_full(w, 2 + b))
                    dve.wait_ge(*beta_ready(w, b, 1))
                    dve.tensor_tensor(vb[b][:].rearrange("p (h d) -> p h d", h=AH), FB[:, 0:D].rearrange("p (h d) -> p h d", h=AH),
                                      along(beta[b][:, 1, :], DA), ALU.mult).then_inc(vb_ready.sems[b], 1)
                    dve.wait_ge(*rn_ready(w, b))
                    dve.tensor_tensor(qk[b][:].rearrange("p (h d) -> p h d", h=2 * AH), FA[:].rearrange("p (h d) -> p h d", h=2 * AH),
                                      along(rn[b][:], DA), ALU.mult).then_inc(qk_ready.sems[b], 1)
                for b in range(B):
                    for e, (bank, full, use) in enumerate(((FB, fb_full, 4), (FC, fc_full, 8))):
                        dve.wait_ge(*full(w, use + b))
                        dve.tensor_tensor(LP[b][:, 2 * e:2 * e + 2].rearrange("p f a k -> p f (a k)"),
                                          bank[:].rearrange("p (f k) -> p f k", f=2),
                                          tables[:, NLEV + 1:NLEV + 3, :].rearrange("p a k -> p (a k)").unsqueeze(1)
                                          .broadcast_to([P, 2, 2 * P]), ALU.mult).then_inc(lp_ready.sems[b], 1)
                    dve.wait_ge(*lp_ready(w, b, 1))
                    dve.tensor_tensor(m1[b][:], LP[b][:, :, 0, :], over_heads(tables[:, NLEV, :], AH), ALU.mult)\
                        .then_inc(m1_ready.sems[b], 1)
                    dve.wait_ge(*m1_ready(w, b))
                    dve.tensor_tensor(R[b][:], over_heads(ident[:], AH), m1[b][:], ALU.subtract).then_inc(R_ready.sems[b], 1)
                for i in range(NLEV):
                    for b in range(B):
                        dve.wait_ge(*q0_full(w, b, 2 * i + 1))
                        dve.tensor_tensor(Xs[b][:], Q0[b][:].rearrange("p (h k) -> p h k", h=AH), over_heads(tables[:, i, :], AH),
                                          ALU.mult).then_inc(Xs_ready.sems[b], 1)
                    yield
                    for b in range(B):
                        dve.wait_ge(*q1_full(w, b, i))
                        dve.tensor_tensor(R[b][:], R[b][:], Q1[b][:].rearrange("p (h k) -> p h k", h=AH), ALU.subtract)\
                            .then_inc(R_ready.sems[b], 1)
                    yield
                for b in range(B):
                    for e in range(2):
                        dve.wait_ge(*(q1_full(w, b, NLEV) if e else q0_full(w, b, 2 * NLEV)))
                        if e == 0:
                            dve.wait_ge(*vb_ready(w, b))
                        dve.tensor_tensor(r[b][:, 2 * e:2 * e + 2, :], vb[b][:].rearrange("p (f e d) -> p e f d", f=2, e=2)[:, e],
                                          (Q0[b], Q1[b])[e][:, 0:2 * DA].rearrange("p (f d) -> p f d", f=2), ALU.subtract)\
                            .then_inc(r_ready.sems[b], 1)
                yield
                for b in range(B):
                    for e in range(2):
                        dve.wait_ge(*(z_full(w, b) if e else q1_full(w, b, NLEV + 1)))
                        dve.tensor_tensor(om[b][:].rearrange("p (f e d) -> p e f d", f=2, e=2)[:, e],
                                          (Q1[b], Z)[e][:, 0:2 * DA].rearrange("p (f d) -> p f d", f=2),
                                          along(mixs[b][:, 1, :].rearrange("p (f e) -> p e f", e=2)[:, e], DA), ALU.mult)\
                            .then_inc(om_ready.sems[b], 1)
                    dve.wait_ge(*om_ready(w, b, 1))
                    dve.wait_ge(*em_ready(w, b))
                    dve.tensor_tensor(o2[b][:], om[b][:], em[b][:], ALU.add).then_inc(o2_ready.sems[b], 1)
                for b in range(B):
                    dve.wait_ge(*q0_full(w, b, 2 * NLEV + 2))
                    dve.tensor_tensor(St[b][:].rearrange("p f d -> p (f d)"), St[b][:].rearrange("p f d -> p (f d)"),
                                      Q0[b][:, 0:2 * DA], ALU.add).then_inc(S_ready.sems[b], 1)
                for b in range(B):
                    dve.wait_ge(*sqo_ready(w, b))
                    dve.tensor_reduce(so[b][:], sqo[b][:].rearrange("p (h d) -> p h d", h=AH), AX.X, ALU.add)\
                        .then_inc(so_ready.sems[b], 1)
                yield
                for b in range(B):
                    dve.wait_ge(*ro_ready(w, b))
                    dve.tensor_tensor(o3[b][:].rearrange("p (h d) -> p h d", h=AH), o2[b][:].rearrange("p (h d) -> p h d", h=AH),
                                      along(ro[b][:], DA), ALU.mult).then_inc(o3_ready.sems[b], 1)
                yield
                for b in range(B):
                    dve.wait_ge(*q1_full(w, b, NLEV + 2))
                    dve.tensor_tensor(xs[b][:], Q1[b][:, 0:D], X[:, bass.ds((b * NW + w) * D, D)], ALU.add).then_inc(xs_ready.sems[b], 1)
                    dve.wait_ge(*xs_ready(w, b))
                    dve.bn_stats(st[b][:], xs[b][:]).then_inc(st_ready.sems[b], 1)
                    dve.wait_ge(*st_ready(w, b))
                    dve.sem_inc(passed_dve, 1)
                    dve.bn_aggr(mv[b][:], st[b][:]).then_inc(mv_ready.sems[b], 1)
                for b in range(B):
                    dve.wait_ge(*rstd_ready(w, b))
                    dve.tensor_scalar(X[:, bass.ds((b * NW + w) * D, D)], xs[b][:], mv[b][:, 0:1], rstd[b][:],
                                      ALU.subtract, ALU.mult).then_inc(x_ready.sems[b], 1)

            pairs(dve, early, late, [6, 7, 8, 9, 12, 13])

        @block.scalar
        def _(act):
            credit(act, [xT_ready, pre_qk, gth_ready, bth_ready, prem_ready, sqa_ready, emat_ready, kbq_turned, k_turned, T_ready,
                         u_ready, sqo_ready, o3T_ready, th_ready, th2_ready, thm_ready, mth_ready])
            act.wait_ge(folded, 3)
            act.wait_ge(zeroed, N_ZEROED)

            def gates(w, b):
                act.wait_ge(*fc_full(w, 2 * b + 1))
                act.wait_ge(*beta_ready(w - 1, b, 1))
                act.activation(bth[b][:], FC[:, 0:AH], ACT.Tanh, scale=0.5).then_inc(bth_ready.sems[b], 1)
                act.activation(prem[:, b, CK - 1:], FC[0:AH, P:2 * P], ACT.Copy).then_inc(prem_ready.sems[b], 1)

            def projected(w, b):
                act.wait_ge(*fb_full(w, b))
                if b == 0:
                    act.wait_ge(*carried(w - 1, 1))
                act.activation(pre[:, 0:4, b, CK - 1:], FB[:].rearrange("p (f k) -> p f k", f=4), ACT.Copy).then_inc(pre_qk.sems[b], 1)
                act.wait_ge(*fc_full(w, 2 * b))
                act.activation(pre[:, 4:6, b, CK - 1:], FC[:, 0:2 * P].rearrange("p (f k) -> p f k", f=2), ACT.Copy)
                if b == 0:
                    act.wait_ge(*inn_ready(w - 1))
                act.activation(gth[:, :, b, :], FC[:, 2 * P:].rearrange("p (f k) -> p f k", f=2), ACT.Tanh, scale=0.5)\
                    .then_inc(gth_ready.sems[b], 1)

            def early(w):
                for b in range(B):
                    act.wait_ge(*fa_full(w, b))
                    act.wait_ge(*fc_full(w - 1, 3))
                    act.activation(xT[:, b].rearrange("p k n -> p (k n)"), FA[:, 0:2 * P], ACT.Copy).then_inc(xT_ready.sems[b], 1)
                yield
                projected(w, 0)
                yield
                gates(w, 0)
                projected(w, 1)
                yield
                gates(w, 1)
                yield
                act.wait_ge(*conv_done(w, NF * CK - 1))
                act.wait_ge(*s2_ready(w - 1))
                act.activation(th[:, 0:4], conv[:, 0:4], ACT.Tanh, scale=0.5).then_inc(th_ready.sem, 1)
                act.wait_ge(*convm_done(w, CK - 1))
                act.activation(thm[:], convm[:], ACT.Tanh, scale=0.5).then_inc(thm_ready.sem, 1)
                act.activation(th[:, 4:6], conv[:, 4:6], ACT.Tanh, scale=0.5).then_inc(th_ready.sem, 1)
                yield
                act.wait_ge(*s1_ready(w, 0))
                act.activation(th[:, 0:4], s1[:, 0:4], ACT.Tanh, scale=0.25).then_inc(th2_ready.sem, 1)
                act.wait_ge(*s1m_ready(w))
                act.wait_ge(*fc_full(w - 1, 5))
                act.activation(mth[:], s1m[:], ACT.Tanh, scale=0.25, bias=mhalf[:]).then_inc(mth_ready.sem, 1)
                yield

            def late(w):
                for b in range(B):
                    act.wait_ge(*fa_full(w, 2 + b))
                    act.activation(sqa[b][:], FA[:], ACT.Square).then_inc(sqa_ready.sems[b], 1)
                    act.wait_ge(*vb_ready(w, b))
                    act.activation(emat[b][:], FB[:, D:2 * D], ACT.Copy, scale=-0.25).then_inc(emat_ready.sems[b], 1)
                for b in range(B):
                    act.wait_ge(*fa_full(w, 4 + b))
                    act.activation(tT[b][:, :, 0:2, :].rearrange("p f a k -> p f (a k)"), FA[:].rearrange("p (f k) -> p f k", f=2),
                                   ACT.Copy).then_inc(kbq_turned.sems[b], 1)
                    act.wait_ge(*fc_full(w, 6 + b))
                    act.activation(tT[b][:, :, 2, :], FC[:, 0:2 * P].rearrange("p (f k) -> p f k", f=2), ACT.Copy)\
                        .then_inc(k_turned.sems[b], 1)
                for i in range(NLEV):
                    for b in range(B):
                        act.wait_ge(*q0_full(w, b, 2 * i))
                        act.activation(T[b][:].rearrange("p h k -> p (h k)"), Q0[b][:], ACT.Copy).then_inc(T_ready.sems[b], 1)
                    yield
                for b in range(B):
                    act.wait_ge(*q0_full(w, b, 2 * NLEV + 1))
                    act.activation(u[b][:].rearrange("p h d -> p (h d)"), Q0[b][:, 0:D], ACT.Copy).then_inc(u_ready.sems[b], 1)
                yield
                for b in range(B):
                    act.wait_ge(*o2_ready(w, b))
                    act.activation(sqo[b][:], o2[b][:], ACT.Square).then_inc(sqo_ready.sems[b], 1)
                yield
                for b in range(B):
                    act.wait_ge(*z_full(w, 2 + b))
                    act.activation(o3T[b][:].rearrange("p f k -> p (f k)"), Z[:, 0:2 * P], ACT.Copy).then_inc(o3T_ready.sems[b], 1)

            pairs(act, early, late, [0, 1, 2, 3, 5, 6])

        @block.gpsimd
        def _(pool):
            credit(pool, [xw_ready, se_ready, rn_ready, kb_ready, em_ready, sv_ready, ro_ready, ve_ready, rstd_ready, carried, est_ready])
            for tile in (pre[:, :, :, 0:CK - 1], prem[:, :, 0:CK - 1], est[:]):
                pool.memset(tile, 0.0).then_inc(zeroed, 1)
            pool.wait_ge(weights, 16 * N_WEIGHTS)

            def early(w):
                for b in range(B):
                    pool.wait_ge(*fa_full(w - 1, b))
                    pool.sem_inc(passed_pool, 1)
                    pool.tensor_copy(xw[b][:], X[:, bass.ds((b * NW + w) * D, D)]).then_inc(xw_ready.sems[b], 1)
                yield
                pool.wait_ge(*conv_done(w, NF * CK - 1))
                pool.sem_inc(passed_pool, 1)
                pool.tensor_copy(pre[:, :, :, 0:CK - 1], pre[:, :, :, P:]).then_inc(carried.sem, 1)
                pool.wait_ge(*convm_done(w, CK - 1))
                pool.sem_inc(passed_pool, 1)
                pool.tensor_copy(prem[:, :, 0:CK - 1], prem[:, :, P:]).then_inc(carried.sem, 1)
                yield
                pool.wait_ge(*ema_ready(w, 2 * B - 1))
                pool.sem_inc(passed_pool, 1)
                pool.tensor_copy(est[:], ema[:, :, :, P - 1]).then_inc(est_ready.sem, 1)
                yield

            def late(w):
                for b in range(B):
                    pool.wait_ge(*ss_ready(w, b))
                    pool.sem_inc(passed_pool, 1)
                    pool.tensor_scalar(se[b][:], ss[b][:], 16e-6, None, ALU.add).then_inc(se_ready.sems[b], 1)
                    pool.wait_ge(*se_ready(w, b))
                    pool.tensor_tensor(rn[b][:], se[b][:], nhalf[:, 0:2 * AH], ALU.pow).then_inc(rn_ready.sems[b], 1)
                for b in range(B):
                    pool.wait_ge(*qk_ready(w, b))
                    pool.wait_ge(*beta_ready(w, b, 1))
                    pool.tensor_tensor(kb[b][:].rearrange("p (h d) -> p h d", h=AH), qk[b][:, D:].rearrange("p (h d) -> p h d", h=AH),
                                       along(beta[b][:, 0, :], DA), ALU.mult).then_inc(kb_ready.sems[b], 1)
                yield
                for b in range(B):
                    pool.wait_ge(*emat_ready(w, b))
                    pool.wait_ge(*mixs_ready(w, b, 1))
                    pool.tensor_tensor(em[b][:].rearrange("p (h d) -> p h d", h=AH), emat[b][:].rearrange("p (h d) -> p h d", h=AH),
                                       along(mixs[b][:, 0, :], DA), ALU.mult).then_inc(em_ready.sems[b], 1)
                yield
                for b in range(B):
                    pool.wait_ge(*so_ready(w, b))
                    pool.sem_inc(passed_pool, 1)
                    pool.tensor_scalar(sv[b][:], so[b][:], 1.0 / DA, RMS_EPS, ALU.mult, ALU.add).then_inc(sv_ready.sems[b], 1)
                    pool.wait_ge(*sv_ready(w, b))
                    pool.tensor_tensor(ro[b][:], sv[b][:], nhalf[:, 0:AH], ALU.pow).then_inc(ro_ready.sems[b], 1)
                for b in range(B):
                    pool.wait_ge(*mv_ready(w, b))
                    pool.sem_inc(passed_pool, 1)
                    pool.tensor_scalar(ve[b][:], mv[b][:, 1:2], LN_EPS, None, ALU.add).then_inc(ve_ready.sems[b], 1)
                    pool.wait_ge(*ve_ready(w, b))
                    pool.tensor_tensor(rstd[b][:], ve[b][:], nhalf[:, 0:1], ALU.pow).then_inc(rstd_ready.sems[b], 1)

            pairs(pool, early, late, [0, 1, 1])

        @block.sync
        def _(sp):
            def rows(t, b):
                return t.rearrange("b (w p) d -> b p w d", p=P)[b]

            def load(out, src):
                sp.dma_start(out, src, allow_slow_non_contiguous=True).then_inc(weights, 16)

            x_sb = X[:].rearrange("p (b w d) -> p b w d", b=B, w=NW)
            for half in range(2):
                for b in range(B):
                    ws = slice(half * NW // 2, (half + 1) * NW // 2)
                    load(x_sb[:, b, ws], rows(a["x"], b)[:, ws])
            for i, name in enumerate(("Wq", "Wk", "Wv")):
                load(wA[:, :, i * D:(i + 1) * D], a[name].rearrange("(k p) n -> p k n", p=P))
            for tile, name in ((wbeta, "Wb"), (wmix, "Wmix"), (wdec, "Wdec"), (woA, "Wo")):
                load(tile[:], a[name].rearrange("(k p) n -> p k n", p=P))
            for e in range(2):
                load(rmsw[DA * e:DA * (e + 1), :], a["rms_w"].rearrange("(p o) -> p o", o=1))
            for i, name in enumerate(("conv_q", "conv_k", "conv_v")):
                load(cw[:, 2 * i:2 * i + 2, :], a[name].rearrange("(f p) c -> p f c", p=P))
            load(cmix[:], a["conv_mix"])
            load(mbias[:], a["mix_bias"].rearrange("(p o) -> p o", o=1))
            load(tables[:], a["tables"].rearrange("p (i k) -> p i k", k=P))

            def store(w, b):
                sp.wait_ge(*x_ready(w, b))
                sp.dma_start(x_norm_dram[b, bass.ds(w * P, P), :], X[:, bass.ds((b * NW + w) * D, D)]).then_inc(stored, 16)

            with sp.Fori(0, NW) as w:
                for b in range(B):
                    store(w, b)
            sp.wait_ge(stored, 16 * UNITS)

    return held


def ffn_layers(nc, ctx, t, x_norm_dram, out_dram):

    def sb(name, shape, dt=F32):
        return ctx.enter_context(nc.sbuf_tensor("f_" + name, shape, dt))

    def pb(name):
        return ctx.enter_context(nc.psum_tensor("f_" + name, [P, 512], F32))

    def signal(name, per=1):
        return Signal(ctx.enter_context(nc.semaphore("f_" + name)), per)

    X, ident, identb = t["X"], t["ident"], t["identb"]
    wqkv, wo, w1, w2 = t["wqkv"], t["wo"], t["w1"], t["w2"]
    bias1, bias2, ones3 = t["bias1"], t["bias2"], t["ones3"]
    rope, scales, mask = t["rope"], t["scales"], t["mask"]

    xw = [sb(f"xw{b}", [P, D]) for b in range(B)]
    xT = [sb(f"xT{b}", [P, 2, W + 1]) for b in range(B)]
    tab = sb("tab", [P, 4, DH])
    sq = sb("sq", [P, 2, INNER])
    ss = sb("ss", [P, 2, FH])
    rn = sb("rn", [P, 2, FH])
    rf = sb("rf", [P, 2, FH])
    rot = sb("rot", [P, 2, INNER])
    rc = sb("rc", [P, 2, INNER])
    rs = sb("rs", [P, 2, INNER])
    qk = sb("qk", [P, 2, INNER])
    qT = sb("qT", [P, 4, W])
    kT = [sb(f"kT{b}", [P, 4, 2, W]) for b in range(B)]
    V = [sb(f"V{b}", [P, 2, INNER]) for b in range(B)]
    nmax = sb("nmax", [P, FH])
    psum_e = sb("psum_e", [P, FH])
    rsum = sb("rsum", [P, FH])
    E = [sb(f"E{i}", [P, 2, 2 * W]) for i in range(2)]
    ET = [sb(f"ET{i}", [P, 2, 2, W]) for i in range(2)]
    o = sb("o", [P, INNER])
    oT = sb("oT", [P, 4, W])
    x1 = sb("x1", [P, D])
    yT = [sb(f"yT{b}", [P, W + 1]) for b in range(B)]
    st = sb("st", [P, 2, 6])
    mv = sb("mv", [P, 2])
    rstd = sb("rstd", [P, 1])
    ve = sb("ve", [P, 1])
    ve2 = sb("ve2", [P, 1])
    z = sb("z", [P, D])
    zT = sb("zT", [P, 2, W])
    gel = sb("gel", [P, 2, HC])
    u = sb("u", [P, 2 * HC])
    uT = sb("uT", [P, NU, W])
    xn = [sb(f"xn{b}", [P, D]) for b in range(B)]
    yres = sb("yres", [P, D])
    ysum = sb("ysum", [P, D])
    st2 = sb("st2", [P, 6])
    mv2 = sb("mv2", [P, 2])
    rstd2 = sb("rstd2", [P, 1])
    y = [sb(f"y{b}", [P, D]) for b in range(B)]
    nhalf = t["nhalf"]

    F0, F1 = pb("F0"), pb("F1")
    S = [pb("S0"), pb("S1")]
    T, O = pb("T"), pb("O")
    H0, H1 = pb("H0"), pb("H1")

    f0_full, f1_full = signal("f0_full", 3), signal("f1_full", 3)
    s_full = [signal("s0_full", 2), signal("s1_full", 2)]
    t_full, o_full = signal("t_full", 5), signal("o_full")
    h0_full, h1_full = signal("h0_full", 6), signal("h1_full", 5)
    xw_ready = signal("xw_ready")
    xT_ready = signal("xT_ready")
    xT_carried = signal("xT_carried")
    tab_ready = signal("tab_ready")
    sq_ready = signal("sq_ready", 2)
    ss_ready = signal("ss_ready", 2)
    rn_floor = signal("rn_floor", 2)
    et_used = signal("et_used", 3)
    rn_ready = signal("rn_ready", 2)
    rc_ready = signal("rc_ready", 2)
    rs_ready = signal("rs_ready", 2)
    rot_summed = signal("rot_summed", 2)
    qk_ready = signal("qk_ready", 2)
    v_ready = signal("v_ready")
    v_carried = signal("v_carried")
    k_carried = signal("k_carried")
    qT_ready = signal("qT_ready")
    kT_ready = signal("kT_ready")
    nmax_ready = signal("nmax_ready", 4)
    e_ready = signal("e_ready", 4)
    eT_ready = signal("eT_ready", 4)
    rsum_ready = signal("rsum_ready")
    o_ready = signal("o_ready")
    oT_ready = signal("oT_ready")
    x1_ready = signal("x1_ready")
    yT_ready = signal("yT_ready")
    yT_carried = signal("yT_carried")
    st_ready = signal("st_ready", 2)
    mv_ready = signal("mv_ready")
    var_eps = signal("var_eps")
    rstd_ready = signal("rstd_ready")
    z_ready = signal("z_ready", 2)
    zT_ready = signal("zT_ready")
    gel_ready = signal("gel_ready", 2)
    u_ready = signal("u_ready", 2)
    uTa_ready = signal("uTa_ready")
    uTb_ready = signal("uTb_ready")
    x_ready = signal("x_ready")
    xn_loaded = [ctx.enter_context(nc.semaphore(f"f_xn_loaded{b}")) for b in range(B)]
    ysum_ready = signal("ysum_ready")
    st2_ready = signal("st2_ready")
    mv2_ready = signal("mv2_ready")
    var2_eps = signal("var2_eps")
    rstd2_ready = signal("rstd2_ready")
    y_ready = signal("y_ready")
    y_stored = [ctx.enter_context(nc.semaphore(f"f_y_stored{b}")) for b in range(B)]
    passed_dve = ctx.enter_context(nc.semaphore("f_passed_dve"))
    passed_pool = ctx.enter_context(nc.semaphore("f_passed_pool"))
    carries_zero = ctx.enter_context(nc.semaphore("f_carries_zero"))

    f0_read = [(xT_ready, 0), (rs_ready, 1), (qT_ready, 0)]
    f1_read = [(rs_ready, 0), (v_ready, 0), (kT_ready, 0)]
    s_read = [[(e_ready, 0), (e_ready, 2)], [(e_ready, 1), (e_ready, 3)]]
    t_read = [(eT_ready, g) for g in range(4)] + [(oT_ready, 0)]
    o_read = [(o_ready, 0)]
    h0_read = [(x1_ready, 0), (z_ready, 1), (gel_ready, 0), (gel_ready, 1), (uTa_ready, 0), (x_ready, 0)]
    h1_read = [(yT_ready, 0), (zT_ready, 0), (u_ready, 0), (u_ready, 1), (uTb_ready, 0)]

    block = ctx.enter_context(nc.Block())

    def n_of(l, w, b):
        return l * UNITS + B * w + b

    def do(unit, piece, *part):
        if unit:
            piece(*unit, *part)

    def layers(eng, step):
        step(None, None, (0, 0, 0))
        step(None, (0, 0, 0), (0, 0, 1))
        for l in range(DEPTH):
            with eng.Fori(0, NW - 1) as w:
                step((l, w, 0), (l, w, 1), (l, w + 1, 0))
                step((l, w, 1), (l, w + 1, 0), (l, w + 1, 1))
            more = l < DEPTH - 1
            step((l, NW - 1, 0), (l, NW - 1, 1), (l + 1, 0, 0) if more else None)
            step((l, NW - 1, 1), (l + 1, 0, 0) if more else None, (l + 1, 0, 1) if more else None)

    @block.tensor
    def _(pe):
        credit(pe, [f0_full, f1_full, s_full[0], s_full[1], t_full, o_full, h0_full, h1_full, et_used])
        pe.wait_ge(carries_zero, 6)

        def xT_turn(l, w, b):
            n = n_of(l, w, b)
            pe.wait_ge(*xw_ready(n))
            pe.wait_ge(*before(f0_read, n, 0))
            for j in range(2):
                mm = pe.transpose(F0[:, j * W:(j + 1) * W], xw[b][:, j * P:(j + 1) * P], ident[:])
            mm.then_inc(f0_full.sem, 1)

        def project(l, w, b, part):
            n = n_of(l, w, b)
            bank, full, read, use = [(F1, f1_full, f1_read, 0), (F0, f0_full, f0_read, 1), (F1, f1_full, f1_read, 1)][part]
            if part == 0:
                pe.wait_ge(*xT_ready(n))
            pe.wait_ge(*before(read, n, use))
            pe.matmul(bank[:], xT[b][:, 0, 1:W + 1], wqkv[:, l, 0, part * INNER:(part + 1) * INNER], start=True, stop=False)
            pe.matmul(bank[:], xT[b][:, 1, 0:W], wqkv[:, l, 1, part * INNER:(part + 1) * INNER], start=False, stop=True)\
                .then_inc(full.sem, 1)

        def qk_turn(l, w, b, part):
            n = n_of(l, w, b)
            bank, full, read = [(F0, f0_full, f0_read), (F1, f1_full, f1_read)][part]
            pe.wait_ge(*qk_ready(n, part))
            pe.wait_ge(*before(read, n, 2))
            for c in range(4):
                mm = pe.transpose(bank[:, c * W:(c + 1) * W], qk[:, part, c * P:(c + 1) * P], ident[:])
            mm.then_inc(full.sem, 1)

        def scores(l, w, b, g):
            n = n_of(l, w, b)
            bank = S[g % 2]
            if g == 0:
                pe.wait_ge(*qT_ready(n))
                pe.wait_ge(*kT_ready(n))
            pe.wait_ge(*before(s_read[g % 2], n, g // 2))
            for j in range(2):
                pe.matmul(bank[:, j * 256:(j + 1) * 256], identb[:], mask[:, bass.ds(w * 256, 256)], start=(j == 0), stop=False,
                          skip_group_check=True)
            rows = slice(64 * (g % 2), 64 * (g % 2) + 64)
            for j in range(2):
                c = 2 * (g // 2) + j
                mm = pe.matmul(bank[:, j * 256:(j + 1) * 256], qT[rows, c, :], kT[b][rows, c, :, :].rearrange("p a k -> p (a k)"),
                               start=False, stop=(j == 1), skip_group_check=True)
            mm.then_inc(s_full[g % 2].sem, 1)

        def probs_turn(l, w, b, g):
            n = n_of(l, w, b)
            pe.wait_ge(*e_ready(n, g))
            pe.wait_ge(*before(t_read, n, g))
            for j in range(2):
                for a in range(2):
                    mm = pe.transpose(T[:, (2 * j + a) * W:(2 * j + a + 1) * W], E[g % 2][:, j, a * W:(a + 1) * W], ident[:])
            mm.then_inc(t_full.sem, 1)

        def attend(l, w, b, g):
            n = n_of(l, w, b)
            if g == 0:
                pe.wait_ge(*v_ready(n))
                pe.wait_ge(*before(o_read, n, 0))
            pe.wait_ge(*eT_ready(n, g))
            for j in range(2):
                h = head_of(g, j)
                for a in range(2):
                    mm = pe.matmul(O[:, h * DH:(h + 1) * DH], ET[g % 2][:, j, a, :], V[b][:, a, h * DH:(h + 1) * DH],
                                   start=(a == 0), stop=(a == 1))
            if g == 3:
                mm.then_inc(o_full.sem, 1)
            else:
                mm.then_inc(et_used.sem, 1)

        def out_turn(l, w, b):
            n = n_of(l, w, b)
            pe.wait_ge(*o_ready(n))
            pe.wait_ge(*before(t_read, n, 4))
            for c in range(4):
                mm = pe.transpose(T[:, c * W:(c + 1) * W], o[:, c * P:(c + 1) * P], ident[:])
            mm.then_inc(t_full.sem, 1)

        def out_project(l, w, b):
            n = n_of(l, w, b)
            pe.wait_ge(*oT_ready(n))
            pe.wait_ge(*before(h0_read, n, 0))
            for c in range(4):
                mm = pe.matmul(H0[:, 0:D], oT[:, c, :], wo[:, l, c, :], start=(c == 0), stop=(c == 3))
            mm.then_inc(h0_full.sem, 1)

        def shift_down(l, w, b):
            n = n_of(l, w, b)
            pe.wait_ge(*x1_ready(n))
            pe.wait_ge(*before(h1_read, n, 0))
            pe.transpose(H1[:, 0:W], x1[:, P:D], ident[:]).then_inc(h1_full.sem, 1)

        def shift_back(l, w, b):
            n = n_of(l, w, b)
            pe.wait_ge(*yT_ready(n))
            pe.wait_ge(*before(h0_read, n, 1))
            pe.transpose(H0[:, 0:P], yT[b][:, 0:W], ident[:]).then_inc(h0_full.sem, 1)

        def z_turn(l, w, b):
            n = n_of(l, w, b)
            pe.wait_ge(*z_ready(n, 1))
            pe.wait_ge(*before(h1_read, n, 1))
            for j in range(2):
                mm = pe.transpose(H1[:, j * W:(j + 1) * W], z[:, j * P:(j + 1) * P], ident[:])
            mm.then_inc(h1_full.sem, 1)

        def hidden(l, w, b, c):
            n = n_of(l, w, b)
            if c == 0:
                pe.wait_ge(*zT_ready(n))
            for bank, full, read, first in ((H0, h0_full, h0_read, HID), (H1, h1_full, h1_read, 0)):
                pe.wait_ge(*before(read, n, 2 + c))
                cols = slice(first + c * HC, first + (c + 1) * HC)
                pe.matmul(bank[:, 0:HC], ones3[:], bias1[:, l, cols], start=True, stop=False)
                pe.matmul(bank[:, 0:HC], zT[:, 0, :], w1[:, l, 0, cols], start=False, stop=False)
                pe.matmul(bank[:, 0:HC], zT[:, 1, :], w1[:, l, 1, cols], start=False, stop=True).then_inc(full.sem, 1)

        def hidden_turn(l, w, b):
            n = n_of(l, w, b)
            pe.wait_ge(*u_ready(n, 1))
            for c in range(NU):
                bank, full, read = [(H0, h0_full, h0_read), (H1, h1_full, h1_read)][c // 4]
                if c % 4 == 0:
                    pe.wait_ge(*before(read, n, 4))
                k = min(P, HID - c * P)
                mm = pe.transpose(bank[0:k, (c % 4) * W:(c % 4 + 1) * W], u[:, c * P:c * P + k], ident[:])
                if c in (3, NU - 1):
                    mm.then_inc(full.sem, 1)

        def down(l, w, b):
            n = n_of(l, w, b)
            pe.wait_ge(*before(h0_read, n, 5))
            pe.matmul(H0[:, 0:D], ones3[:], bias2[:, l, :], start=True, stop=False)
            for c in range(NU):
                if c == 0:
                    pe.wait_ge(*uTa_ready(n))
                if c == 4:
                    pe.wait_ge(*uTb_ready(n))
                k = min(P, HID - c * P)
                mm = pe.matmul(H0[:, 0:D], uT[0:k, c, :], w2[0:k, l, c, :], start=False, stop=(c == NU - 1))
            mm.then_inc(h0_full.sem, 1)

        def step(mlp, att, frt):
            do(att, scores, 0)
            do(att, scores, 1)
            do(mlp, out_project)
            do(frt, xT_turn)
            do(mlp, shift_down)
            do(att, probs_turn, 0)
            do(att, scores, 2)
            do(mlp, shift_back)
            do(frt, project, 0)
            do(att, probs_turn, 1)
            do(att, scores, 3)
            do(att, attend, 0)
            do(mlp, z_turn)
            do(att, probs_turn, 2)
            do(frt, project, 1)
            do(mlp, hidden, 0)
            do(att, attend, 1)
            do(att, probs_turn, 3)
            do(frt, project, 2)
            do(mlp, hidden, 1)
            do(att, attend, 2)
            do(att, attend, 3)
            do(frt, qk_turn, 0)
            do(mlp, hidden_turn)
            do(att, out_turn)
            do(frt, qk_turn, 1)
            do(mlp, down)

        layers(pe, step)

    @block.vector
    def _(dve):
        credit(dve, [ss_ready, rc_ready, rs_ready, nmax_ready, eT_ready, rsum_ready, o_ready, x1_ready, st_ready,
                     mv_ready, z_ready, u_ready, uTa_ready, x_ready, ysum_ready, st2_ready, mv2_ready])

        def norm_sum(l, w, b, part):
            n = n_of(l, w, b)
            dve.wait_ge(*sq_ready(n, part))
            dve.wait_ge(*rn_floor(n - 1, part))
            dve.tensor_reduce(ss[:, part, :], sq[:, part, :].rearrange("p (h d) -> p h d", h=FH), AX.X, ALU.add)\
                .then_inc(ss_ready.sem, 1)

        def rotate(l, w, b, part):
            n = n_of(l, w, b)
            bank = [F1, F0][part]
            xh = bank[:].rearrange("p (h d) -> p h d", h=FH)
            out = rs[:, part, :].rearrange("p (h d) -> p h d", h=FH)
            if part == 0:
                dve.wait_ge(*tab_ready(n))
            dve.wait_ge(*rot_summed(n - 1, part))
            dve.tensor_tensor(rc[:, part, :].rearrange("p (h d) -> p h d", h=FH), xh, over_heads(tab[:, 2 * part, :], FH),
                              ALU.mult).then_inc(rc_ready.sem, 1)
            half = DH // 2
            dve.tensor_tensor(out[:, :, 0:half], xh[:, :, half:DH], over_heads(tab[:, 2 * part + 1, 0:half], FH), ALU.mult)
            dve.tensor_tensor(out[:, :, half:DH], xh[:, :, 0:half], over_heads(tab[:, 2 * part + 1, half:DH], FH), ALU.mult)\
                .then_inc(rs_ready.sem, 1)

        def row_max(l, w, b, g):
            n = n_of(l, w, b)
            dve.wait_ge(*s_full[g % 2](n, g // 2))
            if g == 0:
                dve.wait_ge(*e_ready(n - 1, 3))
            dve.tensor_reduce(nmax[:, 2 * g:2 * g + 2], S[g % 2][:].rearrange("p (j k) -> p j k", j=2), AX.X, ALU.max,
                              negate=True).then_inc(nmax_ready.sem, 1)

        def probs_out(l, w, b, g):
            n = n_of(l, w, b)
            dve.wait_ge(*t_full(n, g))
            if g < 2:
                dve.wait_ge(*o_full(n - 1, 0))
            else:
                dve.wait_ge(*et_used(n, g - 2))
            dve.tensor_copy(ET[g % 2][:].rearrange("p j a k -> p (j a k)"), T[:]).then_inc(eT_ready.sem, 1)

        def normalise(l, w, b):
            n = n_of(l, w, b)
            dve.wait_ge(*e_ready(n, 3))
            dve.reciprocal(rsum[:], psum_e[:]).then_inc(rsum_ready.sem, 1)
            dve.wait_ge(*rsum_ready(n))
            dve.wait_ge(*o_full(n, 0))
            dve.wait_ge(*t_full(n - 1, 4))
            dve.tensor_tensor(o[:].rearrange("p (h d) -> p h d", h=FH), O[:].rearrange("p (h d) -> p h d", h=FH),
                              along(rsum[:], DH), ALU.mult).then_inc(o_ready.sem, 1)

        def residual(l, w, b):
            n = n_of(l, w, b)
            dve.wait_ge(*h0_full(n, 0))
            dve.wait_ge(*h1_full(n - 1, 0))
            dve.wait_ge(*x_ready(n - 1))
            dve.tensor_tensor(x1[:], H0[:, 0:D], X[:, bass.ds((b * NW + w) * D, D)], ALU.add)\
                .then_inc(x1_ready.sem, 1)

        def stats(l, w, b):
            n = n_of(l, w, b)
            dve.wait_ge(*x1_ready(n))
            dve.wait_ge(*mv_ready(n - 1))
            dve.bn_stats(st[:, 0, :], x1[:, 0:P]).then_inc(st_ready.sem, 1)
            dve.wait_ge(*h0_full(n, 1))
            dve.bn_stats(st[:, 1, :], H0[:, 0:P]).then_inc(st_ready.sem, 1)
            dve.wait_ge(*st_ready(n, 1))
            dve.wait_ge(*z_ready(n - 1, 1))
            dve.sem_inc(passed_dve, 1)
            dve.bn_aggr(mv[:], st[:].rearrange("p a c -> p (a c)")).then_inc(mv_ready.sem, 1)

        def normed(l, w, b):
            n = n_of(l, w, b)
            dve.wait_ge(*rstd_ready(n))
            dve.wait_ge(*h1_full(n - 1, 1))
            dve.wait_ge(*mv_ready(n))
            dve.tensor_scalar(z[:, 0:P], x1[:, 0:P], mv[:, 0:1], rstd[:], ALU.subtract, ALU.mult).then_inc(z_ready.sem, 1)
            dve.tensor_scalar(z[:, P:D], H0[:, 0:P], mv[:, 0:1], rstd[:], ALU.subtract, ALU.mult)\
                .then_inc(z_ready.sem, 1)

        def gated(l, w, b, c):
            n = n_of(l, w, b)
            dve.wait_ge(*gel_ready(n, c))
            dve.wait_ge(*h1_full(n, 2 + c))
            dve.tensor_tensor(u[:, c * HC:(c + 1) * HC], gel[:, c, :], H1[:, 0:HC], ALU.mult)\
                .then_inc(u_ready.sem, 1)

        def hidden_out(l, w, b):
            n = n_of(l, w, b)
            dve.wait_ge(*h0_full(n, 4))
            dve.tensor_copy(uT[:, 0:4, :].rearrange("p c k -> p (c k)"), H0[:])\
                .then_inc(uTa_ready.sem, 1)

        def finish(l, w, b):
            n = n_of(l, w, b)
            dve.wait_ge(*h0_full(n, 5))
            dve.wait_ge(*x1_ready(n))
            if l < DEPTH - 1:
                dve.wait_ge(*xw_ready(n))
                dve.tensor_tensor(X[:, bass.ds((b * NW + w) * D, D)], H0[:, 0:D], x1[:], ALU.add)\
                    .then_inc(x_ready.sem, 1)
            else:
                m = n - UNITS
                dve.tensor_tensor(yres[:], H0[:, 0:D], x1[:], ALU.add)\
                    .then_inc(x_ready.sem, 1)
                dve.wait_ge(*x_ready(n))
                dve.wait_ge(xn_loaded[b], 16 * (w + 1))
                dve.wait_ge(*y_ready(m - 1))
                dve.tensor_tensor(ysum[:], yres[:], xn[b][:], ALU.add).then_inc(ysum_ready.sem, 1)
                dve.wait_ge(*ysum_ready(m))
                dve.bn_stats(st2[:], ysum[:]).then_inc(st2_ready.sem, 1)
                dve.wait_ge(*st2_ready(m))
                dve.sem_inc(passed_dve, 1)
                dve.bn_aggr(mv2[:], st2[:]).then_inc(mv2_ready.sem, 1)

        def step(mlp, att, frt):
            do(att, row_max, 0)
            do(att, row_max, 1)
            do(mlp, residual)
            do(att, probs_out, 0)
            do(att, row_max, 2)
            do(mlp, stats)
            do(frt, norm_sum, 0)
            do(frt, rotate, 0)
            do(att, probs_out, 1)
            do(att, row_max, 3)
            do(mlp, normed)
            do(att, probs_out, 2)
            do(frt, norm_sum, 1)
            do(frt, rotate, 1)
            do(mlp, gated, 0)
            do(att, probs_out, 3)
            do(mlp, gated, 1)
            do(att, normalise)
            do(mlp, hidden_out)
            do(mlp, finish)

        layers(dve, step)

    @block.scalar
    def _(act):
        credit(act, [xT_ready, sq_ready, v_ready, qT_ready, kT_ready, e_ready, oT_ready, yT_ready, zT_ready, gel_ready,
                     uTb_ready])

        def xT_out(l, w, b):
            n = n_of(l, w, b)
            act.wait_ge(*f0_full(n, 0))
            act.wait_ge(*xT_carried(n))
            act.activation(xT[b][:, :, 1:W + 1], F0[:, 0:2 * W].rearrange("p (j k) -> p j k", j=2), ACT.Copy)\
                .then_inc(xT_ready.sem, 1)

        def squares(l, w, b, part):
            n = n_of(l, w, b)
            bank, full = [(F1, f1_full), (F0, f0_full)][part]
            act.wait_ge(*full(n, part))
            act.wait_ge(*ss_ready(n - 1, part))
            act.activation(sq[:, part, :], bank[:], ACT.Square).then_inc(sq_ready.sem, 1)

        def v_out(l, w, b):
            n = n_of(l, w, b)
            act.wait_ge(*f1_full(n, 1))
            act.wait_ge(*v_carried(n - 2))
            act.activation(V[b][:, 1, :], F1[:], ACT.Copy).then_inc(v_ready.sem, 1)

        def qT_out(l, w, b):
            n = n_of(l, w, b)
            act.wait_ge(*f0_full(n, 2))
            act.wait_ge(*s_full[1](n - 1, 1))
            act.activation(qT[:].rearrange("p c k -> p (c k)"), F0[:], ACT.Copy)\
                .then_inc(qT_ready.sem, 1)

        def kT_out(l, w, b):
            n = n_of(l, w, b)
            act.wait_ge(*f1_full(n, 2))
            act.wait_ge(*k_carried(n - 2))
            act.activation(kT[b][:, :, 1, :], F1[:].rearrange("p (c k) -> p c k", c=4), ACT.Copy)\
                .then_inc(kT_ready.sem, 1)

        def exponents(l, w, b, g):
            n = n_of(l, w, b)
            act.wait_ge(*nmax_ready(n, g))
            if g == 0:
                act.wait_ge(*rsum_ready(n - 1))
            act.wait_ge(*(t_full(n - 1, 2 + g) if g < 2 else t_full(n, g - 2)))
            for j in range(2):
                h = 2 * g + j
                e = act.activation(E[g % 2][:, j, :], S[g % 2][:, j * 256:(j + 1) * 256], ACT.Exp, bias=nmax[:, h:h + 1],
                                   accum_out=psum_e[:, head_of(g, j):head_of(g, j) + 1])
            e.then_inc(e_ready.sem, 1)

        def oT_out(l, w, b):
            n = n_of(l, w, b)
            act.wait_ge(*t_full(n, 4))
            act.wait_ge(*h0_full(n - 1, 0))
            act.activation(oT[:].rearrange("p c k -> p (c k)"), T[:], ACT.Copy)\
                .then_inc(oT_ready.sem, 1)

        def yT_out(l, w, b):
            n = n_of(l, w, b)
            act.wait_ge(*h1_full(n, 0))
            act.wait_ge(*yT_carried(n - 2))
            act.activation(yT[b][:, 1:W + 1], H1[:, 0:W], ACT.Copy).then_inc(yT_ready.sem, 1)

        def zT_out(l, w, b):
            n = n_of(l, w, b)
            act.wait_ge(*h1_full(n, 1))
            act.activation(zT[:].rearrange("p c k -> p (c k)"), H1[:, 0:2 * W], ACT.Copy)\
                .then_inc(zT_ready.sem, 1)

        def gelu(l, w, b, c):
            n = n_of(l, w, b)
            act.wait_ge(*h0_full(n, 2 + c))
            act.wait_ge(*u_ready(n - 1, c))
            act.activation(gel[:, c, :], H0[:, 0:HC], ACT.Gelu).then_inc(gel_ready.sem, 1)

        def uT_out(l, w, b):
            n = n_of(l, w, b)
            act.wait_ge(*h1_full(n, 4))
            act.wait_ge(*h0_full(n - 1, 5))
            act.activation(uT[:, 4, :], H1[:, 0:W], ACT.Copy)
            k = HID - (NU - 1) * P
            act.activation(uT[0:k, NU - 1, :], H1[0:k, W:2 * W], ACT.Copy)\
                .then_inc(uTb_ready.sem, 1)

        def step(mlp, att, frt):
            do(att, exponents, 0)
            do(att, exponents, 1)
            do(frt, xT_out)
            do(mlp, yT_out)
            do(att, exponents, 2)
            do(frt, squares, 0)
            do(att, exponents, 3)
            do(mlp, zT_out)
            do(frt, squares, 1)
            do(mlp, gelu, 0)
            do(frt, v_out)
            do(mlp, gelu, 1)
            do(frt, qT_out)
            do(mlp, uT_out)
            do(att, oT_out)
            do(frt, kT_out)

        layers(act, step)

    @block.gpsimd
    def _(pool):
        credit(pool, [xw_ready, xT_carried, tab_ready, rn_floor, rn_ready, rot_summed, qk_ready, v_carried, k_carried,
                      yT_carried, var_eps, rstd_ready, var2_eps, rstd2_ready, y_ready])

        def rows_in(l, w, b):
            n = n_of(l, w, b)
            pool.wait_ge(*f0_full(n - 2, 0))
            if l:
                pool.wait_ge(*x_ready(n - UNITS))
            pool.sem_inc(passed_pool, 1)
            pool.tensor_copy(xw[b][:], X[:, bass.ds((b * NW + w) * D, D)]).then_inc(xw_ready.sem, 1)
            pool.wait_ge(*rs_ready(n - 1, 1))
            pool.sem_inc(passed_pool, 1)
            pool.tensor_tensor(tab[:].rearrange("p a d -> p (a d)"), rope[:, bass.ds(w * 4 * DH, 4 * DH)],
                               scales[:, l, :], ALU.mult).then_inc(tab_ready.sem, 1)

        def norm(l, w, b, part):
            n = n_of(l, w, b)
            pool.wait_ge(*ss_ready(n, part))
            pool.sem_inc(passed_pool, 1)
            pool.tensor_scalar(rf[:, part, :], ss[:, part, :], 1e-24, None, ALU.max).then_inc(rn_floor.sem, 1)
            pool.wait_ge(*rn_floor(n, part))
            pool.tensor_tensor(rn[:, part, :], rf[:, part, :], nhalf[:, 0:FH], ALU.pow).then_inc(rn_ready.sem, 1)
            pool.wait_ge(*rs_ready(n, part))
            pool.wait_ge(*rc_ready(n, part))
            pool.tensor_tensor(rot[:, part, :], rc[:, part, :], rs[:, part, :], ALU.add).then_inc(rot_summed.sem, 1)
            pool.wait_ge(*rot_summed(n, part))
            pool.wait_ge(*rn_ready(n, part))
            pool.wait_ge(*[f0_full, f1_full][part](n - 1, 2))
            pool.tensor_tensor(qk[:, part, :].rearrange("p (h d) -> p h d", h=FH),
                               rot[:, part, :].rearrange("p (h d) -> p h d", h=FH), along(rn[:, part, :], DH), ALU.mult)\
                .then_inc(qk_ready.sem, 1)

        def carry_x(l, w, b):
            n = n_of(l, w, b)
            first = isinstance(w, int) and w == 0
            pool.wait_ge(*f1_full(n - 2, 1))
            if first:
                pool.memset(xT[b][:, 1, 0:1], 0.0).then_inc(xT_carried.sem, 1)
            else:
                pool.sem_inc(passed_pool, 1)
                pool.tensor_copy(xT[b][:, 1, 0:1], xT[b][:, 1, W:W + 1]).then_inc(xT_carried.sem, 1)

        def carry_k(l, w, b):
            n = n_of(l, w, b)
            pool.wait_ge(*s_full[1](n, 1))
            pool.wait_ge(*s_full[0](n, 1))
            pool.sem_inc(passed_pool, 1)
            pool.tensor_copy(kT[b][:, :, 0, :], kT[b][:, :, 1, :]).then_inc(k_carried.sem, 1)

        def carry_v(l, w, b):
            n = n_of(l, w, b)
            pool.wait_ge(*o_full(n, 0))
            pool.sem_inc(passed_pool, 1)
            pool.tensor_copy(V[b][:, 0, :], V[b][:, 1, :]).then_inc(v_carried.sem, 1)

        def rstd_of(l, w, b):
            n = n_of(l, w, b)
            pool.wait_ge(*mv_ready(n))
            pool.sem_inc(passed_pool, 1)
            pool.tensor_scalar(ve[:], mv[:, 1:2], LN_EPS, None, ALU.add).then_inc(var_eps.sem, 1)
            pool.wait_ge(*var_eps(n))
            pool.wait_ge(*z_ready(n - 1, 1))
            pool.tensor_tensor(rstd[:], ve[:], nhalf[:, 0:1], ALU.pow).then_inc(rstd_ready.sem, 1)

        def carry_y(l, w, b):
            n = n_of(l, w, b)
            last = isinstance(w, int) and w == NW - 1
            pool.wait_ge(*h0_full(n, 1))
            if last:
                pool.memset(yT[b][:, 0:1], 0.0).then_inc(yT_carried.sem, 1)
            else:
                pool.sem_inc(passed_pool, 1)
                pool.tensor_copy(yT[b][:, 0:1], yT[b][:, W:W + 1]).then_inc(yT_carried.sem, 1)

        def last_norm(l, w, b):
            m = n_of(l, w, b) - UNITS
            pool.wait_ge(*mv2_ready(m))
            pool.sem_inc(passed_pool, 1)
            pool.tensor_scalar(ve2[:], mv2[:, 1:2], LN_EPS, None, ALU.add).then_inc(var2_eps.sem, 1)
            pool.wait_ge(*var2_eps(m))
            pool.tensor_tensor(rstd2[:], ve2[:], nhalf[:, 0:1], ALU.pow).then_inc(rstd2_ready.sem, 1)
            pool.wait_ge(*rstd2_ready(m))
            pool.wait_ge(y_stored[b], 16 * (w + 1))
            pool.sem_inc(passed_pool, 1)
            pool.tensor_scalar(y[b][:], ysum[:], mv2[:, 0:1], rstd2[:], ALU.subtract, ALU.mult).then_inc(y_ready.sem, 1)

        for b in range(B):
            pool.memset(yT[b][:, 0:1], 0.0).then_inc(carries_zero, 1)
            pool.memset(V[b][:, 0, :], 0.0).then_inc(carries_zero, 1)
            pool.memset(kT[b][:, :, 0, :], 0.0).then_inc(carries_zero, 1)
        pool.wait_ge(carries_zero, 3 * B)

        def step(mlp, att, frt):
            do(frt, rows_in)
            do(frt, carry_x)
            do(mlp, rstd_of)
            do(mlp, carry_y)
            do(frt, norm, 0)
            do(att, carry_k)
            do(frt, norm, 1)
            do(att, carry_v)
            if mlp and mlp[0] == DEPTH - 1:
                last_norm(*mlp)

        layers(pool, step)

    @block.sync
    def _(sp):
        for b in range(B):
            sp.sem_inc(y_stored[b], 16)

        def rows(w, b):
            m = B * w + b
            sp.wait_ge(*ysum_ready(m - 2))
            sp.dma_start(xn[b][:], x_norm_dram[b, bass.ds(w * W, W), :]).then_inc(xn_loaded[b], 16)

        def store(w, b):
            m = B * w + b
            sp.wait_ge(*y_ready(m))
            sp.dma_start(out_dram[b, bass.ds(w * W, W), :], y[b][:]).then_inc(y_stored[b], 16)

        rows(0, 0)
        rows(0, 1)
        with sp.Fori(0, NW - 1) as w:
            for b in range(B):
                store(w, b)
                rows(w + 1, b)
        for b in range(B):
            store(NW - 1, b)
        for b in range(B):
            sp.wait_ge(y_stored[b], 16 * (NW + 1))
def rope_tables(np):
    f = np.float32
    half = np.arange(0, DH, 2, dtype=f)
    freqs = np.arange(L, dtype=f)[:, None] * (f(1.0) / f(10000.0) ** (half / f(DH)))[None, :]
    base = (half + f(0.4 * DH)) / f(1.4 * DH)
    power = (np.arange(L, dtype=f) - f(L // 2)) / f(W // 2)
    scale = base[None, :] ** power[:, None]
    cos, sin, scale = np.cos(freqs), np.sin(freqs), np.concatenate([scale, scale], axis=1)
    cos = np.concatenate([cos, cos], axis=1)
    sin = np.concatenate([-sin, sin], axis=1)
    factor = f(8.0)
    return np.concatenate([cos * scale * factor, sin * scale * factor, cos / scale, sin / scale], axis=1).astype(f)


def resident(nc, ctx):
    def sb(name, shape):
        return ctx.enter_context(nc.sbuf_tensor("r_" + name, shape, F32))

    return {"X": sb("X", [P, B * NW * D]), "ident": sb("ident", [P, P]), "nhalf": sb("nhalf", [P, 8])}


def ffn_resident(nc, ctx):
    def sb(name, shape, dt=F32):
        return ctx.enter_context(nc.sbuf_tensor("r_" + name, shape, dt))

    return {
        "wqkv": sb("wqkv", [P, DEPTH, 2, 3 * INNER]), "wo": sb("wo", [P, DEPTH, INNER // P, D]),
        "w1": sb("w1", [P, DEPTH, 2, 2 * HID]), "w2": sb("w2", [P, DEPTH, NU, D]),
        "bias1": sb("bias1", [P, DEPTH, 2 * HID], BF16), "bias2": sb("bias2", [P, DEPTH, D], BF16),
        "ones3": sb("ones3", [P, P], BF16), "identb": sb("identb", [P, P], BF16),
        "rope": sb("rope", [P, NW * 4 * DH]), "scales": sb("scales", [P, DEPTH, 4 * DH]),
        "mask": sb("mask", [P, NW * 2 * W], BF16),
    }


def delta_tables(np):
    i, j = np.arange(P)[:, None], np.arange(P)[None, :]
    joins = [(i // (2 * s) == j // (2 * s)) & (i % (2 * s) >= s) & (j % (2 * s) < s) for s in (2 ** n for n in range(NLEV + 1))]
    return np.concatenate(joins[1:] + [joins[0].T, i < j, i <= j], axis=1).astype(np.float32)


def program(nc, a, out):
    x_norm_dram = nc.dram_tensor("x_norm", (B, L, D), F32, kind="Internal").ap()
    with ExitStack() as ctx:
        t = resident(nc, ctx)
        steps = ctx.enter_context(nc.semaphore("ident_steps"))
        with nc.Block() as block:
            @block.gpsimd
            def _(pool):
                pool.memset(t["ident"][:], 0.0).then_inc(steps, 1)
                pool.memset(t["nhalf"][:], -0.5).then_inc(steps, 1)
                pool.wait_ge(steps, 2)
                pool.affine_select(out=t["ident"][:], in_=t["ident"][:], compare_op=ALU.not_equal, fill=1.0, base=0,
                                   pattern=[[-1, P]], channel_multiplier=1).then_inc(steps, 1)
                pool.wait_ge(steps, 3)

        with ExitStack() as delta:
            held = delta_layer(nc, delta, t, a, x_norm_dram)
            with nc.Block() as block:
                @block.gpsimd
                def _(pool):
                    for sem in held:
                        pool.sem_clear(sem)
        with ExitStack() as ffn:
            t.update(ffn_resident(nc, ffn))
            setup(nc, ctx, a, t)
            ffn_layers(nc, ffn, t, x_norm_dram, out)


_INS = {"hidden_states": "x", "Wq": "Wq", "Wk": "Wk", "Wv": "Wv", "conv_q": "conv_q", "conv_k": "conv_k", "conv_v": "conv_v",
        "Wb": "Wb", "Wdec": "Wdec", "Wmix": "Wmix", "conv_mix": "conv_mix", "mix_bias": "mix_bias", "rms_w": "rms_w", "Wo": "Wo"}
_FFN_INS = ["wqkv", "q_scale", "k_scale", "wo", "ln_g", "ln_b", "w1", "b1", "w2", "b2"]


def kernel(**inputs):
    import numpy as np
    import concourse.bacc as bacc
    from concourse.bass_utils import run_bass_kernel_spmd

    nc = bacc.Bacc("TRN2", target_bir_lowering=False, num_devices=1)
    arrays, a = {}, {}

    def put(key, array):
        name = f"in_{key}_dram"
        arrays[name] = np.ascontiguousarray(array)
        a[key] = nc.dram_tensor(name, array.shape, mybir.dt.from_np(arrays[name].dtype), kind="ExternalInput").ap()

    for name, key in _INS.items():
        put(key, inputs["L0_attn_" + name])
    for name in _FFN_INS:
        put(name, inputs["L0_ffn_" + name])
    put("rope", rope_tables(np))
    put("tables", delta_tables(np))
    out = nc.dram_tensor("out_0_dram", (B, L, D), F32, kind="ExternalOutput").ap()
    program(nc, a, out)
    r = run_bass_kernel_spmd(nc, [arrays], core_ids=[0])
    return r.results[0]["out_0_dram"]
```

```python
from contextlib import ExitStack
from itertools import chain

import concourse.bass as bass
from concourse import mybir

F32 = mybir.dt.float32
BF16 = mybir.dt.bfloat16
ALU = mybir.AluOpType
ACT = mybir.ActivationFunctionType
AX = mybir.AxisListType

P = 128
B, L, D = 2, 2048, 256
W = 128
NW = L // W
UNITS = B * NW
DEPTH = 2
FH, DH = 8, 64
INNER = FH * DH
HID = int(D * 4 * 2 / 3)
NU = -(-HID // P)
AH, DA = 4, 64
CK = 4
NF = 3 * D // P
NLEV = 6
LN_EPS = 1e-5
RMS_EPS = 1e-5
MASKED = 1e30
AHEAD = 2
EARLY = 2


class Signal:

    def __init__(self, sem, per=1):
        self.sem, self.sems, self.per = sem, [sem], per

    def __call__(self, n, k=0):
        return self.sem, (n + AHEAD) * self.per + k + 1


class EachSignal:

    def __init__(self, sems, per=1):
        self.sems, self.per = sems, per

    def __call__(self, n, b, k=0):
        return self.sems[b], (n + AHEAD) * self.per + k + 1


def credit(eng, signals):
    for s in signals:
        for sem in s.sems:
            eng.sem_inc(sem, AHEAD * s.per)


def before(reads, n, use):
    signal, k = reads[use - 1]
    return signal(n if use else n - 1, k)


def head_of(g, j):
    return 4 * (g // 2) + 2 * j + g % 2


def over_heads(ap, heads):
    return ap.unsqueeze(1).broadcast_to([ap.shape[0], heads, ap.shape[1]])


def along(ap, n):
    return ap.unsqueeze(2).broadcast_to([ap.shape[0], ap.shape[1], n])


def setup(nc, sems, a, t):
    with ExitStack() as ctx:
        def sb(name, shape, dt=F32):
            return ctx.enter_context(nc.sbuf_tensor("s_" + name, shape, dt))

        def sem(name):
            return sems.enter_context(nc.semaphore("s_" + name))

        ln_rows = sb("ln_rows", [4 * DEPTH, P])
        ln_cols = sb("ln_cols", [P, 4 * DEPTH])
        lg, lb = (ln_cols[:, i * 2 * DEPTH:(i + 1) * 2 * DEPTH].rearrange("p (l k) -> p l k", l=DEPTH) for i in range(2))
        b1 = sb("b1", [1, DEPTH, 2 * HID])
        one = sb("one", [1, 1])
        row = sb("row", [1, DEPTH, D])
        rest = sb("rest", [1, DEPTH, D])
        rest2 = sb("rest2", [1, DEPTH, D])
        parts = sb("parts", [1, 3, DEPTH, D], BF16)
        shift_ps = ctx.enter_context(nc.psum_tensor("s_shift", [P, DEPTH * 2 * NU], F32))
        ln_ps = ctx.enter_context(nc.psum_tensor("s_ln", [P, 4 * DEPTH], F32))
        ln_turned, ln_ready = sem("ln_turned"), sem("ln_ready")
        loaded, zeroed, tables = sem("loaded"), sem("zeroed"), sem("tables")
        w1_loaded = [sem(f"w1_loaded{l}") for l in range(DEPTH)]
        shifted, added, split, spread, folded = sem("shifted"), sem("added"), sem("split"), sem("spread"), sem("folded")
        block = ctx.enter_context(nc.Block())

        @block.sync
        def _(sp):
            for i, name in enumerate(("ln_g", "ln_b")):
                sp.dma_start(ln_rows[i * 2 * DEPTH:(i + 1) * 2 * DEPTH, :], a[name].rearrange("l (k p) -> (l k) p", p=P))\
                    .then_inc(w1_loaded[0], 16)
            sp.dma_start(b1[:], a["b1"].rearrange("(o l) n -> o l n", o=1)).then_inc(w1_loaded[0], 16)
            sp.dma_start(row[:], a["b2"].rearrange("(o l) n -> o l n", o=1)).then_inc(w1_loaded[0], 16)
            for l in range(DEPTH):
                sp.dma_start(t["w1"][:, l], a["w1"][l].rearrange("(k p) n -> p k n", p=P)).then_inc(w1_loaded[l], 16)
            sp.dma_start(t["wqkv"][:], a["wqkv"].rearrange("l (k p) n -> p l k n", p=P)).then_inc(loaded, 16)
            sp.dma_start(t["wo"][:], a["wo"].rearrange("l (k p) n -> p l k n", p=P)).then_inc(loaded, 16)
            full = (NU - 1) * P
            for l in range(DEPTH):
                sp.dma_start(t["w2"][:, l, 0:NU - 1, :], a["w2"][l, 0:full, :].rearrange("(k p) n -> p k n", p=P))\
                    .then_inc(loaded, 16)
            sp.dma_start(t["w2"][0:HID - full, :, NU - 1, :], a["w2"][:, full:HID, :].rearrange("l p n -> p l n"))\
                .then_inc(loaded, 16)
            sp.dma_start(t["rope"][:].rearrange("p (w c) -> p w c", w=NW), a["rope"].rearrange("(w p) c -> p w c", p=P))\
                .then_inc(loaded, 16)
            sp.wait_ge(split, 5)
            for i in range(3):
                sp.dma_start(t["bias2"][i:i + 1, :, :], parts[:, i]).then_inc(spread, 16)
            sp.wait_ge(spread, 16 * 3)
            sp.wait_ge(loaded, 16 * (4 + DEPTH))

        @block.scalar
        def _(act):
            n = 0
            for l in range(DEPTH):
                for i, name in enumerate(("q_scale", "k_scale")):
                    src = a[name][l:l + 1, :]
                    first = 2 * i * DH
                    for to, frm, size in ((0, 0, DH), (DH, DH // 2, DH // 2), (DH + DH // 2, 0, DH // 2)):
                        act.dma_start(t["scales"][:, l, first + to:first + to + size],
                                      src[:, frm:frm + size].broadcast_to([P, size])).then_inc(tables, 16)
                        n += 1
            act.wait_ge(tables, 16 * n)

        def fold(eng, l, k):
            eng.wait_ge(ln_ready, 1)
            eng.wait_ge(shifted, l + 1)
            eng.tensor_scalar(t["w1"][:, l, k, :], t["w1"][:, l, k, :], lg[:, l, k:k + 1], None, ALU.mult).then_inc(folded, 1)

        @block.gpsimd
        def _(pool):
            for tile, value in ((t["mask"], 0.0), (one, 1.0), (t["bias2"], 0.0), (t["ones3"], 1.0)):
                pool.memset(tile[:], value).then_inc(zeroed, 1)
            pool.wait_ge(zeroed, 4)
            m = t["mask"][:].rearrange("p f (a k) -> p f a k", a=2)
            pool.affine_select(out=m[:, :, 0, :], in_=m[:, :, 0, :], compare_op=ALU.is_ge, fill=MASKED, base=0,
                               pattern=[[0, 2], [1, W]], channel_multiplier=-1).then_inc(zeroed, 1)
            pool.affine_select(out=m[:, :, 1, :], in_=m[:, :, 1, :], compare_op=ALU.is_ge, fill=MASKED, base=0,
                               pattern=[[0, 2], [-1, W]], channel_multiplier=1).then_inc(zeroed, 1)
            pool.wait_ge(zeroed, 6)
            pool.memset(m[:, 0, 0, :], MASKED).then_inc(zeroed, 1)
            for l in range(DEPTH):
                fold(pool, l, 1)
            pool.wait_ge(folded, 2 * DEPTH)
            pool.wait_ge(zeroed, 7)

        @block.tensor
        def _(pe):
            pe.wait_ge(zeroed, 4)
            for l in range(DEPTH):
                pe.wait_ge(w1_loaded[l], 16 if l else 16 * 5)
                if l == 0:
                    pe.transpose(ln_ps[:], ln_rows[:], t["ident"][0:4 * DEPTH, 0:4 * DEPTH]).then_inc(ln_turned, 1)
                    pe.wait_ge(ln_ready, 1)
                for v in range(2):
                    for c in range(NU):
                        size = min(P, HID - c * P)
                        cols = slice(v * HID + c * P, v * HID + c * P + size)
                        out = shift_ps[0:size, (2 * l + v) * NU + c:(2 * l + v) * NU + c + 1]
                        for k in range(2):
                            pe.matmul(out, t["w1"][:, l, k, cols], lb[:, l, k:k + 1], start=(k == 0), stop=False)
                        mm = pe.matmul(out, b1[:, l, cols], one[:], start=False, stop=True)
                mm.then_inc(shifted, 1)

        @block.vector
        def _(dve):
            dve.wait_ge(ln_turned, 1)
            dve.tensor_copy(ln_cols[:], ln_ps[:]).then_inc(ln_ready, 1)
            dve.wait_ge(ln_ready, 1)
            dve.wait_ge(w1_loaded[0], 16 * 5)
            dve.wait_ge(zeroed, 4)
            dve.tensor_copy(parts[:, 0], row[:]).then_inc(split, 1)
            dve.wait_ge(split, 1)
            dve.tensor_tensor(rest[:], row[:], parts[:, 0], ALU.subtract).then_inc(split, 1)
            dve.wait_ge(split, 2)
            dve.tensor_copy(parts[:, 1], rest[:]).then_inc(split, 1)
            dve.wait_ge(split, 3)
            dve.tensor_tensor(rest2[:], rest[:], parts[:, 1], ALU.subtract).then_inc(split, 1)
            dve.wait_ge(split, 4)
            dve.tensor_copy(parts[:, 2], rest2[:]).then_inc(split, 1)
            for l in range(DEPTH):
                fold(dve, l, 0)
            full = HID // P
            bias1 = t["bias1"][:].rearrange("p l v c -> p (l v) c")
            sums = shift_ps[:].rearrange("p (a c) -> p a c", c=NU)
            dve.tensor_copy(bias1[:, :, 0:full], sums[:, :, 0:full]).then_inc(added, 1)
            dve.tensor_copy(bias1[0:HID - full * P, :, full:], sums[0:HID - full * P, :, full:]).then_inc(added, 1)
            dve.wait_ge(added, 2)


def delta_layer(nc, sems, t, a, x_norm_dram):
    with ExitStack() as ctx:
        def sb(name, shape, dt=F32):
            return ctx.enter_context(nc.sbuf_tensor("a_" + name, shape, dt))

        def pb(name):
            return ctx.enter_context(nc.psum_tensor("a_" + name, [P, 512], F32))

        held = []

        def sem(name):
            held.append(sems.enter_context(nc.semaphore("a_" + name)))
            return held[-1]

        def signal(name, per=1):
            return Signal(sem(name), per)

        def signals(name, per=1):
            return EachSignal([sem(f"{name}{b}") for b in range(B)], per)

        def by_pair(name, shape):
            return [[sb(f"{name}{g}{b}", shape) for b in range(B)] for g in range(2)]

        def each(name, shape):
            return [sb(f"{name}{b}", shape) for b in range(B)]

        X, ident, nhalf = t["X"], t["ident"], t["nhalf"]

        wA = sb("wA", [P, 2, 3 * D])
        wbeta = sb("wbeta", [P, 2, AH])
        wmix = sb("wmix", [P, 2, AH])
        wdec = sb("wdec", [P, 2, AH])
        wdecw = sb("wdecw", [P, 2, D])
        woA = sb("woA", [P, 2, D])
        rmsw = sb("rmsw", [P, 1])
        cw = sb("cw", [P, NF, CK])
        cmix = sb("cmix", [AH, CK])
        mbias = sb("mbias", [AH, 1])
        mhalf = sb("mhalf", [AH, 1])
        tables = sb("tables", [P, NLEV + 3, P])
        xT = sb("xT", [P, B, 2, P])
        pre = [sb(f"pre{g}", [P, NF, B, CK - 1 + P]) for g in range(2)]
        prem = [sb(f"prem{g}", [AH, B, CK - 1 + P]) for g in range(2)]
        conv = [sb(f"conv{g}", [P, NF, B, P]) for g in range(2)]
        convm = [sb(f"convm{g}", [AH, B, P]) for g in range(2)]
        th = sb("th", [P, NF, B, P])
        thm = sb("thm", [AH, B, P])
        s1 = sb("s1", [P, NF, B, P])
        s1m = sb("s1m", [AH, B, P])
        mth = sb("mth", [AH, B, P])
        s2 = sb("s2", [P, 4, B, P])
        gth = [sb(f"gth{g}", [P, 2, B, P]) for g in range(2)]
        gam = sb("gam", [P, 2, B, P])
        inn = sb("inn", [P, 2, B, P])
        ema = sb("ema", [P, 2, B, P])
        est = sb("est", [P, 2, B])
        xw = each("xw", [P, D])
        bth = by_pair("bth", [P, AH])
        beta = each("beta", [P, 2, AH])
        mixs = by_pair("mixs", [P, 2, AH])
        sqa = each("sqa", [P, 2 * D])
        ss = each("ss", [P, 2 * AH])
        se = each("se", [P, 2 * AH])
        rn = each("rn", [P, 2 * AH])
        qk = by_pair("qk", [P, 2 * D])
        vb = by_pair("vb", [P, D])
        emat = each("emat", [P, D])
        kb = each("kb", [P, D])
        tT = by_pair("tT", [P, 2, 3, P])
        LP = by_pair("LP", [P, AH, 2, P])
        m1 = each("m1", [P, AH, P])
        R = by_pair("R", [P, AH, P])
        T = each("T", [P, AH * P // 2])
        Xs = each("Xs", [P, AH, P])
        St = each("St", [P, 2, DA])
        r = each("r", [P, AH, DA])
        u = each("u", [P, AH, DA])
        om = each("om", [P, D])
        em = by_pair("em", [P, D])
        o2 = each("o2", [P, D])
        sqo = each("sqo", [P, D])
        so = each("so", [P, AH])
        sv = each("sv", [P, AH])
        ro = each("ro", [P, AH])
        o3 = each("o3", [P, D])
        o3T = each("o3T", [P, 2, P])
        xs = each("xs", [P, D])
        st = each("st", [P, 6])
        mv = each("mv", [P, 2])
        ve = each("ve", [P, 1])
        rstd = each("rstd", [P, 1])

        FA, FB, FC = pb("FA"), pb("FB"), pb("FC")
        Q = [pb("Q0"), pb("Q1")]
        Z0, Z1, Z2 = pb("Z0"), pb("Z1"), pb("Z2")

        xw_ready = signals("xw_ready")
        q_full = signals("q_full", 3 * NLEV)
        xT_ready = signals("xT_ready")
        pre_qk, gth_ready, bth_ready, prem_ready = (signals(x) for x in ("pre_qk", "gth", "bth", "prem"))
        beta_ready = signals("beta_ready", 2)
        sqa_ready, ss_ready, se_ready, rn_ready, qk_ready = (signals(x) for x in ("sqa", "ss", "se", "rn", "qk"))
        vb_ready, emat_ready, kb_ready = (signals(x) for x in ("vb", "emat", "kb"))
        mixs_ready = signals("mixs", 2)
        kbq_turned, k_turned = signals("kbq_turned"), signals("k_turned")
        lp_ready = signals("lp", 2)
        m1_ready, R0_ready = signals("m1"), signals("R_first")
        R_ready, T_ready, Xs_ready = (signals(x, NLEV) for x in ("R", "T", "Xs"))
        r_ready, u_ready, S_ready = signals("r", 2), signals("u"), signals("S")
        om_ready, em_ready, o2_ready = signals("om", 2), signals("em"), signals("o2")
        sqo_ready, so_ready, sv_ready, ro_ready, o3_ready = (signals(x) for x in ("sqo", "so", "sv", "ro", "o3"))
        o3T_ready, xs_ready, st_ready, mv_ready, ve_ready, rstd_ready, x_ready = (
            signals(x) for x in ("o3T", "xs", "st", "mv", "ve", "rstd", "x"))
        fa_full, fb_full, fc_full = signal("fa_full", 2), signal("fb_full", 2), signal("fc_full", 4)
        fam_full, fbm_full, fcm_full = signal("fam_full", 3), signal("fbm_full", 4), signal("fcm_full", 7)
        z0_full, z1_full, z2_full = signal("z0_full", 6), signal("z1_full", 4), signal("z2_full", 6)
        conv_done, convm_done = signal("conv", NF * (CK - 1)), signal("convm", CK - 1)
        carried = signal("carried", 2)
        th_ready, s1_ready, th2_ready, s2_ready = signal("th", 2), signal("s1", 2), signal("th2"), signal("s2")
        thm_ready, s1m_ready, mth_ready = signal("thm"), signal("s1m"), signal("mth")
        gam_ready, inn_ready, ema_ready, est_ready = signal("gam"), signal("inn"), signal("ema", 2 * B), signal("est")
        weights, folded, zeroed, stored = sem("weights"), sem("folded"), sem("zeroed"), sem("stored")
        rows_loaded = sem("rows_loaded")
        passed_pe, passed_dve, passed_pool = sem("passed_pe"), sem("passed_dve"), sem("passed_pool")
        N_WEIGHTS = 15 + B
        N_ZEROED = 3 + B

        fa_read = [(xT_ready, b, 0) for b in range(B)]
        fb_read = [(pre_qk, b, 0) for b in range(B)]
        fc_read = [(signal, b, 0) for b in range(B) for signal in (gth_ready, prem_ready)]
        fam_read = [(qk_ready, 0, 0)] + [(kbq_turned, b, 0) for b in range(B)]
        fbm_read = [(emat_ready, b, 0) for b in range(B)] + [(lp_ready, b, 0) for b in range(B)]
        fcm_read = [(mixs_ready, b, 1) for b in range(B)] + [(qk_ready, 1, 0)] + [(k_turned, b, 0) for b in range(B)]\
            + [(lp_ready, b, 1) for b in range(B)]
        z0_read = [(signal, b, 0) for signal in (r_ready, om_ready, xs_ready) for b in range(B)]
        z1_read = [(signal, b, 1) for signal in (r_ready, om_ready) for b in range(B)]
        z2_read = [(signal, b, 0) for signal in (u_ready, S_ready, o3T_ready) for b in range(B)]

        def freed_pair(reads, w, use):
            signal, b, k = reads[use - 1]
            return signal(w if use else w - 1, b, k)

        ORDER_PE = "EDEDDDEDEEDDEDPPDDPDEDPEPDEDPDEDPDDDFDDFDDDDDDDFDFDDFDFDDDD"
        ORDER_DVE = "EEDFDDEDFEFEDEFDEFFDDFEDEDEDFFDFDDFDDFFDDDDFFDDDD"
        ORDER_ACT = "DDEEDPEDEPEPFDEPDFPDFDFFDFDFFDD"
        ORDER_POOL = "PPEEFFFFF"
        def bank_for_projections(own, others, w, use):
            return freed_pair(own, w, use) if use else freed_pair(others, w - 1, 0)

        def bank_for_products(own, others, w, use):
            if use:
                return freed_pair(own, w, use)
            return freed_pair(own, w, 0) if isinstance(w, int) and w == NW - 1 else freed_pair(others, w + 2, 0)

        def halves(ap, i, side):
            return ap.rearrange("p (c side s) -> p side c s", side=2, s=2 ** (i + 1))[:, side]

        block = ctx.enter_context(nc.Block())

        def pairs(eng, projections, averages, products, doublings, end, order):
            def step(w, g):
                def stage(pair, piece, *args):
                    return piece(pair, *args) if not isinstance(pair, int) or 0 <= pair < NW else ()

                front = chain(stage(w + 1, averages, 1 - g), stage(w + 1, products, 1 - g))
                pieces = {"P": iter(stage(w + 2, projections, g)), "F": front,
                          "D": iter(stage(w, doublings, g)), "E": iter(stage(w - 1, end, 1 - g))}
                for whose in order.replace(" ", ""):
                    next(pieces[whose], None)
                for whose in "PEDF":
                    for _ in pieces[whose]:
                        pass

            for w in (-2, -1, 0):
                step(w, w % 2)
            with eng.Fori(0, NW // 2 - 2) as j:
                step(2 * j + 1, 1)
                step(2 * j + 2, 0)
            for w in range(NW - 3, NW + 1):
                step(w, w % 2)

        @block.tensor
        def _(pe):
            credit(pe, [fa_full, fb_full, fc_full, fam_full, fbm_full, fcm_full, q_full, z0_full, z1_full, z2_full])
            pe.wait_ge(folded, 3)
            pe.wait_ge(zeroed, N_ZEROED)

            def turn(bank, full, freed, tiles):
                pe.wait_ge(*freed)
                for i, tile in enumerate(tiles):
                    mm = pe.transpose(bank[:, i * P:(i + 1) * P], tile, ident[:])
                mm.then_inc(full.sem, 1)

            def projections(w, g):
                for b in range(B):
                    pe.wait_ge(*xw_ready(w, b))
                    pe.wait_ge(*bank_for_projections(fa_read, fam_read, w, b))
                    for j in range(2):
                        mm = pe.transpose(FA[:, j * P:(j + 1) * P], xw[b][:, j * P:(j + 1) * P], ident[:])
                    mm.then_inc(fa_full.sem, 1)
                yield
                for b in range(B):
                    pe.wait_ge(*xT_ready(w, b))
                    pe.wait_ge(*bank_for_projections(fb_read, fbm_read, w, b))
                    for f in range(4):
                        for k in range(2):
                            mm = pe.matmul(FB[:, f * P:(f + 1) * P], wA[:, k, f * P:(f + 1) * P], xT[:, b, k, :],
                                           start=(k == 0), stop=(k == 1))
                    mm.then_inc(fb_full.sem, 1)
                    yield
                    pe.wait_ge(*bank_for_projections(fc_read, fcm_read, w, 2 * b))
                    for f in range(4):
                        for k in range(2):
                            lhsT = wA[:, k, (4 + f) * P:(5 + f) * P] if f < 2 else wdecw[:, k, (f - 2) * P:(f - 1) * P]
                            mm = pe.matmul(FC[:, f * P:(f + 1) * P], lhsT, xT[:, b, k, :], start=(k == 0), stop=(k == 1))
                    mm.then_inc(fc_full.sem, 1)
                    yield
                    pe.wait_ge(*bank_for_projections(fc_read, fcm_read, w, 2 * b + 1))
                    for k in range(2):
                        pe.matmul(FC[:, 0:AH], xT[:, b, k, :], wbeta[:, k, :], start=(k == 0), stop=(k == 1))
                    for k in range(2):
                        mm = pe.matmul(FC[0:AH, P:2 * P], wmix[:, k, :], xT[:, b, k, :], start=(k == 0), stop=(k == 1))
                    mm.then_inc(fc_full.sem, 1)
                    yield

            def averages(w, g):
                return ()

            def products(w, g):
                pe.wait_ge(*mth_ready(w))
                for b in range(B):
                    pe.wait_ge(*bank_for_products(fcm_read, fc_read, w, b))
                    pe.sem_inc(passed_pe, 1)
                    pe.transpose(FC[:, 0:AH], mth[:, b, :], ident[0:AH, 0:AH]).then_inc(fcm_full.sem, 1)
                pe.wait_ge(*s2_ready(w))
                pe.wait_ge(*ema_ready(w, 2 * B - 1))
                for b in range(B):
                    tiles = [s2[:, f, b, :] for f in range(4)]
                    if b == 0:
                        turn(FA, fam_full, bank_for_products(fam_read, fa_read, w, 0), tiles)
                    else:
                        turn(FC, fcm_full, bank_for_products(fcm_read, fc_read, w, 2), tiles)
                    turn(FB, fbm_full, bank_for_products(fbm_read, fb_read, w, b),
                         [s1[:, 4 + f, b, :] for f in range(2)] + [ema[:, f, b, :] for f in range(2)])
                    yield
                for b in range(B):
                    pe.wait_ge(*kb_ready(w, b))
                    turn(FA, fam_full, bank_for_products(fam_read, fa_read, w, 1 + b),
                         [x for f in range(2) for x in (kb[b][:, f * P:(f + 1) * P], qk[g][b][:, f * P:(f + 1) * P])])
                    turn(FC, fcm_full, bank_for_products(fcm_read, fc_read, w, 3 + b),
                         [qk[g][b][:, (2 + f) * P:(3 + f) * P] for f in range(2)])
                    yield
                for b in range(B):
                    pe.wait_ge(*kbq_turned(w, b))
                    pe.wait_ge(*k_turned(w, b))
                    for e, (bank, full, use, reads) in enumerate(((FB, fbm_full, 2, fbm_read), (FC, fcm_full, 5, fcm_read))):
                        pe.wait_ge(*freed_pair(reads, w, use + b))
                        rows = slice(DA * e, DA * (e + 1))
                        for f in range(2):
                            mm = pe.matmul(bank[:, f * 2 * P:(f + 1) * 2 * P], tT[g][b][rows, f, 2, :],
                                           tT[g][b][rows, f, 0:2, :].rearrange("p a k -> p (a k)"), start=True, stop=True)
                        mm.then_inc(full.sem, 1)
                    yield

            def doublings(w, g):
                for i in range(NLEV):
                    for b in range(B):
                        if i == 0:
                            pe.wait_ge(*R0_ready(w, b))
                            pe.wait_ge(*R_ready(w - 1, b, NLEV - 1))
                        else:
                            pe.wait_ge(*R_ready(w, b, i - 1))
                        for h in range(AH):
                            mm = pe.transpose(Q[b][:, h * P:(h + 1) * P], R[g][b][:, h, :], ident[:])
                        mm.then_inc(q_full.sems[b], 1)
                        yield
                    for b in range(B):
                        pe.wait_ge(*T_ready(w, b, i))
                        for h in range(AH):
                            mm = pe.matmul(halves(Q[b][:, h * P:(h + 1) * P], i, 0), LP[g][b][:, h, 0, :],
                                           T[b][:, h * P // 2:(h + 1) * P // 2], start=True, stop=True)
                        mm.then_inc(q_full.sems[b], 1)
                        yield
                    for b in range(B):
                        pe.wait_ge(*Xs_ready(w, b, i))
                        for h in range(AH):
                            mm = pe.matmul(Q[b][:, h * P // 2:(h + 1) * P // 2], Xs[b][:, h, :],
                                           halves(R[g][b][:, h, :], i, 1), start=True, stop=True)
                        mm.then_inc(q_full.sems[b], 1)
                        yield

            def end(w, g):
                for b in range(B):
                    pe.wait_ge(*S_ready(w - 1, b))
                    for e, (bank, full, reads) in enumerate(((Z0, z0_full, z0_read), (Z1, z1_full, z1_read))):
                        pe.wait_ge(*freed_pair(reads, w, b))
                        rows = slice(DA * e, DA * (e + 1))
                        for f in range(2):
                            mm = pe.matmul(bank[:, f * DA:(f + 1) * DA], tT[g][b][rows, f, 0, :], St[b][rows, f, :],
                                           start=True, stop=True)
                        mm.then_inc(full.sem, 1)
                    yield
                for b in range(B):
                    pe.wait_ge(*r_ready(w, b, 1))
                    pe.wait_ge(*R_ready(w, b, NLEV - 1))
                    pe.wait_ge(*freed_pair(z2_read, w, b))
                    for h in range(AH):
                        mm = pe.matmul(Z2[:, h * DA:(h + 1) * DA], R[g][b][:, h, :], r[b][:, h, :], start=True, stop=True)
                    mm.then_inc(z2_full.sem, 1)
                    yield
                for b in range(B):
                    pe.wait_ge(*u_ready(w, b))
                    for e, (bank, full, reads) in enumerate(((Z0, z0_full, z0_read), (Z1, z1_full, z1_read))):
                        pe.wait_ge(*freed_pair(reads, w, 2 + b))
                        rows = slice(DA * e, DA * (e + 1))
                        for f in range(2):
                            h = 2 * e + f
                            cols = slice(f * DA, (f + 1) * DA)
                            pe.matmul(bank[:, cols], tT[g][b][rows, f, 1, :], St[b][rows, f, :], start=True, stop=False)
                            mm = pe.matmul(bank[:, cols], LP[g][b][:, h, 1, :], u[b][:, h, :], start=False, stop=True)
                        mm.then_inc(full.sem, 1)
                    pe.wait_ge(*freed_pair(z2_read, w, 2 + b))
                    for e in range(2):
                        for f in range(2):
                            mm = pe.matmul(Z2[DA * e:DA * (e + 1), f * DA:(f + 1) * DA],
                                           qk[g][b][:, D + (2 * f + e) * DA:D + (2 * f + e + 1) * DA], u[b][:, 2 * e + f, :],
                                           start=True, stop=True)
                    mm.then_inc(z2_full.sem, 1)
                    yield
                for b in range(B):
                    pe.wait_ge(*o3_ready(w, b))
                    turn(Z2, z2_full, freed_pair(z2_read, w, 4 + b), [o3[b][:, f * P:(f + 1) * P] for f in range(2)])
                    yield
                for b in range(B):
                    pe.wait_ge(*o3T_ready(w, b))
                    pe.wait_ge(*freed_pair(z0_read, w, 4 + b))
                    for k in range(2):
                        mm = pe.matmul(Z0[:, 0:D], o3T[b][:, k, :], woA[:, k, :], start=(k == 0), stop=(k == 1))
                    mm.then_inc(z0_full.sem, 1)
                    yield

            pairs(pe, projections, averages, products, doublings, end, ORDER_PE)

        @block.vector
        def _(dve):
            credit(dve, [beta_ready, ss_ready, qk_ready, vb_ready, mixs_ready, lp_ready, R_ready, Xs_ready, r_ready,
                         S_ready, om_ready, o2_ready, so_ready, o3_ready, xs_ready, st_ready, mv_ready, x_ready,
                         conv_done, convm_done, s1_ready, s1m_ready, s2_ready, gam_ready, inn_ready, ema_ready])
            dve.wait_ge(weights, 16 * N_WEIGHTS)
            dve.tensor_copy(wdecw[:].rearrange("p k (h d) -> p k h d", h=AH), wdec[:].unsqueeze(3).broadcast_to([P, 2, AH, DA]))\
                .then_inc(folded, 1)
            dve.tensor_scalar(woA[:].rearrange("p k n -> p (k n)"), woA[:].rearrange("p k n -> p (k n)"), rmsw[:], None, ALU.mult)\
                .then_inc(folded, 1)
            dve.tensor_scalar(mhalf[:], mbias[:], 0.5, None, ALU.mult).then_inc(folded, 1)
            for b in range(B):
                dve.memset(St[b][:], 0.0).then_inc(zeroed, 1)
            dve.wait_ge(zeroed, N_ZEROED)

            def projections(w, g):
                return ()

            def averages(w, g):
                for tap in range(1, CK):
                    if tap == 1:
                        for b in range(B):
                            dve.wait_ge(*gth_ready(w, b))
                            dve.wait_ge(*prem_ready(w, b))
                    for f in range(NF + 1):
                        m = f == NF
                        src, acc, c = (prem[g][:], convm[g][:], cmix) if m else (pre[g][:, f], conv[g][:, f], cw[:, f, :])
                        src = src[:, :, CK - 1 - tap:CK - 1 - tap + P]
                        weight = c[:, CK - 1 - tap:CK - tap]
                        if tap == 1 and f == 0:
                            dve.wait_ge(*carried(w, 1))
                        if tap > 1:
                            dve.wait_ge(*(convm_done(w, tap - 2) if m else conv_done(w, NF * (tap - 2) + f)))
                        dve.scalar_tensor_tensor(out=acc, in0=src, scalar=weight, in1=acc, op0=ALU.mult, op1=ALU.add)\
                            .then_inc((convm_done if m else conv_done).sem, 1)
                        if f == 3:
                            yield
                    yield
                for b in range(B):
                    dve.wait_ge(*gth_ready(w, b))
                dve.tensor_scalar(gam[:], gth[g][:], 0.5, 0.5, ALU.mult, ALU.add).then_inc(gam_ready.sem, 1)
                dve.wait_ge(*th_ready(w, 0))
                dve.scalar_tensor_tensor(out=s1[:, 0:4], in0=th[:, 0:4], scalar=1.0, in1=conv[g][:, 0:4], op0=ALU.add, op1=ALU.mult)\
                    .then_inc(s1_ready.sem, 1)
                dve.wait_ge(*thm_ready(w))
                dve.scalar_tensor_tensor(out=s1m[:], in0=thm[:], scalar=1.0, in1=convm[g][:], op0=ALU.add, op1=ALU.mult)\
                    .then_inc(s1m_ready.sem, 1)
                dve.wait_ge(*th_ready(w, 1))
                dve.wait_ge(*fbm_full(w - 1, 1))
                dve.scalar_tensor_tensor(out=s1[:, 4:6], in0=th[:, 4:6], scalar=1.0, in1=conv[g][:, 4:6], op0=ALU.add, op1=ALU.mult)\
                    .then_inc(s1_ready.sem, 1)
                dve.wait_ge(*s1_ready(w, 1))
                dve.scalar_tensor_tensor(out=inn[:], in0=gth[g][:], scalar=1.0, in1=s1[:, 4:6], op0=ALU.subtract, op1=ALU.mult)\
                    .then_inc(inn_ready.sem, 1)
                dve.wait_ge(*inn_ready(w))
                dve.wait_ge(*est_ready(w - 1))
                for f in range(2):
                    for b in range(B):
                        dve.tensor_tensor_scan(ema[:, f, b, :], gam[:, f, b, :], inn[:, f, b, :], est[:, f, b:b + 1],
                                               ALU.mult, ALU.add).then_inc(ema_ready.sem, 1)
                yield
                dve.wait_ge(*th2_ready(w))
                dve.wait_ge(*fam_full(w - 1, 0))
                dve.wait_ge(*fcm_full(w - 1, 2))
                dve.scalar_tensor_tensor(out=s2[:], in0=th[:, 0:4], scalar=1.0, in1=s1[:, 0:4], op0=ALU.add, op1=ALU.mult)\
                    .then_inc(s2_ready.sem, 1)
                yield

            def products(w, g):
                for b in range(B):
                    dve.wait_ge(*bth_ready(w, b))
                    dve.tensor_scalar(beta[b][:, 0, :], bth[g][b][:], 0.5, 0.5, ALU.mult, ALU.add).then_inc(beta_ready.sems[b], 1)
                    dve.tensor_scalar(beta[b][:, 1, :], bth[g][b][:], 0.25, 0.25, ALU.mult, ALU.add).then_inc(beta_ready.sems[b], 1)
                    dve.wait_ge(*fcm_full(w, b))
                    dve.tensor_scalar(mixs[g][b][:, 0, :], FC[:, 0:AH], 0.5, 0.5, ALU.mult, ALU.add).then_inc(mixs_ready.sems[b], 1)
                    dve.tensor_scalar(mixs[g][b][:, 1, :], FC[:, 0:AH], -0.5, 0.5, ALU.mult, ALU.add).then_inc(mixs_ready.sems[b], 1)
                yield
                for b in range(B):
                    dve.wait_ge(*sqa_ready(w, b))
                    dve.tensor_reduce(ss[b][:], sqa[b][:].rearrange("p (h d) -> p h d", h=2 * AH), AX.X, ALU.add)\
                        .then_inc(ss_ready.sems[b], 1)
                    dve.wait_ge(*fbm_full(w, b))
                    dve.wait_ge(*beta_ready(w, b, 1))
                    dve.tensor_tensor(vb[g][b][:].rearrange("p (h d) -> p h d", h=AH), FB[:, 0:D].rearrange("p (h d) -> p h d", h=AH),
                                      along(beta[b][:, 1, :], DA), ALU.mult).then_inc(vb_ready.sems[b], 1)
                    yield
                    dve.wait_ge(*rn_ready(w, b))
                    dve.wait_ge(*z2_full(w - 2, 2 + b))
                    dve.tensor_tensor(qk[g][b][:].rearrange("p (h d) -> p h d", h=2 * AH),
                                      (FA, FC)[b][:].rearrange("p (h d) -> p h d", h=2 * AH),
                                      along(rn[b][:], DA), ALU.mult).then_inc(qk_ready.sems[b], 1)
                    yield
                for b in range(B):
                    dve.wait_ge(*z1_full(w - 2, 2 + b))
                    for e, (bank, full, use) in enumerate(((FB, fbm_full, 2), (FC, fcm_full, 5))):
                        dve.wait_ge(*full(w, use + b))
                        dve.tensor_tensor(LP[g][b][:, 2 * e:2 * e + 2].rearrange("p f a k -> p f (a k)"),
                                          bank[:].rearrange("p (f k) -> p f k", f=2),
                                          tables[:, NLEV + 1:NLEV + 3, :].rearrange("p a k -> p (a k)").unsqueeze(1)
                                          .broadcast_to([P, 2, 2 * P]), ALU.mult).then_inc(lp_ready.sems[b], 1)
                    yield

            def doublings(w, g):
                for i in range(NLEV):
                    for b in range(B):
                        dve.wait_ge(*q_full(w, b, 3 * i + 1))
                        dve.tensor_tensor(Xs[b][:], Q[b][:].rearrange("p (h k) -> p h k", h=AH), over_heads(tables[:, i, :], AH),
                                          ALU.mult).then_inc(Xs_ready.sems[b], 1)
                        yield
                    for b in range(B):
                        dve.wait_ge(*q_full(w, b, 3 * i + 2))
                        right = halves(R[g][b][:].rearrange("p h k -> p (h k)"), i, 1)
                        dve.tensor_tensor(right, right, Q[b][:, 0:AH * P // 2].rearrange("p (c s) -> p c s", s=2 ** (i + 1)),
                                          ALU.subtract).then_inc(R_ready.sems[b], 1)
                        yield

            def end(w, g):
                for b in range(B):
                    for e, (bank, full) in enumerate(((Z0, z0_full), (Z1, z1_full))):
                        dve.wait_ge(*full(w, b))
                        if e == 0:
                            dve.wait_ge(*vb_ready(w, b))
                        dve.tensor_tensor(r[b][:, 2 * e:2 * e + 2, :], vb[g][b][:].rearrange("p (f e d) -> p e f d", f=2, e=2)[:, e],
                                          bank[:, 0:2 * DA].rearrange("p (f d) -> p f d", f=2), ALU.subtract)\
                            .then_inc(r_ready.sems[b], 1)
                    yield
                for b in range(B):
                    for e, (bank, full) in enumerate(((Z0, z0_full), (Z1, z1_full))):
                        dve.wait_ge(*full(w, 2 + b))
                        dve.tensor_tensor(om[b][:].rearrange("p (f e d) -> p e f d", f=2, e=2)[:, e],
                                          bank[:, 0:2 * DA].rearrange("p (f d) -> p f d", f=2),
                                          along(mixs[g][b][:, 1, :].rearrange("p (f e) -> p e f", e=2)[:, e], DA), ALU.mult)\
                            .then_inc(om_ready.sems[b], 1)
                    dve.wait_ge(*om_ready(w, b, 1))
                    dve.wait_ge(*em_ready(w, b))
                    dve.tensor_tensor(o2[b][:], om[b][:], em[g][b][:], ALU.add).then_inc(o2_ready.sems[b], 1)
                    dve.wait_ge(*z2_full(w, 2 + b))
                    dve.tensor_tensor(St[b][:].rearrange("p f d -> p (f d)"), St[b][:].rearrange("p f d -> p (f d)"),
                                      Z2[:, 0:2 * DA], ALU.add).then_inc(S_ready.sems[b], 1)
                    yield
                for b in range(B):
                    dve.wait_ge(*sqo_ready(w, b))
                    dve.tensor_reduce(so[b][:], sqo[b][:].rearrange("p (h d) -> p h d", h=AH), AX.X, ALU.add)\
                        .then_inc(so_ready.sems[b], 1)
                yield
                for b in range(B):
                    dve.wait_ge(*ro_ready(w, b))
                    dve.tensor_tensor(o3[b][:].rearrange("p (h d) -> p h d", h=AH), o2[b][:].rearrange("p (h d) -> p h d", h=AH),
                                      along(ro[b][:], DA), ALU.mult).then_inc(o3_ready.sems[b], 1)
                    yield
                for b in range(B):
                    dve.wait_ge(*z0_full(w, 4 + b))
                    dve.tensor_tensor(xs[b][:], Z0[:, 0:D], X[:, bass.ds((b * NW + w) * D, D)], ALU.add).then_inc(xs_ready.sems[b], 1)
                    dve.wait_ge(*xs_ready(w, b))
                    dve.bn_stats(st[b][:], xs[b][:]).then_inc(st_ready.sems[b], 1)
                    dve.wait_ge(*st_ready(w, b))
                    dve.sem_inc(passed_dve, 1)
                    dve.bn_aggr(mv[b][:], st[b][:]).then_inc(mv_ready.sems[b], 1)
                    yield
                for b in range(B):
                    dve.wait_ge(*rstd_ready(w, b))
                    dve.tensor_scalar(X[:, bass.ds((b * NW + w) * D, D)], xs[b][:], mv[b][:, 0:1], rstd[b][:],
                                      ALU.subtract, ALU.mult).then_inc(x_ready.sems[b], 1)
                yield

            pairs(dve, projections, averages, products, doublings, end, ORDER_DVE)

        @block.scalar
        def _(act):
            credit(act, [xT_ready, pre_qk, gth_ready, bth_ready, prem_ready, sqa_ready, emat_ready, kbq_turned, k_turned, T_ready,
                         u_ready, sqo_ready, o3T_ready, th_ready, th2_ready, thm_ready, mth_ready])
            act.wait_ge(folded, 3)
            act.wait_ge(zeroed, N_ZEROED)

            def gates(w, g, b):
                act.wait_ge(*fc_full(w, 2 * b + 1))
                act.wait_ge(*beta_ready(w - 2, b, 1))
                act.activation(bth[g][b][:], FC[:, 0:AH], ACT.Tanh, scale=0.5).then_inc(bth_ready.sems[b], 1)
                act.wait_ge(*s1m_ready(w - 2))
                act.activation(convm[g][:, b, :], FC[0:AH, P:2 * P], ACT.Copy, scale=cmix[:, CK - 1:CK])
                act.activation(prem[g][:, b, CK - 1:], FC[0:AH, P:2 * P], ACT.Copy).then_inc(prem_ready.sems[b], 1)

            def projected(w, g, b):
                act.wait_ge(*fb_full(w, b))
                if b == 0:
                    act.wait_ge(*carried(w - 1, 1))
                act.wait_ge(*s1_ready(w - 2, 1))
                for f in range(4):
                    act.activation(conv[g][:, f, b, :], FB[:, f * P:(f + 1) * P], ACT.Copy, scale=cw[:, f, CK - 1:CK])
                act.activation(pre[g][:, 0:4, b, CK - 1:], FB[:].rearrange("p (f k) -> p f k", f=4), ACT.Copy).then_inc(pre_qk.sems[b], 1)
                act.wait_ge(*fc_full(w, 2 * b))
                for f in range(2):
                    act.activation(conv[g][:, 4 + f, b, :], FC[:, f * P:(f + 1) * P], ACT.Copy, scale=cw[:, 4 + f, CK - 1:CK])
                act.activation(pre[g][:, 4:6, b, CK - 1:], FC[:, 0:2 * P].rearrange("p (f k) -> p f k", f=2), ACT.Copy)
                if b == 0:
                    act.wait_ge(*inn_ready(w - 2))
                act.activation(gth[g][:, :, b, :], FC[:, 2 * P:].rearrange("p (f k) -> p f k", f=2), ACT.Tanh, scale=0.5)\
                    .then_inc(gth_ready.sems[b], 1)

            def projections(w, g):
                for b in range(B):
                    act.wait_ge(*fa_full(w, b))
                    act.wait_ge(*fc_full(w - 1, 3))
                    act.activation(xT[:, b].rearrange("p k n -> p (k n)"), FA[:, 0:2 * P], ACT.Copy).then_inc(xT_ready.sems[b], 1)
                yield
                projected(w, g, 0)
                yield
                gates(w, g, 0)
                yield
                projected(w, g, 1)
                yield
                gates(w, g, 1)
                yield

            def averages(w, g):
                act.wait_ge(*conv_done(w, NF * (CK - 1) - 1))
                act.wait_ge(*s2_ready(w - 1))
                act.activation(th[:, 0:4], conv[g][:, 0:4], ACT.Tanh, scale=0.5).then_inc(th_ready.sem, 1)
                act.wait_ge(*convm_done(w, CK - 2))
                act.activation(thm[:], convm[g][:], ACT.Tanh, scale=0.5).then_inc(thm_ready.sem, 1)
                act.activation(th[:, 4:6], conv[g][:, 4:6], ACT.Tanh, scale=0.5).then_inc(th_ready.sem, 1)
                yield
                act.wait_ge(*s1_ready(w, 0))
                act.activation(th[:, 0:4], s1[:, 0:4], ACT.Tanh, scale=0.25).then_inc(th2_ready.sem, 1)
                act.wait_ge(*s1m_ready(w))
                act.wait_ge(*fcm_full(w - 1, 1))
                act.activation(mth[:], s1m[:], ACT.Tanh, scale=0.25, bias=mhalf[:]).then_inc(mth_ready.sem, 1)
                yield

            def products(w, g):
                for b in range(B):
                    act.wait_ge(*(fcm_full(w, 2) if b else fam_full(w, 0)))
                    act.activation(sqa[b][:], (FA, FC)[b][:], ACT.Square).then_inc(sqa_ready.sems[b], 1)
                    yield
                    act.wait_ge(*vb_ready(w, b))
                    act.wait_ge(*em_ready(w - 1, b))
                    act.activation(emat[b][:], FB[:, D:2 * D], ACT.Copy, scale=-0.25).then_inc(emat_ready.sems[b], 1)
                    yield
                for b in range(B):
                    act.wait_ge(*z1_full(w - 2, 2 + b))
                    act.wait_ge(*fam_full(w, 1 + b))
                    act.activation(tT[g][b][:, :, 0:2, :].rearrange("p f a k -> p f (a k)"), FA[:].rearrange("p (f k) -> p f k", f=2),
                                   ACT.Copy).then_inc(kbq_turned.sems[b], 1)
                    act.wait_ge(*fcm_full(w, 3 + b))
                    act.activation(tT[g][b][:, :, 2, :], FC[:, 0:2 * P].rearrange("p (f k) -> p f k", f=2), ACT.Copy)\
                        .then_inc(k_turned.sems[b], 1)
                    yield

            def doublings(w, g):
                for i in range(NLEV):
                    for b in range(B):
                        act.wait_ge(*q_full(w, b, 3 * i))
                        act.activation(T[b][:].rearrange("p (c s) -> p c s", s=2 ** (i + 1)), halves(Q[b][:], i, 0), ACT.Copy)\
                            .then_inc(T_ready.sems[b], 1)
                        yield

            def end(w, g):
                for b in range(B):
                    act.wait_ge(*z2_full(w, b))
                    act.activation(u[b][:].rearrange("p h d -> p (h d)"), Z2[:, 0:D], ACT.Copy).then_inc(u_ready.sems[b], 1)
                    yield
                for b in range(B):
                    act.wait_ge(*o2_ready(w, b))
                    act.activation(sqo[b][:], o2[b][:], ACT.Square).then_inc(sqo_ready.sems[b], 1)
                    yield
                for b in range(B):
                    act.wait_ge(*z2_full(w, 4 + b))
                    act.activation(o3T[b][:].rearrange("p f k -> p (f k)"), Z2[:, 0:2 * P], ACT.Copy).then_inc(o3T_ready.sems[b], 1)
                    yield

            pairs(act, projections, averages, products, doublings, end, ORDER_ACT)

        @block.gpsimd
        def _(pool):
            credit(pool, [m1_ready, R0_ready, xw_ready, se_ready, rn_ready, kb_ready, em_ready, sv_ready, ro_ready,
                          ve_ready, rstd_ready, carried, est_ready])
            for tile in (pre[1][:, :, :, P:], prem[1][:, :, P:], est[:]):
                pool.memset(tile, 0.0).then_inc(zeroed, 1)
            pool.wait_ge(weights, 16 * N_WEIGHTS)
            pool.wait_ge(zeroed, N_ZEROED)

            def projections(w, g):
                if isinstance(w, int) and w == EARLY:
                    pool.wait_ge(rows_loaded, 16 * B)
                for b in range(B):
                    pool.wait_ge(*fa_full(w - 1, b))
                    pool.sem_inc(passed_pool, 1)
                    pool.tensor_copy(xw[b][:], X[:, bass.ds((b * NW + w) * D, D)]).then_inc(xw_ready.sems[b], 1)
                yield
                for b in range(B):
                    pool.wait_ge(*gth_ready(w - 1, b))
                    pool.wait_ge(*prem_ready(w - 1, b))
                pool.wait_ge(*conv_done(w - 2, NF * (CK - 1) - 1))
                pool.sem_inc(passed_pool, 1)
                pool.tensor_copy(pre[g][:, :, :, 0:CK - 1], pre[1 - g][:, :, :, P:]).then_inc(carried.sem, 1)
                pool.wait_ge(*convm_done(w - 2, CK - 2))
                pool.sem_inc(passed_pool, 1)
                pool.tensor_copy(prem[g][:, :, 0:CK - 1], prem[1 - g][:, :, P:]).then_inc(carried.sem, 1)
                yield

            def averages(w, g):
                pool.wait_ge(*ema_ready(w, 2 * B - 1))
                pool.sem_inc(passed_pool, 1)
                pool.tensor_copy(est[:], ema[:, :, :, P - 1]).then_inc(est_ready.sem, 1)
                yield

            def products(w, g):
                for b in range(B):
                    pool.wait_ge(*ss_ready(w, b))
                    pool.sem_inc(passed_pool, 1)
                    pool.tensor_scalar(se[b][:], ss[b][:], 16e-6, None, ALU.add).then_inc(se_ready.sems[b], 1)
                    pool.wait_ge(*se_ready(w, b))
                    pool.tensor_tensor(rn[b][:], se[b][:], nhalf[:, 0:2 * AH], ALU.pow).then_inc(rn_ready.sems[b], 1)
                for b in range(B):
                    pool.wait_ge(*qk_ready(w, b))
                    pool.wait_ge(*beta_ready(w, b, 1))
                    pool.tensor_tensor(kb[b][:].rearrange("p (h d) -> p h d", h=AH), qk[g][b][:, D:].rearrange("p (h d) -> p h d", h=AH),
                                       along(beta[b][:, 0, :], DA), ALU.mult).then_inc(kb_ready.sems[b], 1)
                yield
                for b in range(B):
                    pool.wait_ge(*emat_ready(w, b))
                    pool.wait_ge(*o2_ready(w - 2, b))
                    pool.wait_ge(*mixs_ready(w, b, 1))
                    pool.tensor_tensor(em[g][b][:].rearrange("p (h d) -> p h d", h=AH), emat[b][:].rearrange("p (h d) -> p h d", h=AH),
                                       along(mixs[g][b][:, 0, :], DA), ALU.mult).then_inc(em_ready.sems[b], 1)
                yield
                for b in range(B):
                    pool.wait_ge(*lp_ready(w, b, 1))
                    pool.tensor_tensor(m1[b][:], LP[g][b][:, :, 0, :], over_heads(tables[:, NLEV, :], AH), ALU.mult)\
                        .then_inc(m1_ready.sems[b], 1)
                    pool.wait_ge(*m1_ready(w, b))
                    pool.wait_ge(*z2_full(w - 2, b))
                    pool.tensor_tensor(R[g][b][:], over_heads(ident[:], AH), m1[b][:], ALU.subtract).then_inc(R0_ready.sems[b], 1)
                    yield

            def doublings(w, g):
                return ()

            def end(w, g):
                for b in range(B):
                    pool.wait_ge(*so_ready(w, b))
                    pool.sem_inc(passed_pool, 1)
                    pool.tensor_scalar(sv[b][:], so[b][:], 1.0 / DA, RMS_EPS, ALU.mult, ALU.add).then_inc(sv_ready.sems[b], 1)
                    pool.wait_ge(*sv_ready(w, b))
                    pool.tensor_tensor(ro[b][:], sv[b][:], nhalf[:, 0:AH], ALU.pow).then_inc(ro_ready.sems[b], 1)
                yield
                for b in range(B):
                    pool.wait_ge(*mv_ready(w, b))
                    pool.sem_inc(passed_pool, 1)
                    pool.tensor_scalar(ve[b][:], mv[b][:, 1:2], LN_EPS, None, ALU.add).then_inc(ve_ready.sems[b], 1)
                    pool.wait_ge(*ve_ready(w, b))
                    pool.tensor_tensor(rstd[b][:], ve[b][:], nhalf[:, 0:1], ALU.pow).then_inc(rstd_ready.sems[b], 1)
                yield

            pairs(pool, projections, averages, products, doublings, end, ORDER_POOL)

        @block.sync
        def _(sp):
            def rows(t, b):
                return t.rearrange("b (w p) d -> b p w d", p=P)[b]

            def load(out, src):
                sp.dma_start(out, src, allow_slow_non_contiguous=True).then_inc(weights, 16)

            x_sb = X[:].rearrange("p (b w d) -> p b w d", b=B, w=NW)
            for b in range(B):
                load(x_sb[:, b, 0:EARLY], rows(a["x"], b)[:, 0:EARLY])
            for i, name in enumerate(("Wq", "Wk", "Wv")):
                load(wA[:, :, i * D:(i + 1) * D], a[name].rearrange("(k p) n -> p k n", p=P))
            for tile, name in ((wbeta, "Wb"), (wmix, "Wmix"), (wdec, "Wdec"), (woA, "Wo")):
                load(tile[:], a[name].rearrange("(k p) n -> p k n", p=P))
            for e in range(2):
                load(rmsw[DA * e:DA * (e + 1), :], a["rms_w"].rearrange("(p o) -> p o", o=1))
            for i, name in enumerate(("conv_q", "conv_k", "conv_v")):
                load(cw[:, 2 * i:2 * i + 2, :], a[name].rearrange("(f p) c -> p f c", p=P))
            load(cmix[:], a["conv_mix"])
            load(mbias[:], a["mix_bias"].rearrange("(p o) -> p o", o=1))
            load(tables[:], a["tables"].rearrange("p (i k) -> p i k", k=P))
            for b in range(B):
                sp.dma_start(x_sb[:, b, EARLY:], rows(a["x"], b)[:, EARLY:]).then_inc(rows_loaded, 16)

            def store(w, b):
                sp.wait_ge(*x_ready(w, b))
                sp.dma_start(x_norm_dram[b, bass.ds(w * P, P), :], X[:, bass.ds((b * NW + w) * D, D)]).then_inc(stored, 16)

            with sp.Fori(0, NW) as w:
                for b in range(B):
                    store(w, b)
            sp.wait_ge(stored, 16 * UNITS)

    return held


def ffn_layers(nc, ctx, t, x_norm_dram, out_dram):

    def sb(name, shape, dt=F32):
        return ctx.enter_context(nc.sbuf_tensor("f_" + name, shape, dt))

    def pb(name):
        return ctx.enter_context(nc.psum_tensor("f_" + name, [P, 512], F32))

    def signal(name, per=1):
        return Signal(ctx.enter_context(nc.semaphore("f_" + name)), per)

    X, ident = t["X"], t["ident"]
    wqkv, wo, w1, w2 = t["wqkv"], t["wo"], t["w1"], t["w2"]
    bias1, bias2, ones3 = t["bias1"], t["bias2"], t["ones3"]
    halves = (range(0, 4), range(4, NU))
    rope, scales, mask = t["rope"], t["scales"], t["mask"]

    xw = [sb(f"xw{b}", [P, D]) for b in range(B)]
    xT = [sb(f"xT{b}", [P, 2, W + 1]) for b in range(B)]
    tab = sb("tab", [P, 4, DH])
    sq = sb("sq", [P, 2, INNER])
    ss = sb("ss", [P, 2, FH])
    rn = sb("rn", [P, 2, FH])
    rf = sb("rf", [P, 2, FH])
    rot = sb("rot", [P, 2, INNER])
    rc = sb("rc", [P, 2, INNER])
    rs = sb("rs", [P, 2, INNER])
    qk = sb("qk", [P, 2, INNER])
    qT = sb("qT", [P, 4, W])
    kT = [sb(f"kT{b}", [P, 4, 2, W]) for b in range(B)]
    V = [sb(f"V{b}", [P, 2, INNER]) for b in range(B)]
    nmax = sb("nmax", [P, FH])
    psum_e = sb("psum_e", [P, FH])
    rsum = sb("rsum", [P, FH])
    masked = [sb(f"masked{i}", [P, 2, 2 * W]) for i in range(2)]
    E = [sb(f"E{i}", [P, 2, 2 * W]) for i in range(2)]
    ET = [sb(f"ET{i}", [P, 2, 2, W]) for i in range(2)]
    o = sb("o", [P, INNER])
    oT = sb("oT", [P, 4, W])
    x1 = sb("x1", [P, D])
    yT = [sb(f"yT{b}", [P, W + 1]) for b in range(B)]
    st = sb("st", [P, 2, 6])
    mv = sb("mv", [P, 2])
    rstd = sb("rstd", [P, 1])
    ve = sb("ve", [P, 1])
    ve2 = sb("ve2", [P, 1])
    z = sb("z", [P, D])
    zT = sb("zT", [P, 2, W])
    gel = sb("gel", [P, NU, W])
    uT = sb("uT", [P, NU, W])
    xn = [sb(f"xn{b}", [P, D]) for b in range(B)]
    yres = sb("yres", [P, D])
    ysum = sb("ysum", [P, D])
    st2 = sb("st2", [P, 6])
    mv2 = sb("mv2", [P, 2])
    rstd2 = sb("rstd2", [P, 1])
    y = [sb(f"y{b}", [P, D]) for b in range(B)]
    nhalf = t["nhalf"]

    F0, F1 = pb("F0"), pb("F1")
    S = [pb("S0"), pb("S1")]
    T, O = pb("T"), pb("O")
    H0, H1 = pb("H0"), pb("H1")

    f0_full, f1_full = signal("f0_full", 3), signal("f1_full", 3)
    s_full = [signal("s0_full", 2), signal("s1_full", 2)]
    t_full, o_full = signal("t_full", 5), signal("o_full")
    h0_full, h1_full = signal("h0_full", 5), signal("h1_full", 4)
    xw_ready = signal("xw_ready")
    xT_ready = signal("xT_ready")
    xT_carried = signal("xT_carried")
    tab_ready = signal("tab_ready")
    sq_ready = signal("sq_ready", 2)
    ss_ready = signal("ss_ready", 2)
    rn_floor = signal("rn_floor", 2)
    et_used = signal("et_used", 3)
    rn_ready = signal("rn_ready", 2)
    rc_ready = signal("rc_ready", 2)
    rs_ready = signal("rs_ready", 2)
    rot_summed = signal("rot_summed", 2)
    qk_ready = signal("qk_ready", 2)
    v_ready = signal("v_ready")
    v_carried = signal("v_carried")
    k_carried = signal("k_carried")
    qT_ready = signal("qT_ready")
    kT_ready = signal("kT_ready")
    nmax_ready = signal("nmax_ready", 4)
    e_ready = signal("e_ready", 4)
    eT_ready = signal("eT_ready", 4)
    rsum_ready = signal("rsum_ready")
    o_ready = signal("o_ready")
    oT_ready = signal("oT_ready")
    x1_ready = signal("x1_ready")
    yT_ready = signal("yT_ready")
    yT_carried = signal("yT_carried")
    st_ready = signal("st_ready", 2)
    mv_ready = signal("mv_ready")
    var_eps = signal("var_eps")
    rstd_ready = signal("rstd_ready")
    z_ready = signal("z_ready", 2)
    zT_ready = signal("zT_ready")
    gel_ready = signal("gel_ready", 2)
    u_ready = signal("u_ready", 2)
    x_ready = signal("x_ready")
    xn_loaded = [ctx.enter_context(nc.semaphore(f"f_xn_loaded{b}")) for b in range(B)]
    ysum_ready = signal("ysum_ready")
    st2_ready = signal("st2_ready")
    mv2_ready = signal("mv2_ready")
    var2_eps = signal("var2_eps")
    rstd2_ready = signal("rstd2_ready")
    y_ready = signal("y_ready")
    y_stored = [ctx.enter_context(nc.semaphore(f"f_y_stored{b}")) for b in range(B)]
    passed_dve = ctx.enter_context(nc.semaphore("f_passed_dve"))
    passed_pool = ctx.enter_context(nc.semaphore("f_passed_pool"))
    carries_zero = ctx.enter_context(nc.semaphore("f_carries_zero"))

    f0_read = [(xT_ready, 0), (rs_ready, 1), (qT_ready, 0)]
    f1_read = [(rs_ready, 0), (v_ready, 0), (kT_ready, 0)]
    s_read = [[(nmax_ready, 0), (nmax_ready, 2)], [(nmax_ready, 1), (nmax_ready, 3)]]
    t_read = [(eT_ready, g) for g in range(4)] + [(oT_ready, 0)]
    o_read = [(o_ready, 0)]
    h0_read = [(x1_ready, 0), (z_ready, 1), (gel_ready, 0), (gel_ready, 1), (x_ready, 0)]
    h1_read = [(yT_ready, 0), (zT_ready, 0), (u_ready, 0), (u_ready, 1)]

    block = ctx.enter_context(nc.Block())

    def n_of(l, w, b):
        return l * UNITS + B * w + b

    def do(unit, piece, *part):
        if unit:
            piece(*unit, *part)

    def layers(eng, step):
        step(None, None, (0, 0, 0))
        step(None, (0, 0, 0), (0, 0, 1))
        for l in range(DEPTH):
            step((l, 0, 0), (l, 0, 1), (l, 1, 0))
            step((l, 0, 1), (l, 1, 0), (l, 1, 1))
            with eng.Fori(1, NW - 1) as w:
                step((l, w, 0), (l, w, 1), (l, w + 1, 0))
                step((l, w, 1), (l, w + 1, 0), (l, w + 1, 1))
            more = l < DEPTH - 1
            step((l, NW - 1, 0), (l, NW - 1, 1), (l + 1, 0, 0) if more else None)
            step((l, NW - 1, 1), (l + 1, 0, 0) if more else None, (l + 1, 0, 1) if more else None)

    @block.tensor
    def _(pe):
        credit(pe, [f0_full, f1_full, s_full[0], s_full[1], t_full, o_full, h0_full, h1_full, et_used])
        pe.wait_ge(carries_zero, 6)

        def xT_turn(l, w, b):
            n = n_of(l, w, b)
            pe.wait_ge(*xw_ready(n))
            pe.wait_ge(*before(f0_read, n, 0))
            for j in range(2):
                mm = pe.transpose(F0[:, j * W:(j + 1) * W], xw[b][:, j * P:(j + 1) * P], ident[:])
            mm.then_inc(f0_full.sem, 1)

        def project(l, w, b, part):
            n = n_of(l, w, b)
            bank, full, read, use = [(F1, f1_full, f1_read, 0), (F0, f0_full, f0_read, 1), (F1, f1_full, f1_read, 1)][part]
            if part == 0:
                pe.wait_ge(*xT_ready(n))
            pe.wait_ge(*before(read, n, use))
            pe.matmul(bank[:], xT[b][:, 0, 1:W + 1], wqkv[:, l, 0, part * INNER:(part + 1) * INNER], start=True, stop=False)
            pe.matmul(bank[:], xT[b][:, 1, 0:W], wqkv[:, l, 1, part * INNER:(part + 1) * INNER], start=False, stop=True)\
                .then_inc(full.sem, 1)

        def qk_turn(l, w, b, part):
            n = n_of(l, w, b)
            bank, full, read = [(F0, f0_full, f0_read), (F1, f1_full, f1_read)][part]
            pe.wait_ge(*qk_ready(n, part))
            pe.wait_ge(*before(read, n, 2))
            for c in range(4):
                mm = pe.transpose(bank[:, c * W:(c + 1) * W], qk[:, part, c * P:(c + 1) * P], ident[:])
            mm.then_inc(full.sem, 1)

        def scores(l, w, b, g):
            n = n_of(l, w, b)
            bank = S[g % 2]
            if g == 0:
                pe.wait_ge(*qT_ready(n))
                pe.wait_ge(*kT_ready(n))
            pe.wait_ge(*before(s_read[g % 2], n, g // 2))
            rows = slice(64 * (g % 2), 64 * (g % 2) + 64)
            for j in range(2):
                c = 2 * (g // 2) + j
                mm = pe.matmul(bank[:, j * 256:(j + 1) * 256], qT[rows, c, :], kT[b][rows, c, :, :].rearrange("p a k -> p (a k)"),
                               start=True, stop=True)
            mm.then_inc(s_full[g % 2].sem, 1)

        def probs_turn(l, w, b, g):
            n = n_of(l, w, b)
            pe.wait_ge(*e_ready(n, g))
            pe.wait_ge(*before(t_read, n, g))
            for j in range(2):
                for a in range(2):
                    mm = pe.transpose(T[:, (2 * j + a) * W:(2 * j + a + 1) * W], E[g % 2][:, j, a * W:(a + 1) * W], ident[:])
            mm.then_inc(t_full.sem, 1)

        def attend(l, w, b, g):
            n = n_of(l, w, b)
            if g == 0:
                pe.wait_ge(*v_ready(n))
                pe.wait_ge(*before(o_read, n, 0))
            pe.wait_ge(*eT_ready(n, g))
            for j in range(2):
                h = head_of(g, j)
                for a in range(2):
                    mm = pe.matmul(O[:, h * DH:(h + 1) * DH], ET[g % 2][:, j, a, :], V[b][:, a, h * DH:(h + 1) * DH],
                                   start=(a == 0), stop=(a == 1))
            if g == 3:
                mm.then_inc(o_full.sem, 1)
            else:
                mm.then_inc(et_used.sem, 1)

        def out_turn(l, w, b):
            n = n_of(l, w, b)
            pe.wait_ge(*o_ready(n))
            pe.wait_ge(*before(t_read, n, 4))
            for c in range(4):
                mm = pe.transpose(T[:, c * W:(c + 1) * W], o[:, c * P:(c + 1) * P], ident[:])
            mm.then_inc(t_full.sem, 1)

        def out_project(l, w, b):
            n = n_of(l, w, b)
            pe.wait_ge(*oT_ready(n))
            pe.wait_ge(*before(h0_read, n, 0))
            for c in range(4):
                mm = pe.matmul(H0[:, 0:D], oT[:, c, :], wo[:, l, c, :], start=(c == 0), stop=(c == 3))
            mm.then_inc(h0_full.sem, 1)

        def shift_down(l, w, b):
            n = n_of(l, w, b)
            pe.wait_ge(*x1_ready(n))
            pe.wait_ge(*before(h1_read, n, 0))
            pe.transpose(H1[:, 0:W], x1[:, P:D], ident[:]).then_inc(h1_full.sem, 1)

        def shift_back(l, w, b):
            n = n_of(l, w, b)
            pe.wait_ge(*yT_ready(n))
            pe.wait_ge(*before(h0_read, n, 1))
            pe.transpose(H0[:, 0:P], yT[b][:, 0:W], ident[:]).then_inc(h0_full.sem, 1)

        def z_turn(l, w, b):
            n = n_of(l, w, b)
            pe.wait_ge(*z_ready(n, 1))
            pe.wait_ge(*before(h1_read, n, 1))
            for j in range(2):
                mm = pe.transpose(H1[:, j * W:(j + 1) * W], z[:, j * P:(j + 1) * P], ident[:])
            mm.then_inc(h1_full.sem, 1)

        def hidden(l, w, b, part):
            n = n_of(l, w, b)
            if part == 0:
                pe.wait_ge(*zT_ready(n))
            for bank, full, read, first in ((H0, h0_full, h0_read, HID), (H1, h1_full, h1_read, 0)):
                pe.wait_ge(*before(read, n, 2 + part))
                for i, c in enumerate(halves[part]):
                    size = min(P, HID - c * P)
                    cols = slice(first + c * P, first + c * P + size)
                    for k in range(2):
                        mm = pe.matmul(bank[0:size, i * W:(i + 1) * W], w1[:, l, k, cols], zT[:, k, :], start=(k == 0), stop=(k == 1))
                mm.then_inc(full.sem, 1)

        def down(l, w, b):
            n = n_of(l, w, b)
            pe.wait_ge(*before(h0_read, n, 4))
            pe.matmul(H0[:, 0:D], ones3[:], bias2[:, l, :], start=True, stop=False)
            for c in range(NU):
                if c == 0:
                    pe.wait_ge(*u_ready(n, 0))
                if c == 4:
                    pe.wait_ge(*u_ready(n, 1))
                k = min(P, HID - c * P)
                mm = pe.matmul(H0[:, 0:D], uT[0:k, c, :], w2[0:k, l, c, :], start=False, stop=(c == NU - 1))
            mm.then_inc(h0_full.sem, 1)

        def step(mlp, att, frt):
            do(att, scores, 0)
            do(mlp, out_project)
            do(att, scores, 1)
            do(frt, xT_turn)
            do(att, probs_turn, 0)
            do(mlp, shift_down)
            do(att, scores, 2)
            do(att, probs_turn, 1)
            do(mlp, shift_back)
            do(frt, project, 0)
            do(att, scores, 3)
            do(att, attend, 0)
            do(mlp, z_turn)
            do(frt, project, 1)
            do(att, probs_turn, 2)
            do(mlp, hidden, 0)
            do(att, attend, 2)
            do(att, attend, 1)
            do(frt, project, 2)
            do(att, probs_turn, 3)
            do(mlp, hidden, 1)
            do(frt, qk_turn, 0)
            do(att, attend, 3)
            do(frt, qk_turn, 1)
            do(mlp, down)
            do(att, out_turn)

        layers(pe, step)

    @block.vector
    def _(dve):
        credit(dve, [ss_ready, rc_ready, rs_ready, nmax_ready, eT_ready, rsum_ready, o_ready, x1_ready, st_ready,
                     mv_ready, z_ready, u_ready, x_ready, ysum_ready, st2_ready, mv2_ready])

        def norm_sum(l, w, b, part):
            n = n_of(l, w, b)
            dve.wait_ge(*sq_ready(n, part))
            dve.wait_ge(*rn_floor(n - 1, part))
            dve.tensor_reduce(ss[:, part, :], sq[:, part, :].rearrange("p (h d) -> p h d", h=FH), AX.X, ALU.add)\
                .then_inc(ss_ready.sem, 1)

        def rotate(l, w, b, part):
            n = n_of(l, w, b)
            bank = [F1, F0][part]
            xh = bank[:].rearrange("p (h d) -> p h d", h=FH)
            out = rs[:, part, :].rearrange("p (h d) -> p h d", h=FH)
            if part == 0:
                dve.wait_ge(*tab_ready(n))
            dve.wait_ge(*rot_summed(n - 1, part))
            dve.tensor_tensor(rc[:, part, :].rearrange("p (h d) -> p h d", h=FH), xh, over_heads(tab[:, 2 * part, :], FH),
                              ALU.mult).then_inc(rc_ready.sem, 1)
            half = DH // 2
            dve.tensor_tensor(out[:, :, 0:half], xh[:, :, half:DH], over_heads(tab[:, 2 * part + 1, 0:half], FH), ALU.mult)
            dve.tensor_tensor(out[:, :, half:DH], xh[:, :, 0:half], over_heads(tab[:, 2 * part + 1, half:DH], FH), ALU.mult)\
                .then_inc(rs_ready.sem, 1)

        def row_max(l, w, b, g):
            n = n_of(l, w, b)
            dve.wait_ge(*s_full[g % 2](n, g // 2))
            dve.wait_ge(*(e_ready(n - 1, 2 + g) if g < 2 else e_ready(n, g - 2)))
            if g == 0:
                dve.wait_ge(*rsum_ready(n - 1))
            window = 0 if isinstance(w, int) and w == 0 else 1
            for j in range(2):
                h = 2 * g + j
                if j == 0:
                    dve.sem_inc(passed_dve, 1)
                low = dve.tensor_tensor_reduce(masked[g % 2][:, j, :], mask[:, window, :], S[g % 2][:, j * 256:(j + 1) * 256],
                                               1.0, 3e38, ALU.add, ALU.min, accum_out=nmax[:, h:h + 1])
            low.then_inc(nmax_ready.sem, 1)

        def probs_out(l, w, b, g):
            n = n_of(l, w, b)
            dve.wait_ge(*t_full(n, g))
            if g < 2:
                dve.wait_ge(*o_full(n - 1, 0))
            else:
                dve.wait_ge(*et_used(n, g - 2))
            dve.tensor_copy(ET[g % 2][:].rearrange("p j a k -> p (j a k)"), T[:]).then_inc(eT_ready.sem, 1)

        def normalise(l, w, b):
            n = n_of(l, w, b)
            dve.wait_ge(*e_ready(n, 3))
            dve.reciprocal(rsum[:], psum_e[:]).then_inc(rsum_ready.sem, 1)
            dve.wait_ge(*rsum_ready(n))
            dve.wait_ge(*o_full(n, 0))
            dve.wait_ge(*t_full(n - 1, 4))
            dve.tensor_tensor(o[:].rearrange("p (h d) -> p h d", h=FH), O[:].rearrange("p (h d) -> p h d", h=FH),
                              along(rsum[:], DH), ALU.mult).then_inc(o_ready.sem, 1)

        def residual(l, w, b):
            n = n_of(l, w, b)
            dve.wait_ge(*h0_full(n, 0))
            dve.wait_ge(*h1_full(n - 1, 0))
            dve.wait_ge(*x_ready(n - 1))
            dve.tensor_tensor(x1[:], H0[:, 0:D], X[:, bass.ds((b * NW + w) * D, D)], ALU.add)\
                .then_inc(x1_ready.sem, 1)

        def stats(l, w, b):
            n = n_of(l, w, b)
            dve.wait_ge(*x1_ready(n))
            dve.wait_ge(*mv_ready(n - 1))
            dve.bn_stats(st[:, 0, :], x1[:, 0:P]).then_inc(st_ready.sem, 1)
            dve.wait_ge(*h0_full(n, 1))
            dve.bn_stats(st[:, 1, :], H0[:, 0:P]).then_inc(st_ready.sem, 1)
            dve.wait_ge(*st_ready(n, 1))
            dve.wait_ge(*z_ready(n - 1, 1))
            dve.sem_inc(passed_dve, 1)
            dve.bn_aggr(mv[:], st[:].rearrange("p a c -> p (a c)")).then_inc(mv_ready.sem, 1)

        def normed(l, w, b):
            n = n_of(l, w, b)
            dve.wait_ge(*rstd_ready(n))
            dve.wait_ge(*h1_full(n - 1, 1))
            dve.wait_ge(*mv_ready(n))
            dve.tensor_scalar(z[:, 0:P], x1[:, 0:P], mv[:, 0:1], rstd[:], ALU.subtract, ALU.mult).then_inc(z_ready.sem, 1)
            dve.tensor_scalar(z[:, P:D], H0[:, 0:P], mv[:, 0:1], rstd[:], ALU.subtract, ALU.mult)\
                .then_inc(z_ready.sem, 1)

        def gated(l, w, b, part):
            n = n_of(l, w, b)
            dve.wait_ge(*gel_ready(n, part))
            dve.wait_ge(*h1_full(n, 2 + part))
            for i, c in enumerate(halves[part]):
                size = min(P, HID - c * P)
                op = dve.scalar_tensor_tensor(out=uT[0:size, c, :], in0=H1[0:size, i * W:(i + 1) * W],
                                              scalar=bias1[0:size, l, 0, c:c + 1], in1=gel[0:size, c, :], op0=ALU.add, op1=ALU.mult)
            op.then_inc(u_ready.sem, 1)

        def finish(l, w, b):
            n = n_of(l, w, b)
            dve.wait_ge(*h0_full(n, 4))
            dve.wait_ge(*x1_ready(n))
            if l < DEPTH - 1:
                dve.wait_ge(*xw_ready(n))
                dve.tensor_tensor(X[:, bass.ds((b * NW + w) * D, D)], H0[:, 0:D], x1[:], ALU.add)\
                    .then_inc(x_ready.sem, 1)
            else:
                m = n - UNITS
                dve.tensor_tensor(yres[:], H0[:, 0:D], x1[:], ALU.add)\
                    .then_inc(x_ready.sem, 1)
                dve.wait_ge(*x_ready(n))
                dve.wait_ge(xn_loaded[b], 16 * (w + 1))
                dve.wait_ge(*y_ready(m - 1))
                dve.tensor_tensor(ysum[:], yres[:], xn[b][:], ALU.add).then_inc(ysum_ready.sem, 1)
                dve.wait_ge(*ysum_ready(m))
                dve.bn_stats(st2[:], ysum[:]).then_inc(st2_ready.sem, 1)
                dve.wait_ge(*st2_ready(m))
                dve.sem_inc(passed_dve, 1)
                dve.bn_aggr(mv2[:], st2[:]).then_inc(mv2_ready.sem, 1)

        def step(mlp, att, frt):
            do(att, row_max, 0)
            do(mlp, residual)
            do(att, row_max, 1)
            do(att, probs_out, 0)
            do(att, row_max, 2)
            do(mlp, stats)
            do(mlp, normed)
            do(att, probs_out, 1)
            do(frt, norm_sum, 0)
            do(att, row_max, 3)
            do(frt, rotate, 0)
            do(att, probs_out, 2)
            do(frt, norm_sum, 1)
            do(frt, rotate, 1)
            do(mlp, gated, 0)
            do(att, probs_out, 3)
            do(mlp, gated, 1)
            do(att, normalise)
            do(mlp, finish)

        layers(dve, step)

    @block.scalar
    def _(act):
        credit(act, [xT_ready, sq_ready, v_ready, qT_ready, kT_ready, e_ready, oT_ready, yT_ready, zT_ready, gel_ready])

        def xT_out(l, w, b):
            n = n_of(l, w, b)
            act.wait_ge(*f0_full(n, 0))
            act.wait_ge(*xT_carried(n))
            act.activation(xT[b][:, :, 1:W + 1], F0[:, 0:2 * W].rearrange("p (j k) -> p j k", j=2), ACT.Copy)\
                .then_inc(xT_ready.sem, 1)

        def squares(l, w, b, part):
            n = n_of(l, w, b)
            bank, full = [(F1, f1_full), (F0, f0_full)][part]
            act.wait_ge(*full(n, part))
            act.wait_ge(*ss_ready(n - 1, part))
            act.activation(sq[:, part, :], bank[:], ACT.Square).then_inc(sq_ready.sem, 1)

        def v_out(l, w, b):
            n = n_of(l, w, b)
            act.wait_ge(*f1_full(n, 1))
            act.wait_ge(*v_carried(n - 2))
            act.activation(V[b][:, 1, :], F1[:], ACT.Copy).then_inc(v_ready.sem, 1)

        def qT_out(l, w, b):
            n = n_of(l, w, b)
            act.wait_ge(*f0_full(n, 2))
            act.wait_ge(*s_full[1](n - 1, 1))
            act.activation(qT[:].rearrange("p c k -> p (c k)"), F0[:], ACT.Copy)\
                .then_inc(qT_ready.sem, 1)

        def kT_out(l, w, b):
            n = n_of(l, w, b)
            act.wait_ge(*f1_full(n, 2))
            act.wait_ge(*k_carried(n - 2))
            act.activation(kT[b][:, :, 1, :], F1[:].rearrange("p (c k) -> p c k", c=4), ACT.Copy)\
                .then_inc(kT_ready.sem, 1)

        def exponents(l, w, b, g):
            n = n_of(l, w, b)
            act.wait_ge(*nmax_ready(n, g))
            if g == 0:
                act.wait_ge(*rsum_ready(n - 1))
            act.wait_ge(*(t_full(n - 1, 2 + g) if g < 2 else t_full(n, g - 2)))
            for j in range(2):
                h = 2 * g + j
                e = act.activation(E[g % 2][:, j, :], masked[g % 2][:, j, :], ACT.Exp, scale=-1.0, bias=nmax[:, h:h + 1],
                                   accum_out=psum_e[:, head_of(g, j):head_of(g, j) + 1])
            e.then_inc(e_ready.sem, 1)

        def oT_out(l, w, b):
            n = n_of(l, w, b)
            act.wait_ge(*t_full(n, 4))
            act.wait_ge(*h0_full(n - 1, 0))
            act.activation(oT[:].rearrange("p c k -> p (c k)"), T[:], ACT.Copy)\
                .then_inc(oT_ready.sem, 1)

        def yT_out(l, w, b):
            n = n_of(l, w, b)
            act.wait_ge(*h1_full(n, 0))
            act.wait_ge(*yT_carried(n - 2))
            act.activation(yT[b][:, 1:W + 1], H1[:, 0:W], ACT.Copy).then_inc(yT_ready.sem, 1)

        def zT_out(l, w, b):
            n = n_of(l, w, b)
            act.wait_ge(*h1_full(n, 1))
            act.activation(zT[:].rearrange("p c k -> p (c k)"), H1[:, 0:2 * W], ACT.Copy)\
                .then_inc(zT_ready.sem, 1)

        def gelu(l, w, b, part):
            n = n_of(l, w, b)
            act.wait_ge(*h0_full(n, 2 + part))
            act.wait_ge(*u_ready(n - 1, part))
            for i, c in enumerate(halves[part]):
                size = min(P, HID - c * P)
                g = act.activation(gel[0:size, c, :], H0[0:size, i * W:(i + 1) * W], ACT.Gelu, bias=bias1[0:size, l, 1, c:c + 1])
            g.then_inc(gel_ready.sem, 1)

        def step(mlp, att, frt):
            do(att, exponents, 0)
            do(att, exponents, 1)
            do(frt, xT_out)
            do(mlp, yT_out)
            do(frt, squares, 0)
            do(att, exponents, 2)
            do(mlp, zT_out)
            do(att, exponents, 3)
            do(frt, squares, 1)
            do(mlp, gelu, 0)
            do(mlp, gelu, 1)
            do(frt, v_out)
            do(frt, qT_out)
            do(frt, kT_out)
            do(att, oT_out)

        layers(act, step)

    @block.gpsimd
    def _(pool):
        credit(pool, [xw_ready, xT_carried, tab_ready, rn_floor, rn_ready, rot_summed, qk_ready, v_carried, k_carried,
                      yT_carried, var_eps, rstd_ready, var2_eps, rstd2_ready, y_ready])

        def rows_in(l, w, b):
            n = n_of(l, w, b)
            pool.wait_ge(*f0_full(n - 2, 0))
            if l:
                pool.wait_ge(*x_ready(n - UNITS))
            pool.sem_inc(passed_pool, 1)
            pool.tensor_copy(xw[b][:], X[:, bass.ds((b * NW + w) * D, D)]).then_inc(xw_ready.sem, 1)
            pool.wait_ge(*rs_ready(n - 1, 1))
            pool.sem_inc(passed_pool, 1)
            pool.tensor_tensor(tab[:].rearrange("p a d -> p (a d)"), rope[:, bass.ds(w * 4 * DH, 4 * DH)],
                               scales[:, l, :], ALU.mult).then_inc(tab_ready.sem, 1)

        def norm(l, w, b, part):
            n = n_of(l, w, b)
            pool.wait_ge(*ss_ready(n, part))
            pool.sem_inc(passed_pool, 1)
            pool.tensor_scalar(rf[:, part, :], ss[:, part, :], 1e-24, None, ALU.max).then_inc(rn_floor.sem, 1)
            pool.wait_ge(*rn_floor(n, part))
            pool.tensor_tensor(rn[:, part, :], rf[:, part, :], nhalf[:, 0:FH], ALU.pow).then_inc(rn_ready.sem, 1)
            pool.wait_ge(*rs_ready(n, part))
            pool.wait_ge(*rc_ready(n, part))
            pool.tensor_tensor(rot[:, part, :], rc[:, part, :], rs[:, part, :], ALU.add).then_inc(rot_summed.sem, 1)
            pool.wait_ge(*rot_summed(n, part))
            pool.wait_ge(*rn_ready(n, part))
            pool.wait_ge(*[f0_full, f1_full][part](n - 1, 2))
            pool.tensor_tensor(qk[:, part, :].rearrange("p (h d) -> p h d", h=FH),
                               rot[:, part, :].rearrange("p (h d) -> p h d", h=FH), along(rn[:, part, :], DH), ALU.mult)\
                .then_inc(qk_ready.sem, 1)

        def carry_x(l, w, b):
            n = n_of(l, w, b)
            first = isinstance(w, int) and w == 0
            pool.wait_ge(*f1_full(n - 2, 1))
            if first:
                pool.memset(xT[b][:, 1, 0:1], 0.0).then_inc(xT_carried.sem, 1)
            else:
                pool.sem_inc(passed_pool, 1)
                pool.tensor_copy(xT[b][:, 1, 0:1], xT[b][:, 1, W:W + 1]).then_inc(xT_carried.sem, 1)

        def carry_k(l, w, b):
            n = n_of(l, w, b)
            pool.wait_ge(*s_full[1](n, 1))
            pool.wait_ge(*s_full[0](n, 1))
            pool.sem_inc(passed_pool, 1)
            pool.tensor_copy(kT[b][:, :, 0, :], kT[b][:, :, 1, :]).then_inc(k_carried.sem, 1)

        def carry_v(l, w, b):
            n = n_of(l, w, b)
            pool.wait_ge(*o_full(n, 0))
            pool.sem_inc(passed_pool, 1)
            pool.tensor_copy(V[b][:, 0, :], V[b][:, 1, :]).then_inc(v_carried.sem, 1)

        def rstd_of(l, w, b):
            n = n_of(l, w, b)
            pool.wait_ge(*mv_ready(n))
            pool.sem_inc(passed_pool, 1)
            pool.tensor_scalar(ve[:], mv[:, 1:2], LN_EPS, None, ALU.add).then_inc(var_eps.sem, 1)
            pool.wait_ge(*var_eps(n))
            pool.wait_ge(*z_ready(n - 1, 1))
            pool.tensor_tensor(rstd[:], ve[:], nhalf[:, 0:1], ALU.pow).then_inc(rstd_ready.sem, 1)

        def carry_y(l, w, b):
            n = n_of(l, w, b)
            last = isinstance(w, int) and w == NW - 1
            pool.wait_ge(*h0_full(n, 1))
            if last:
                pool.memset(yT[b][:, 0:1], 0.0).then_inc(yT_carried.sem, 1)
            else:
                pool.sem_inc(passed_pool, 1)
                pool.tensor_copy(yT[b][:, 0:1], yT[b][:, W:W + 1]).then_inc(yT_carried.sem, 1)

        def last_norm(l, w, b):
            m = n_of(l, w, b) - UNITS
            pool.wait_ge(*mv2_ready(m))
            pool.sem_inc(passed_pool, 1)
            pool.tensor_scalar(ve2[:], mv2[:, 1:2], LN_EPS, None, ALU.add).then_inc(var2_eps.sem, 1)
            pool.wait_ge(*var2_eps(m))
            pool.tensor_tensor(rstd2[:], ve2[:], nhalf[:, 0:1], ALU.pow).then_inc(rstd2_ready.sem, 1)
            pool.wait_ge(*rstd2_ready(m))
            pool.wait_ge(y_stored[b], 16 * (w + 1))
            pool.sem_inc(passed_pool, 1)
            pool.tensor_scalar(y[b][:], ysum[:], mv2[:, 0:1], rstd2[:], ALU.subtract, ALU.mult).then_inc(y_ready.sem, 1)

        for b in range(B):
            pool.memset(yT[b][:, 0:1], 0.0).then_inc(carries_zero, 1)
            pool.memset(V[b][:, 0, :], 0.0).then_inc(carries_zero, 1)
            pool.memset(kT[b][:, :, 0, :], 0.0).then_inc(carries_zero, 1)
        pool.wait_ge(carries_zero, 3 * B)

        def step(mlp, att, frt):
            do(frt, carry_x)
            do(frt, rows_in)
            do(mlp, rstd_of)
            do(mlp, carry_y)
            do(frt, norm, 0)
            do(frt, norm, 1)
            do(att, carry_v)
            do(att, carry_k)
            if mlp and mlp[0] == DEPTH - 1:
                last_norm(*mlp)

        layers(pool, step)

    @block.sync
    def _(sp):
        for b in range(B):
            sp.sem_inc(y_stored[b], 16)

        def rows(w, b):
            m = B * w + b
            sp.wait_ge(*ysum_ready(m - 2))
            sp.dma_start(xn[b][:], x_norm_dram[b, bass.ds(w * W, W), :]).then_inc(xn_loaded[b], 16)

        def store(w, b):
            m = B * w + b
            sp.wait_ge(*y_ready(m))
            sp.dma_start(out_dram[b, bass.ds(w * W, W), :], y[b][:]).then_inc(y_stored[b], 16)

        rows(0, 0)
        rows(0, 1)
        with sp.Fori(0, NW - 1) as w:
            for b in range(B):
                store(w, b)
                rows(w + 1, b)
        for b in range(B):
            store(NW - 1, b)
        for b in range(B):
            sp.wait_ge(y_stored[b], 16 * (NW + 1))
def rope_tables(np):
    f = np.float32
    half = np.arange(0, DH, 2, dtype=f)
    freqs = np.arange(L, dtype=f)[:, None] * (f(1.0) / f(10000.0) ** (half / f(DH)))[None, :]
    base = (half + f(0.4 * DH)) / f(1.4 * DH)
    power = (np.arange(L, dtype=f) - f(L // 2)) / f(W // 2)
    scale = base[None, :] ** power[:, None]
    cos, sin, scale = np.cos(freqs), np.sin(freqs), np.concatenate([scale, scale], axis=1)
    cos = np.concatenate([cos, cos], axis=1)
    sin = np.concatenate([-sin, sin], axis=1)
    factor = f(-8.0)
    return np.concatenate([cos * scale * factor, sin * scale * factor, cos / scale, sin / scale], axis=1).astype(f)


def resident(nc, ctx):
    def sb(name, shape):
        return ctx.enter_context(nc.sbuf_tensor("r_" + name, shape, F32))

    return {"X": sb("X", [P, B * NW * D]), "ident": sb("ident", [P, P]), "nhalf": sb("nhalf", [P, 8])}


def ffn_resident(nc, ctx):
    def sb(name, shape, dt=F32):
        return ctx.enter_context(nc.sbuf_tensor("r_" + name, shape, dt))

    return {
        "wqkv": sb("wqkv", [P, DEPTH, 2, 3 * INNER]), "wo": sb("wo", [P, DEPTH, INNER // P, D]),
        "w1": sb("w1", [P, DEPTH, 2, 2 * HID]), "w2": sb("w2", [P, DEPTH, NU, D]),
        "bias1": sb("bias1", [P, DEPTH, 2, NU]), "bias2": sb("bias2", [P, DEPTH, D], BF16),
        "ones3": sb("ones3", [P, P], BF16),
        "rope": sb("rope", [P, NW * 4 * DH]), "scales": sb("scales", [P, DEPTH, 4 * DH]),
        "mask": sb("mask", [P, 2, 2 * W]),
    }


def delta_tables(np):
    i, j = np.arange(P)[:, None], np.arange(P)[None, :]
    joins = [(i // (2 * s) == j // (2 * s)) & (i % (2 * s) >= s) & (j % (2 * s) < s) for s in (2 ** n for n in range(NLEV + 1))]
    return np.concatenate(joins[1:] + [joins[0].T, i < j, i <= j], axis=1).astype(np.float32)


def program(nc, a, out):
    x_norm_dram = nc.dram_tensor("x_norm", (B, L, D), F32, kind="Internal").ap()
    with ExitStack() as ctx:
        t = resident(nc, ctx)
        steps = ctx.enter_context(nc.semaphore("ident_steps"))
        with nc.Block() as block:
            @block.gpsimd
            def _(pool):
                pool.memset(t["ident"][:], 0.0).then_inc(steps, 1)
                pool.memset(t["nhalf"][:], -0.5).then_inc(steps, 1)
                pool.wait_ge(steps, 2)
                pool.affine_select(out=t["ident"][:], in_=t["ident"][:], compare_op=ALU.not_equal, fill=1.0, base=0,
                                   pattern=[[-1, P]], channel_multiplier=1).then_inc(steps, 1)
                pool.wait_ge(steps, 3)

        with ExitStack() as delta:
            held = delta_layer(nc, delta, t, a, x_norm_dram)
            with nc.Block() as block:
                @block.gpsimd
                def _(pool):
                    for sem in held:
                        pool.sem_clear(sem)
        with ExitStack() as ffn:
            t.update(ffn_resident(nc, ffn))
            setup(nc, ctx, a, t)
            ffn_layers(nc, ffn, t, x_norm_dram, out)


_INS = {"hidden_states": "x", "Wq": "Wq", "Wk": "Wk", "Wv": "Wv", "conv_q": "conv_q", "conv_k": "conv_k", "conv_v": "conv_v",
        "Wb": "Wb", "Wdec": "Wdec", "Wmix": "Wmix", "conv_mix": "conv_mix", "mix_bias": "mix_bias", "rms_w": "rms_w", "Wo": "Wo"}
_FFN_INS = ["wqkv", "q_scale", "k_scale", "wo", "ln_g", "ln_b", "w1", "b1", "w2", "b2"]


def kernel(**inputs):
    import numpy as np
    import concourse.bacc as bacc
    from concourse.bass_utils import run_bass_kernel_spmd

    nc = bacc.Bacc("TRN2", target_bir_lowering=False, num_devices=1)
    arrays, a = {}, {}

    def put(key, array):
        name = f"in_{key}_dram"
        arrays[name] = np.ascontiguousarray(array)
        a[key] = nc.dram_tensor(name, array.shape, mybir.dt.from_np(arrays[name].dtype), kind="ExternalInput").ap()

    for name, key in _INS.items():
        put(key, inputs["L0_attn_" + name])
    for name in _FFN_INS:
        put(name, inputs["L0_ffn_" + name])
    put("rope", rope_tables(np))
    put("tables", delta_tables(np))
    out = nc.dram_tensor("out_0_dram", (B, L, D), F32, kind="ExternalOutput").ap()
    program(nc, a, out)
    r = run_bass_kernel_spmd(nc, [arrays], core_ids=[0])
    return r.results[0]["out_0_dram"]
```
